# Optimizing a Trainium2 kernel written in Bass

```python
import numpy as np
import jax
import jax.numpy as jnp

def _softmax(x, axis=-1):
    return jax.nn.softmax(x, axis=axis)

def _gelu(x):
    return jax.nn.gelu(x, approximate=True)

def _silu(x):
    return jax.nn.silu(x)

def _sigmoid(x):
    return jax.nn.sigmoid(x)

def _layernorm(x, axis=-1, eps=1e-05):
    m = jnp.mean(x, axis=axis, keepdims=True)
    v = jnp.var(x, axis=axis, keepdims=True)
    return (x - m) / jnp.sqrt(v + eps)

def _scatter_add(tgt, idx, src, axis=0):
    return tgt.at[idx].add(src)

def _segment_sum(src, seg, n):
    return jax.ops.segment_sum(src, seg, n)
kernel_name = 'mk_macaron_d1_jaxref_r8_7fd0fa'

def setup_inputs(seed: int=0):
    np.random.seed(seed)
    _w = jnp.asarray

    def _L0_attn_setup():
        import jax, jax.numpy as jnp
        import numpy as np
        EPS = 1e-06
        CHUNK = 16

        def _ln(x, g, b):
            mu = jnp.mean(x, -1, keepdims=True)
            var = jnp.var(x, -1, keepdims=True)
            xhat = (x - mu) * jax.lax.rsqrt(var + EPS)
            return g * xhat + b

        def chunk_ttt_linear(q, k, v, w, b, eta, scale=1.0):
            B, T, H, D = q.shape
            NC = T // CHUNK
            q = q * scale
            qc = q.reshape(B, NC, CHUNK, H, D).swapaxes(0, 1)
            kc = k.reshape(B, NC, CHUNK, H, D).swapaxes(0, 1)
            vc = v.reshape(B, NC, CHUNK, H, D).swapaxes(0, 1)
            ec = eta.reshape(B, NC, CHUNK, H).swapaxes(0, 1)
            tri = jnp.tril(jnp.ones((CHUNK, CHUNK), bool))
            S0 = jnp.zeros((B, H, D, D), q.dtype)

            def step(S, inp):
                qi, ki, vi, ei = inp
                kh = jnp.einsum('bchd,bhde->bche', ki, S)
                target = vi - ki
                mu = jnp.mean(kh, -1, keepdims=True)
                rstd = jax.lax.rsqrt(jnp.var(kh, -1, keepdims=True) + EPS)
                kh_hat = (kh - mu) * rstd
                g = w * kh_hat + b - target
                gw = g * w
                v_new = (gw - jnp.mean(gw, -1, keepdims=True) - kh_hat * jnp.mean(gw * kh_hat, -1, keepdims=True)) * rstd
                A = jnp.einsum('bchd,bshd->bhcs', qi, ki)
                A = jnp.where(tri, A, 0.0) * jnp.transpose(ei, (0, 2, 1))[:, :, None, :]
                qh = jnp.einsum('bchd,bhde->bche', qi, S) - jnp.einsum('bhcs,bshe->bche', A, v_new)
                o = qi + _ln(qh, w, b)
                S = S - jnp.einsum('bchd,bche->bhde', ki * ei[..., None], v_new)
                return (S, o)
            S_fin, o = jax.lax.scan(step, S0, (qc, kc, vc, ec))
            o = o.swapaxes(0, 1).reshape(B, T, H, D)
            return (o, S_fin)
        key = jax.random.key(seed)
        ks = jax.random.split(key, 11)
        B, T, D, H = (2, 512, 256, 16)
        Dh = D // H
        std = 0.02
        x = jax.random.normal(ks[0], (B, T, D), jnp.float32)
        Wq = jax.random.normal(ks[1], (D, D), jnp.float32) * std
        Wk = jax.random.normal(ks[2], (D, D), jnp.float32) * std
        Wv = jax.random.normal(ks[3], (D, D), jnp.float32) * std
        Wo = jax.random.normal(ks[4], (D, D), jnp.float32) * std
        Wbeta = jax.random.normal(ks[5], (D, H), jnp.float32) * std
        ln_w = 1.0 + jax.random.normal(ks[6], (H, Dh), jnp.float32) * std
        ln_b = jax.random.normal(ks[7], (H, Dh), jnp.float32) * std
        Wg1 = jax.random.normal(ks[8], (D, Dh), jnp.float32) * std
        Wg2 = jax.random.normal(ks[9], (Dh, D), jnp.float32) * std
        norm_w = 1.0 + jax.random.normal(ks[10], (D,), jnp.float32) * std
        return dict(x=x, Wq=Wq, Wk=Wk, Wv=Wv, Wo=Wo, Wbeta=Wbeta, ln_w=ln_w, ln_b=ln_b, Wg1=Wg1, Wg2=Wg2, norm_w=norm_w)
    _L0_attn_in = _L0_attn_setup()

    def _L0_ffn_setup():
        import jax, jax.numpy as jnp
        import numpy as np
        B, S, H = (1, 64, 256)
        I = 192
        E = 32
        K = 4
        SCALE = 1.8
        key = jax.random.key(seed)
        ks = jax.random.split(key, 9)
        init = lambda k, shape: jax.random.normal(k, shape, jnp.float32) * (1.0 / np.sqrt(shape[-1]))
        return {'x': jax.random.normal(ks[0], (B, S, H), jnp.float32), 'router_w': init(ks[1], (E, H)), 'router_b': jnp.zeros((E,), jnp.float32), 'gate_w': init(ks[2], (E, I, H)), 'up_w': init(ks[3], (E, I, H)), 'down_w': init(ks[4], (E, H, I)), 'shared_gate_w': init(ks[5], (I, H)), 'shared_up_w': init(ks[6], (I, H)), 'shared_down_w': init(ks[7], (H, I))}
    _L0_ffn_in = _L0_ffn_setup()
    _d = {'L0_attn_x': _L0_attn_in['x'], 'L0_attn_Wq': _L0_attn_in['Wq'], 'L0_attn_Wk': _L0_attn_in['Wk'], 'L0_attn_Wv': _L0_attn_in['Wv'], 'L0_attn_Wo': _L0_attn_in['Wo'], 'L0_attn_Wbeta': _L0_attn_in['Wbeta'], 'L0_attn_ln_w': _L0_attn_in['ln_w'], 'L0_attn_ln_b': _L0_attn_in['ln_b'], 'L0_attn_Wg1': _L0_attn_in['Wg1'], 'L0_attn_Wg2': _L0_attn_in['Wg2'], 'L0_attn_norm_w': _L0_attn_in['norm_w'], 'L0_ffn_router_w': _L0_ffn_in['router_w'], 'L0_ffn_router_b': _L0_ffn_in['router_b'], 'L0_ffn_gate_w': _L0_ffn_in['gate_w'], 'L0_ffn_up_w': _L0_ffn_in['up_w'], 'L0_ffn_down_w': _L0_ffn_in['down_w'], 'L0_ffn_shared_gate_w': _L0_ffn_in['shared_gate_w'], 'L0_ffn_shared_up_w': _L0_ffn_in['shared_up_w'], 'L0_ffn_shared_down_w': _L0_ffn_in['shared_down_w']}
    _x0 = _d['L0_attn_x']
    _d['L0_attn_x'] = jax.random.normal(jax.random.fold_in(jax.random.key(seed), 1), (1, 1024, 256), dtype=_x0.dtype)
    del _x0
    return _d

def reference(L0_attn_x, L0_attn_Wq, L0_attn_Wk, L0_attn_Wv, L0_attn_Wo, L0_attn_Wbeta, L0_attn_ln_w, L0_attn_ln_b, L0_attn_Wg1, L0_attn_Wg2, L0_attn_norm_w, L0_ffn_router_w, L0_ffn_router_b, L0_ffn_gate_w, L0_ffn_up_w, L0_ffn_down_w, L0_ffn_shared_gate_w, L0_ffn_shared_up_w, L0_ffn_shared_down_w):

    def _L0_attn_ref(x, Wq, Wk, Wv, Wo, Wbeta, ln_w, ln_b, Wg1, Wg2, norm_w):
        import jax, jax.numpy as jnp
        import numpy as np
        EPS = 1e-06
        CHUNK = 16

        def _ln(x, g, b):
            mu = jnp.mean(x, -1, keepdims=True)
            var = jnp.var(x, -1, keepdims=True)
            xhat = (x - mu) * jax.lax.rsqrt(var + EPS)
            return g * xhat + b

        def chunk_ttt_linear(q, k, v, w, b, eta, scale=1.0):
            B, T, H, D = q.shape
            NC = T // CHUNK
            q = q * scale
            qc = q.reshape(B, NC, CHUNK, H, D).swapaxes(0, 1)
            kc = k.reshape(B, NC, CHUNK, H, D).swapaxes(0, 1)
            vc = v.reshape(B, NC, CHUNK, H, D).swapaxes(0, 1)
            ec = eta.reshape(B, NC, CHUNK, H).swapaxes(0, 1)
            tri = jnp.tril(jnp.ones((CHUNK, CHUNK), bool))
            S0 = jnp.zeros((B, H, D, D), q.dtype)

            def step(S, inp):
                qi, ki, vi, ei = inp
                kh = jnp.einsum('bchd,bhde->bche', ki, S)
                target = vi - ki
                mu = jnp.mean(kh, -1, keepdims=True)
                rstd = jax.lax.rsqrt(jnp.var(kh, -1, keepdims=True) + EPS)
                kh_hat = (kh - mu) * rstd
                g = w * kh_hat + b - target
                gw = g * w
                v_new = (gw - jnp.mean(gw, -1, keepdims=True) - kh_hat * jnp.mean(gw * kh_hat, -1, keepdims=True)) * rstd
                A = jnp.einsum('bchd,bshd->bhcs', qi, ki)
                A = jnp.where(tri, A, 0.0) * jnp.transpose(ei, (0, 2, 1))[:, :, None, :]
                qh = jnp.einsum('bchd,bhde->bche', qi, S) - jnp.einsum('bhcs,bshe->bche', A, v_new)
                o = qi + _ln(qh, w, b)
                S = S - jnp.einsum('bchd,bche->bhde', ki * ei[..., None], v_new)
                return (S, o)
            S_fin, o = jax.lax.scan(step, S0, (qc, kc, vc, ec))
            o = o.swapaxes(0, 1).reshape(B, T, H, D)
            return (o, S_fin)
        B, T, D = x.shape
        H, Dh = ln_w.shape
        q = jax.nn.silu(x @ Wq).reshape(B, T, H, Dh)
        k = (x @ Wk).reshape(B, T, H, Dh)
        k = k * jax.lax.rsqrt(jnp.sum(k * k, -1, keepdims=True) + EPS)
        v = (x @ Wv).reshape(B, T, H, Dh)
        beta = jax.nn.sigmoid(x @ Wbeta) * 2.0
        o, _ = chunk_ttt_linear(q, k, v, ln_w, ln_b, beta, 1.0)
        gate = x @ Wg1 @ Wg2
        og = o * jax.nn.sigmoid(gate.reshape(B, T, H, Dh))
        og = og * jax.lax.rsqrt(jnp.mean(og * og, -1, keepdims=True) + EPS)
        o = og.reshape(B, T, D) * norm_w
        return o @ Wo

    def _L0_ffn_ref(x, router_w, router_b, gate_w, up_w, down_w, shared_gate_w, shared_up_w, shared_down_w):
        import jax, jax.numpy as jnp
        import numpy as np
        B, S, H = (1, 64, 256)
        I = 192
        E = 32
        K = 4
        SCALE = 1.8
        b, s, h = x.shape
        xf = x.reshape(-1, h).astype(jnp.float32)
        logits = xf @ router_w.T + router_b
        top_vals, top_idx = jax.lax.top_k(logits, K)
        rw = jax.nn.softmax(top_vals, axis=-1) * SCALE
        combine = jnp.einsum('tke,tk->te', jax.nn.one_hot(top_idx, E, dtype=xf.dtype), rw)
        g = jax.nn.silu(jnp.einsum('th,eih->tei', xf, gate_w))
        u = jnp.einsum('th,eih->tei', xf, up_w)
        routed = jnp.einsum('tei,ehi,te->th', g * u, down_w, combine)
        sg = jax.nn.silu(xf @ shared_gate_w.T)
        su = xf @ shared_up_w.T
        shared = sg * su @ shared_down_w.T
        return (routed + shared).reshape(b, s, h)
    x = L0_attn_x
    x = x + 0.5 * _L0_ffn_ref(_layernorm(x, axis=-1), L0_ffn_router_w, L0_ffn_router_b, L0_ffn_gate_w, L0_ffn_up_w, L0_ffn_down_w, L0_ffn_shared_gate_w, L0_ffn_shared_up_w, L0_ffn_shared_down_w)
    x = x + _L0_attn_ref(_layernorm(x, axis=-1), L0_attn_Wq, L0_attn_Wk, L0_attn_Wv, L0_attn_Wo, L0_attn_Wbeta, L0_attn_ln_w, L0_attn_ln_b, L0_attn_Wg1, L0_attn_Wg2, L0_attn_norm_w)
    x = x + 0.5 * _L0_ffn_ref(_layernorm(x, axis=-1), L0_ffn_router_w, L0_ffn_router_b, L0_ffn_gate_w, L0_ffn_up_w, L0_ffn_down_w, L0_ffn_shared_gate_w, L0_ffn_shared_up_w, L0_ffn_shared_down_w)
    return x

_drawn_inputs = setup_inputs


def setup_inputs(seed=0):
    import zlib

    import numpy as np

    out = dict(_drawn_inputs(seed))
    spreads = {'L0_ffn_router_b': (0.0, 0.1)}
    factors = {'L0_attn_ln_w': 2.841, 'L0_attn_Wg1': 6.332, 'L0_attn_Wg2': 6.772, 'L0_attn_norm_w': 3.718}
    for name, (base, spread) in spreads.items():
        noise = np.random.default_rng([zlib.crc32(name.encode()), seed]).standard_normal(out[name].shape)
        drawn = base * np.exp(spread * noise) if base else spread * noise
        out[name] = jnp.asarray(drawn.astype(out[name].dtype))
    for name, factor in factors.items():
        out[name] = (out[name] * factor).astype(out[name].dtype)
    return out
```

```python
from contextlib import ExitStack

import concourse.bass as bass
from concourse import mybir

ALU = mybir.AluOpType
ACT = mybir.ActivationFunctionType
F32 = mybir.dt.float32
I32 = mybir.dt.int32
U32 = mybir.dt.uint32
AX_X = mybir.AxisListType.X

P = 128
T, D = 1024, 256
NT = T // P
DH = D // P
E, I, K = 32, 192, 4
IR = I - P
H, DK, C = 16, 16, 16
HH = H // 2
NC = T // C
CT = P // C
ROUTED = (T * K + E * (P - 1)) // P
TILES = NT + ROUTED
SKIP = 100000
LN_EPS, EPS = 1e-5, 1e-6
SCALE = 1.8
ROWS = (K + 1) * T


def build(nc, d):
    with ExitStack() as ctx:
        def sb(name, shape, dt=F32):
            return ctx.enter_context(nc.sbuf_tensor(name, shape, dt))

        def sem(name):
            return ctx.enter_context(nc.semaphore(name))

        def dram(name, shape):
            return nc.dram_tensor(name, shape, F32, kind="Internal").ap()

        def named(name):
            if name not in sems:
                sems[name] = sem(name)
            return sems[name]

        sems = {}

        w_gu = sb("w_gu", [P, E + 1, DH * 2 * I])
        w_d1 = sb("w_d1", [P, E + 1, D])
        w_d2 = sb("w_d2", [P, E + 1, D])
        aux = w_d2[IR:P, :, :].rearrange("p e n -> p (e n)")
        ident = sb("ident", [P, P])
        same_head = sb("same_head", [P, P])
        causal = sb("causal", [P, P])
        earlier = sb("earlier", [P, P])
        ones = sb("ones", [P, P])
        count = sb("count", [P, P])
        pair_row = sb("pair_row", [P, NT, K])
        take = sb("take", [P, TILES], I32)
        put = sb("put", [P, TILES], I32)
        tile_expert = sb("tile_expert", [1, TILES], I32)
        mix = sb("mix", [P, NT, K])
        rt = sb("rt", [P, DH * E])
        rb = sb("rb", [1, E])
        work = sb("work", [P, 9500])
        bank = [ctx.enter_context(nc.psum_tensor(f"bank{n}", [P, 512], F32)) for n in range(8)]

        S = dict(w_gu=w_gu, aux=aux, w_d1=w_d1, w_d2=w_d2, ident=ident, same_head=same_head, causal=causal,
                 earlier=earlier, ones=ones, count=count, pair_row=pair_row, take=take, put=put,
                 tile_expert=tile_expert, mix=mix, rt=rt, rb=rb, work=work, bank=bank,
                 weights_in=sem("weights_in"), sem=named)
        S["xln_d"] = dram("xln_d", [T, D])
        S["res_d"] = dram("res_d", [ROWS, D])
        x1_d, x2_d = dram("x1_d", [T, D]), dram("x2_d", [T, D])
        S["q_d"], S["gate_d"] = dram("q_d", [T, D]), dram("gate_d", [T, D])
        S["r_d"], S["qh_d"] = dram("r_d", [T, D]), dram("qh_d", [T, D])

        constants(nc, S, d, sem)
        route(nc, S, "a", d["x"])
        expert_tiles(nc, S, "a")
        combine(nc, S, "a", x1_d)
        clear(nc, [sems[name] for name in sems if name.startswith("ffn_")])
        attention_inputs(nc, S, d)
        scan(nc, S, d)
        attention_output(nc, S, d, x1_d, x2_d)
        route(nc, S, "b", x2_d)
        expert_tiles(nc, S, "b")
        combine(nc, S, "b", d["out"])


def clear(nc, semaphores):
    with nc.Block() as block:
        @block.sync
        def _(sp):
            for s in semaphores:
                sp.sem_clear(s)


def carve(work, sizes):
    out, at = {}, 0
    for name, shape in sizes:
        n = 1
        for s in shape:
            n *= s
        v = work[:, at:at + n]
        if len(shape) == 2:
            v = v.rearrange("p (a b) -> p a b", a=shape[0])
        elif len(shape) == 3:
            v = v.rearrange("p (a b c) -> p a b c", a=shape[0], b=shape[1])
        out[name] = v
        at += n
    assert at <= work.shape[1], at
    return out


def by_tile(ap):
    return ap.rearrange("(j p) n -> p j n", p=P)


def constants(nc, S, d, sem):
    made, read = sem("made"), sem("c_read")
    with nc.Block() as block:
        @block.sync
        def _(sp):
            sp.dma_start(S["rt"][:], d["rt"]).then_inc(read, 16)
            sp.dma_start(S["rb"][:], d["rb"]).then_inc(read, 16)
            sp.wait_ge(read, 32)

        @block.gpsimd
        def _(pool):
            ident, same, causal, earlier = S["ident"], S["same_head"], S["causal"], S["earlier"]
            heads = lambda t: t[:].rearrange("p (h c) -> p h c", c=C)
            pool.memset(S["ones"][:], 1.0).then_inc(made, 1)
            pool.iota(S["count"][:], [[1, P]], base=0, channel_multiplier=0,
                      allow_small_or_imprecise_dtypes=True)
            pool.iota(S["pair_row"][:], [[P, NT], [T, K]], base=1, channel_multiplier=1,
                      allow_small_or_imprecise_dtypes=True)
            pool.iota(S["take"][:, 0:NT], [[P, NT]], base=0, channel_multiplier=1)
            pool.iota(S["put"][:, 0:NT], [[P, NT]], base=K * T, channel_multiplier=1)
            pool.iota(S["tile_expert"][:, 0:NT], [[0, NT]], base=E, channel_multiplier=0).then_inc(made, 1)
            pool.wait_ge(made, 2)
            pool.affine_select(out=ident[:], in_=S["ones"][:], pattern=[[-1, P]], compare_op=ALU.is_equal,
                               fill=0.0, base=0, channel_multiplier=1).then_inc(made, 1)
            pool.affine_select(out=earlier[:], in_=S["ones"][:], pattern=[[1, P]], compare_op=ALU.is_ge,
                               fill=0.0, base=-1, channel_multiplier=-1).then_inc(made, 1)
            pool.affine_select(out=heads(causal), in_=heads(S["ones"]), pattern=[[-C, HH], [0, C]],
                               compare_op=ALU.is_ge, fill=0.0, base=0, channel_multiplier=1).then_inc(made, 1)
            pool.wait_ge(made, 5)
            pool.affine_select(out=heads(same), in_=heads(causal), pattern=[[C, HH], [0, C]],
                               compare_op=ALU.is_ge, fill=0.0, base=C - 1, channel_multiplier=-1).then_inc(made, 1)
            pool.wait_ge(made, 6)
            pool.affine_select(out=heads(causal), in_=heads(same), pattern=[[C, HH], [1, C]],
                               compare_op=ALU.is_ge, fill=0.0, base=0, channel_multiplier=-1).then_inc(made, 1)

        @block.scalar
        def _(act):
            step = 11
            for e in range(0, E + 1, step):
                act.dma_start(S["w_gu"][:, e:e + step, :], d["w_gu"][:, e:e + step, :]).then_inc(S["weights_in"], 16)
                act.dma_start(S["w_d1"][:, e:e + step, :], d["w_d1"][:, e:e + step, :]).then_inc(S["weights_in"], 16)
                act.dma_start(S["w_d2"][0:IR, e:e + step, :], d["w_d2"][:, e:e + step, :]).then_inc(S["weights_in"], 16)


WEIGHT_LOADS = 9


def ffn_views(S):
    return carve(S["work"], [
        ("x", (NT, D)), ("xn", (2, D)), ("xt", (2, D)), ("logits", (NT, E)), ("top", (NT, 8)),
        ("top_i", (NT, 8)), ("expert", (NT, 8)), ("chosen", (NT * K, E)), ("members", (NT, E)),
        ("before", (NT, E)), ("slot_of", (NT, E)), ("picked", (NT * K, E)), ("slot", (NT * K,)),
        ("slot_tile", (NT * K,)), ("slot_pos", (NT * K,)), ("is_pos", (2, K * P)), ("is_tile", (2, K * ROUTED)),
        ("small", (600,))])


def layer_stats(nc, dve, act_sem, V, x, loaded, tag, sem):
    done = sem(f"{tag}_stat")
    st, mean, var = V["stats"], V["mean"], V["var"]
    if loaded:
        dve.wait_ge(loaded, 16)
    with dve.Fori(0, NT) as j:
        dve.bn_stats(st[:, bass.ds(j, 1), :], x[:, bass.ds(j, 1), :]).then_inc(done, 1)
    dve.wait_ge(done, NT)
    dve.tensor_tensor(V["t1"], st[:, :, 1], st[:, :, 4], ALU.subtract).then_inc(done, 1)
    dve.tensor_tensor(V["t2"], st[:, :, 1], st[:, :, 4], ALU.add).then_inc(done, 1)
    dve.tensor_tensor(V["t3"], st[:, :, 2], st[:, :, 5], ALU.add).then_inc(done, 1)
    dve.wait_ge(done, NT + 3)
    dve.scalar_tensor_tensor(out=V["t4"], in0=V["t1"], scalar=0.25, in1=V["t1"], op0=ALU.mult,
                             op1=ALU.mult).then_inc(done, 1)
    dve.tensor_scalar(mean, V["t2"], 0.5, None, ALU.mult).then_inc(done, 1)
    dve.tensor_scalar(V["t5"], V["t3"], 1.0 / D, LN_EPS, ALU.mult, ALU.add).then_inc(done, 1)
    dve.wait_ge(done, NT + 6)
    dve.tensor_tensor(var, V["t5"], V["t4"], ALU.add).then_inc(done, 1)
    dve.wait_ge(done, NT + 7)
    dve.reciprocal(V["t6"], var).then_inc(act_sem, 1)


def stat_views(at):
    V = {"stats": at[:, 0:48].rearrange("p (j s) -> p j s", s=6)}
    for n, name in enumerate(("mean", "rstd", "var", "t1", "t2", "t3", "t4", "t5", "t6")):
        V[name] = at[:, 48 + 8 * n:56 + 8 * n]
    return V


def route(nc, S, tag, x_d):
    V = ffn_views(S)
    small = V["small"]
    st = stat_views(small[:, 0:120])
    shifted = small[:, 120:152].rearrange("p (j k) -> p j k", k=K)
    exps = small[:, 152:184].rearrange("p (j k) -> p j k", k=K)
    total = small[:, 184:192]
    per = small[:, 192:200]
    members_all = small[:, 200:232]
    counted = small[:, 232:264].bitcast(I32)
    tiles_of = small[:, 264:296].bitcast(I32)
    tiles_end = small[:, 296:328]
    first_slot = small[:, 328:360]
    slot_int = small[:, 360:392].bitcast(I32)
    tile_int = small[:, 392:424].bitcast(I32)
    pos_int = small[:, 424:456].bitcast(I32)
    row_f = small[:, 456:456 + ROUTED]
    empty = small[:, 520:520 + ROUTED]
    x, xn, xt = V["x"], V["xn"], V["xt"]
    logits, top, expert = V["logits"], V["top"], V["expert"]
    top_i = V["top_i"].bitcast(U32)
    chosen = V["chosen"].rearrange("p (j k) e -> p j k e", k=K)
    picked = V["picked"].rearrange("p (j k) e -> p j k e", k=K)
    is_pos = V["is_pos"].rearrange("p u (k q) -> p u k q", k=K)
    is_tile = V["is_tile"].rearrange("p u (k q) -> p u k q", k=K)
    bank = S["bank"]
    ps_t, ps_l = bank[0:2], bank[2:4]
    ps_cum, ps_all, ps_pair = bank[4], bank[5], bank[6]
    rt = S["rt"][:].rearrange("p (f e) -> p f e", f=DH)

    g = lambda n: S["sem"](f"ffn_{n}")
    x_in, var_ready, rstd_ready = g("x_in"), g("var_ready"), g("rstd_ready")
    xn_ready, xn_out = g("xn_ready"), [g("xn_out0"), g("xn_out1")]
    xt_ps, xt_ready, logit_ps, logit_ready = g("xt_ps"), g("xt_ready"), g("logit_ps"), g("logit_ready")
    shifted_ready, exp_ready = g("shifted_ready"), g("exp_ready")
    members_ready, cum_ps = g("members_ready"), g("cum_ps")
    onehot_ready, pair_ps = g("onehot_ready"), g("pair_ps")
    step = g("route_step")

    with nc.Block() as block:
        @block.sync
        def _(sp):
            sp.dma_start(x[:], by_tile(x_d)).then_inc(x_in, 16)
            out = S["xln_d"].rearrange("(j p) n -> j p n", p=P)
            for j in range(NT):
                sp.wait_ge(xn_ready, j + 1)
                sp.dma_start(out[j], xn[:, j % 2, :]).then_inc(xn_out[j % 2], 16)
            for u in range(2):
                sp.wait_ge(xn_out[u], 16 * NT // 2)

        @block.vector
        def _(dve):
            n = [0]

            def then(ins):
                n[0] += 1
                ins.then_inc(step, 1)
                dve.wait_ge(step, n[0])

            layer_stats(nc, dve, var_ready, st, x, x_in, "ffn", S["sem"])
            dve.wait_ge(rstd_ready, 1)
            for j in range(NT):
                if j >= 2:
                    dve.wait_ge(xn_out[j % 2], 16 * (j // 2))
                    dve.wait_ge(xt_ps, j - 1)
                dve.tensor_scalar(xn[:, j % 2, :], x[:, j, :], st["mean"][:, j:j + 1], st["rstd"][:, j:j + 1],
                                  ALU.subtract, ALU.mult).then_inc(xn_ready, 1)
            dve.wait_ge(logit_ready, NT)
            for j in range(NT):
                dve.max(top[:, j, :], logits[:, j, :]).then_inc(step, 1)
            n[0] = NT
            dve.wait_ge(step, NT)
            dve.tensor_tensor(shifted, top[:, :, 0:K], top[:, :, 0:1].broadcast_to([P, NT, K]),
                              ALU.subtract).then_inc(shifted_ready, 1)
            for j in range(NT):
                dve.max_index(top_i[:, j, :], top[:, j, :], logits[:, j, :]).then_inc(step, 1)
            n[0] += NT
            dve.wait_ge(step, n[0])
            then(dve.tensor_copy(expert[:], top_i[:]))
            then(dve.tensor_tensor(
                chosen, S["count"][:, 0:E].unsqueeze(1).unsqueeze(1).broadcast_to([P, NT, K, E]),
                expert[:, :, 0:K].unsqueeze(3).broadcast_to([P, NT, K, E]), ALU.is_equal))
            then(dve.tensor_reduce(V["members"], chosen.rearrange("p j k e -> p j e k"), AX_X, ALU.add))
            then(dve.memset(V["before"][:, 0, :], 0.0))
            for j in range(1, NT):
                then(dve.tensor_tensor(V["before"][:, j, :], V["before"][:, j - 1, :], V["members"][:, j - 1, :],
                                       ALU.add))
            dve.tensor_tensor(members_all, V["before"][:, NT - 1, :], V["members"][:, NT - 1, :],
                              ALU.add).then_inc(members_ready, 1)
            dve.wait_ge(exp_ready, 1)
            then(dve.tensor_reduce(total, exps, AX_X, ALU.add))
            then(dve.reciprocal(per, total))
            then(dve.scalar_tensor_tensor(out=S["mix"][:], in0=exps, scalar=0.5 * SCALE,
                                          in1=per.unsqueeze(2).broadcast_to([P, NT, K]), op0=ALU.mult, op1=ALU.mult))
            dve.wait_ge(cum_ps, 1)
            then(dve.tensor_scalar(counted, bank[5][:, 0:E], float(P - 1), None, ALU.add))
            then(dve.tensor_scalar(tiles_of, counted, 7, None, ALU.logical_shift_right))
            then(dve.tensor_copy(row_f[:, 0:E], tiles_of))
            then(dve.tensor_tensor_scan(tiles_end, S["ones"][:, 0:E], row_f[:, 0:E], 0.0, ALU.mult, ALU.add))
            then(dve.tensor_tensor(first_slot, tiles_end, row_f[:, 0:E], ALU.subtract))
            then(dve.scalar_tensor_tensor(out=V["slot_of"], in0=first_slot.unsqueeze(1).broadcast_to([P, NT, E]),
                                          scalar=float(P), in1=ps_cum[:, 0:NT * E].rearrange("p (j e) -> p j e", e=E),
                                          op0=ALU.mult, op1=ALU.add))
            then(dve.tensor_tensor(picked, chosen, V["slot_of"].unsqueeze(2).broadcast_to([P, NT, K, E]), ALU.mult))
            then(dve.tensor_reduce(V["slot"], V["picked"], AX_X, ALU.add))
            then(dve.tensor_copy(slot_int, V["slot"]))
            then(dve.tensor_scalar(tile_int, slot_int, 7, None, ALU.logical_shift_right))
            then(dve.tensor_scalar(pos_int, slot_int, P - 1, None, ALU.bitwise_and))
            then(dve.tensor_copy(V["slot_tile"], tile_int))
            then(dve.tensor_copy(V["slot_pos"], pos_int))
            half = (ROUTED + 1) // 2
            for a, b in ((0, half), (half, ROUTED)):
                w = (b - a) * E
                v = V["picked"].rearrange("p n e -> p (n e)")[0:1, 0:w].rearrange("p (i e) -> p i e", e=E)
                then(dve.tensor_tensor(v, tiles_end[0:1, :].unsqueeze(1).broadcast_to([1, b - a, E]),
                                       S["count"][0:1, a:b].unsqueeze(2).broadcast_to([1, b - a, E]), ALU.is_le))
                then(dve.tensor_reduce(row_f[0:1, a:b], v, AX_X, ALU.add))
            then(dve.tensor_scalar(S["tile_expert"][0:1, NT:TILES], row_f[0:1, :], float(E - 1), None, ALU.min))
            at = lambda v, j: v.rearrange("p (j k) -> p j k", k=K)[:, j, :]
            for j in range(NT):
                u = j % 2
                if j >= 2:
                    dve.wait_ge(pair_ps, j - 1)
                dve.tensor_tensor(is_pos[:, u], S["count"][:].unsqueeze(1).broadcast_to([P, K, P]),
                                  at(V["slot_pos"], j).unsqueeze(2).broadcast_to([P, K, P]),
                                  ALU.is_equal).then_inc(onehot_ready, 1)
                then(dve.tensor_tensor(is_tile[:, u], S["count"][:, 0:ROUTED].unsqueeze(1).broadcast_to([P, K, ROUTED]),
                                       at(V["slot_tile"], j).unsqueeze(2).broadcast_to([P, K, ROUTED]), ALU.is_equal))
                dve.tensor_tensor(is_tile[:, u], is_tile[:, u],
                                  S["pair_row"][:, j, :].unsqueeze(2).broadcast_to([P, K, ROUTED]),
                                  ALU.mult).then_inc(onehot_ready, 1)
            dve.wait_ge(pair_ps, NT)
            pair = ps_pair[:, 0:ROUTED]
            then(dve.tensor_scalar(row_f, pair, -1.0, None, ALU.add))
            then(dve.tensor_scalar(empty, pair, 0.0, float(SKIP), ALU.is_equal, ALU.mult))
            then(dve.tensor_tensor(S["put"][:, NT:TILES], row_f, empty, ALU.add))
            then(dve.tensor_scalar(S["take"][:, NT:TILES], row_f, 0.0, None, ALU.max))
            then(dve.tensor_scalar(S["take"][:, NT:TILES], S["take"][:, NT:TILES], T - 1, None, ALU.bitwise_and))

        @block.scalar
        def _(act):
            act.wait_ge(var_ready, 1)
            act.activation(st["rstd"], st["t6"], ACT.Sqrt).then_inc(rstd_ready, 1)
            for j in range(NT):
                act.wait_ge(xt_ps, j + 1)
                if j >= 2:
                    act.wait_ge(logit_ps, j - 1)
                act.copy(xt[:, j % 2, :], ps_t[j % 2][:, 0:D]).then_inc(xt_ready, 1)
                act.wait_ge(logit_ps, j + 1)
                act.copy(logits[:, j, :], ps_l[j % 2][:, 0:E]).then_inc(logit_ready, 1)
            act.wait_ge(shifted_ready, 1)
            act.activation(exps, shifted, ACT.Exp).then_inc(exp_ready, 1)

        @block.tensor
        def _(pe):
            for j in range(NT):
                u = j % 2
                pe.wait_ge(xn_ready, j + 1)
                if j >= 2:
                    pe.wait_ge(xt_ready, j - 1)
                for f in range(DH):
                    mm = pe.transpose(ps_t[u][:, f * P:(f + 1) * P], xn[:, u, f * P:(f + 1) * P], S["ident"][:])
                mm.then_inc(xt_ps, 1)
                pe.wait_ge(xt_ready, j + 1)
                if j >= 2:
                    pe.wait_ge(logit_ready, j - 1)
                for f in range(DH):
                    pe.matmul(ps_l[u][:, 0:E], xt[:, u, f * P:(f + 1) * P], rt[:, f, :], start=(f == 0), stop=False)
                pe.matmul(ps_l[u][:, 0:E], S["ones"][0:1, :], S["rb"][:], start=False, stop=True).then_inc(logit_ps, 1)
            pe.wait_ge(members_ready, 1)
            flat = lambda v: v.rearrange("p j e -> p (j e)")
            pe.matmul(ps_cum[:, 0:NT * E], S["earlier"][:], flat(V["members"]), start=True, stop=False)
            pe.matmul(ps_cum[:, 0:NT * E], S["ones"][:], flat(V["before"]), start=False, stop=True)
            pe.matmul(ps_all[:, 0:E], S["ones"][:], members_all, start=True, stop=True).then_inc(cum_ps, 1)
            for j in range(NT):
                u = j % 2
                pe.wait_ge(onehot_ready, 2 * (j + 1))
                for k in range(K):
                    mm = pe.matmul(ps_pair[:, 0:ROUTED], is_pos[:, u, k, :], is_tile[:, u, k, :],
                                   start=(j == 0 and k == 0), stop=(j == NT - 1 and k == K - 1))
                mm.then_inc(pair_ps, 1)


def expert_tiles(nc, S, tag):
    W = carve(S["work"][:, NT * D:], [
        ("xg", (4, D)), ("xt", (2, D)), ("gated", (2, I)), ("h", (2, I)), ("ht", (2, D)), ("y", (4, D)),
        ("take4", (4,)), ("put4", (4,))])
    xg, xt, gated, h, ht, y = (W[n] for n in ("xg", "xt", "gated", "h", "ht", "y"))
    take4, put4 = W["take4"].bitcast(I32), W["put4"].bitcast(I32)
    bank = S["bank"]
    ps_x, ps_gu, ps_h, ps_y = bank[0:2], bank[2:4], bank[4:6], bank[6:8]
    g = lambda n: S["sem"](f"ffn_{n}")
    x_in = [S["sem"](f"{tag}_xg_in{u}") for u in range(4)]
    y_out = [S["sem"](f"{tag}_y_out{u}") for u in range(4)]
    take_ready, put_ready = g("take_ready"), g("put_ready")
    x_ps, x_ready = g("x_ps"), g("x_ready")
    gu_ps, gated_ready, h_ready = g("gu_ps"), g("gated_ready"), g("h_ready")
    h_ps, ht_ready = g("h_ps"), g("ht_ready")
    y_ps, y_ready = g("y_ps"), g("y_ready")
    U, WARM = 4, 2
    ROUNDS = (TILES - 4) // U

    def steps(eng, step, last):
        for s in range(WARM * U):
            step(s // U, s % U)
        with eng.Fori(WARM, ROUNDS) as n:
            for u in range(U):
                step(n, u)
        for s in range(ROUNDS * U, last):
            step(s // U, s % U)

    def back(n, u, by):
        return (n, u - by) if u >= by else (n - 1, u - by + U)

    def is_tile(n, u, ahead=0):
        return not isinstance(n, int) or 0 <= n * U + u + ahead < TILES

    def from_tile(n, u, first):
        return not isinstance(n, int) or n * U + u >= first

    with nc.Block() as block:
        @block.gpsimd
        def _(pool):
            last_row = pool.to_reg(ROWS - 1)

            def gather(u):
                pool.indirect_dma_start(xg[:, u, :], None, S["xln_d"],
                                        bass.IndirectOffsetOnAxis(ap=take4[:, u:u + 1], axis=0)).then_inc(x_in[u], 16)

            def scatter(u):
                pool.indirect_dma_start(S["res_d"], bass.IndirectOffsetOnAxis(ap=put4[:, u:u + 1], axis=0),
                                        y[:, u, :], None, bounds_check=last_row,
                                        oob_is_err=False).then_inc(y_out[u], 16)

            def step(n, u):
                s = n * U + u
                if isinstance(n, int):
                    if is_tile(n, u):
                        pool.wait_ge(take_ready, s + 1)
                        gather(u)
                    if from_tile(n, u, 4):
                        pool.wait_ge(put_ready, s - 3)
                        scatter(u)
                    return
                take_at, put_at = pool.to_reg(s + 1), pool.to_reg(s - 3)
                pool.wait_ge(take_ready, 1)
                pool.wait_ge(take_ready, take_at)
                gather(u)
                pool.wait_ge(put_ready, 1)
                pool.wait_ge(put_ready, put_at)
                scatter(u)

            steps(pool, step, TILES + 4)
            for u in range(4):
                pool.wait_ge(y_out[u], 16 * len(range(u, TILES, 4)))

        @block.vector
        def _(dve):
            def take_numbers(s, u):
                dve.tensor_copy(take4[:, u:u + 1], S["take"][:, bass.ds(s, 1)]).then_inc(take_ready, 1)

            for s in range(4):
                take_numbers(s, s)

            def step(n, u):
                s = n * U + u
                if is_tile(n, u):
                    dve.wait_ge(gated_ready, s + 1)
                    if from_tile(n, u, 2):
                        dve.wait_ge(h_ps, s - 1)
                    dve.tensor_tensor(h[:, u % 2, :], gated[:, u % 2, :], ps_gu[u % 2][:, I:2 * I],
                                      ALU.mult).then_inc(h_ready, 1)
                    if is_tile(n, u, 4):
                        take_numbers(s + 4, u)
                if from_tile(n, u, 2):
                    m, v = back(n, u, 2)
                    dve.wait_ge(y_ps, s - 1)
                    if from_tile(n, u, 6):
                        dve.wait_ge(y_out[v], m * 16)
                    dve.tensor_copy(y[:, v, :], ps_y[u % 2][:, 0:D]).then_inc(y_ready, 1)
                    dve.wait_ge(y_ready, s - 1)
                    dve.tensor_copy(put4[:, v:v + 1], S["put"][:, bass.ds(s - 2, 1)]).then_inc(put_ready, 1)

            steps(dve, step, TILES + 2)

        @block.scalar
        def _(act):
            def x_copy(s, n, u):
                act.wait_ge(x_ps, s + 1)
                if from_tile(n, u, 2):
                    act.wait_ge(gu_ps, s - 1)
                act.copy(xt[:, u % 2, :], ps_x[u % 2][:, 0:D]).then_inc(x_ready, 1)

            def step(n, u):
                s = n * U + u
                if is_tile(n, u):
                    act.wait_ge(gu_ps, s + 1)
                    if from_tile(n, u, 2):
                        act.wait_ge(h_ready, s - 1)
                    act.activation(gated[:, u % 2, :], ps_gu[u % 2][:, 0:I], ACT.Silu).then_inc(gated_ready, 1)
                if is_tile(n, u, -1):
                    v = (u + 1) % 2
                    act.wait_ge(h_ps, s)
                    if from_tile(n, u, 3):
                        act.wait_ge(y_ps, s - 2)
                    act.copy(ht[:, v, 0:P], ps_h[v][:, 0:P]).then_inc(ht_ready, 1)
                    act.copy(ht[0:IR, v, P:D], ps_h[v][0:IR, P:D]).then_inc(ht_ready, 1)
                if is_tile(n, u, 1):
                    x_copy(s + 1, n, u + 1)

            x_copy(0, 0, 0)
            steps(act, step, TILES + 1)

        @block.tensor
        def _(pe):
            def turn_x(s, n, u):
                pe.wait_ge(x_in[u], n * 16 + 16)
                if from_tile(n, u, 2):
                    pe.wait_ge(x_ready, s - 1)
                for f in range(DH):
                    mm = pe.transpose(ps_x[u % 2][:, f * P:(f + 1) * P], xg[:, u, f * P:(f + 1) * P], S["ident"][:])
                mm.then_inc(x_ps, 1)

            def gate_up(s, n, u, e):
                pe.wait_ge(x_ready, s + 1)
                if from_tile(n, u, 2):
                    pe.wait_ge(h_ready, s - 1)
                for f in range(DH):
                    mm = pe.matmul(ps_gu[u % 2][:, 0:2 * I], xt[:, u % 2, f * P:(f + 1) * P],
                                   S["w_gu"][:, bass.ds(e, 1), f * 2 * I:(f + 1) * 2 * I],
                                   start=(f == 0), stop=(f == DH - 1))
                mm.then_inc(gu_ps, 1)

            def turn_h(s, n, u):
                pe.wait_ge(h_ready, s + 1)
                if from_tile(n, u, 2):
                    pe.wait_ge(ht_ready, s * 2 - 2)
                pe.transpose(ps_h[u % 2][:, 0:P], h[:, u % 2, 0:P], S["ident"][:])
                pe.transpose(ps_h[u % 2][0:IR, P:D], h[:, u % 2, P:I], S["ident"][:]).then_inc(h_ps, 1)

            def down(s, n, u, e):
                pe.wait_ge(ht_ready, s * 2 + 2)
                if from_tile(n, u, 2):
                    pe.wait_ge(y_ready, s - 1)
                pe.matmul(ps_y[u % 2][:, 0:D], ht[:, u % 2, 0:P], S["w_d1"][:, bass.ds(e, 1), :],
                          start=True, stop=False)
                pe.matmul(ps_y[u % 2][:, 0:D], ht[0:IR, u % 2, P:D], S["w_d2"][0:IR, bass.ds(e, 1), :],
                          start=False, stop=True).then_inc(y_ps, 1)

            def expert_of(s):
                return pe.value_load(S["tile_expert"][0:1, bass.ds(s, 1)], min_val=0, max_val=E)

            def step(n, u):
                s = n * U + u
                if is_tile(n, u):
                    gate_up(s, n, u, expert_of(s))
                if is_tile(n, u, -1):
                    turn_h(s - 1, *back(n, u, 1))
                if is_tile(n, u, -2):
                    down(s - 2, *back(n, u, 2), expert_of(s - 2))
                if is_tile(n, u, 1):
                    turn_x(s + 1, *((n, u + 1) if u + 1 < U else (n + 1, 0)))

            if tag == "a":
                pe.wait_ge(S["weights_in"], 16 * WEIGHT_LOADS)
            turn_x(0, 0, 0)
            steps(pe, step, TILES + 2)


def combine(nc, S, tag, out_d):
    V = ffn_views(S)
    x = V["x"]
    rows = S["work"][:, NT * D:NT * D + 2 * (K + 1) * D].rearrange("p (u k n) -> p u k n", u=2, k=K + 1)
    res = S["res_d"].rearrange("(k j p) n -> j p k n", p=P, j=NT)
    out = out_d.rearrange("(j p) n -> j p n", p=P)
    rows_in = [S["sem"](f"ffn_rows_in{u}") for u in range(2)]
    added, stored = S["sem"](f"ffn_added"), S["sem"](f"ffn_stored")

    with nc.Block() as block:
        @block.sync
        def _(sp):
            for j in range(NT):
                if j >= 2:
                    sp.wait_ge(added, (K + 1) * (j - 1))
                sp.dma_start(rows[:, j % 2, :, :], res[j]).then_inc(rows_in[j % 2], 16)

        @block.scalar
        def _(act):
            for j in range(NT):
                act.wait_ge(added, (K + 1) * (j + 1))
                act.dma_start(out[j], x[:, j, :]).then_inc(stored, 16)
            act.wait_ge(stored, 16 * NT)

        @block.vector
        def _(dve):
            for j in range(NT):
                dve.wait_ge(rows_in[j % 2], 16 * (j // 2 + 1))
                for k in range(K + 1):
                    if k:
                        dve.wait_ge(added, (K + 1) * j + k)
                    dve.scalar_tensor_tensor(out=x[:, j, :], in0=rows[:, j % 2, k, :],
                                             scalar=S["mix"][:, j, k:k + 1] if k < K else 0.5, in1=x[:, j, :],
                                             op0=ALU.mult, op1=ALU.add).then_inc(added, 1)


ATT = [("kt", (NC, 2 * C)), ("qt", (NC, 2 * C)), ("r", (NC, 2 * DK)), ("eta", (NC, 2))]
IN_HEADS = "p (h e) -> p h e"


def attention_inputs(nc, S, d):
    V = carve(S["work"], ATT + [
        ("w_kv", (DH, 2 * D)), ("w_q", (DH, D + 2 * H)), ("stat", (120,)), ("xn", (D,)), ("xt", (D,)),
        ("eta_n", (NT * H,)), ("ss", (NT * H,)), ("q", (D + H,)), ("gate", (D,)), ("mean_r", (2, H))])
    R2 = carve(S["work"][:, 6272:], [("kn", (2, D)), ("z", (2, D)), ("w_row", (D,)), ("b_row", (D,)), ("tmp", (2 * D,))])
    rows_of = S["work"][:, 6272:6272 + CT * P]
    kt, qt, xn, xt, q, gate = (V[n] for n in ("kt", "qt", "xn", "xt", "q", "gate"))
    w_kv, w_q, ss, eta_n = V["w_kv"], V["w_q"], V["ss"], V["eta_n"]
    w_g2, g1 = S["aux"][0:H, 0:D], S["aux"][0:H, D:D + P]
    tiles = lambda v: v.rearrange("p i n -> p (i n)").rearrange("p (j n) -> p j n", j=NT)
    x, v_nat = tiles(kt), tiles(V["r"])
    by_chunk = lambda t, j: t[:, j * CT:(j + 1) * CT, :].rearrange("p r (f c) -> p f r c", f=2)
    st = stat_views(V["stat"])
    bank = S["bank"]
    ps_t, ps_kv, ps_q, ps_g1, ps_gate, ps_sq = bank[0], bank[1], bank[2], bank[3], bank[4], bank[5]
    ps_qt = bank[6]
    g = lambda n: S["sem"](f"att_{n}")
    w_in, x_in, var_ready, rstd_ready = g("w_in"), g("x_in"), g("var_ready"), g("rstd_ready")
    xn_ready, xt_ps, xt_ready = g("xn_ready"), g("xt_ps"), g("xt_ready")
    g1_ps, g1_ready, q_ps, sig_ready, q_ready = g("g1_ps"), g("g1_ready"), g("q_ps"), g("sig_ready"), g("q_ready")
    kv_ps, kv_read, gate_ps, gate_ready = g("kv_ps"), g("kv_read"), g("gate_ps"), g("gate_ready")
    qt_ps, qt_ready, v_ready = g("qt_ps"), g("qt_ready"), g("v_ready")
    q_out, gate_out = g("q_out"), g("gate_out")

    with nc.Block() as block:
        @block.sync
        def _(sp):
            sp.dma_start(w_kv[:], d["w_kv"]).then_inc(w_in, 16)
            sp.dma_start(w_q[:], d["w_q"]).then_inc(w_in, 16)
            sp.dma_start(w_g2, d["w_g2"]).then_inc(w_in, 16)
            sp.wait_ge(w_in, 48)
            q_rows = S["q_d"].rearrange("(j p) n -> j p n", p=P)
            gate_rows = S["gate_d"].rearrange("(j p) n -> j p n", p=P)
            for j in range(NT):
                sp.wait_ge(q_ready, 2 * (j + 1))
                sp.dma_start(q_rows[j], q[:, 0:D]).then_inc(q_out, 16)
                sp.wait_ge(gate_ready, j + 1)
                sp.dma_start(gate_rows[j], gate[:]).then_inc(gate_out, 16)
            sp.wait_ge(q_out, 16 * NT)
            sp.wait_ge(gate_out, 16 * NT)

        @block.vector
        def _(dve):
            layer_stats(nc, dve, var_ready, st, x, None, "att", S["sem"])
            dve.wait_ge(rstd_ready, 1)
            for j in range(NT):
                if j:
                    dve.wait_ge(xt_ps, j)
                dve.tensor_scalar(xn, x[:, j, :], st["mean"][:, j:j + 1], st["rstd"][:, j:j + 1],
                                  ALU.subtract, ALU.mult).then_inc(xn_ready, 1)
                dve.wait_ge(sig_ready, j + 1)
                dve.tensor_tensor(q[:, 0:D], q[:, 0:D], ps_q[:, 0:D], ALU.mult).then_inc(q_ready, 1)
                dve.tensor_scalar(eta_n[:, j * H:(j + 1) * H], q[:, D:D + H], 2.0, None, ALU.mult).then_inc(q_ready, 1)
                dve.wait_ge(kv_read, j + 1)
                dve.tensor_reduce(ss[:, j * H:(j + 1) * H], ps_sq[:, 0:D].rearrange(IN_HEADS, e=DK), AX_X,
                                  ALU.add).then_inc(v_ready, 1)
                dve.tensor_copy(v_nat[:, j, :], ps_kv[:, D:2 * D]).then_inc(v_ready, 1)

        @block.scalar
        def _(act):
            act.wait_ge(var_ready, 1)
            act.activation(st["rstd"], st["t6"], ACT.Sqrt).then_inc(rstd_ready, 1)
            for j in range(NT):
                act.wait_ge(xt_ps, j + 1)
                if j:
                    act.wait_ge(kv_ps, j)
                act.copy(xt, ps_t[:, 0:D]).then_inc(xt_ready, 1)
                act.wait_ge(g1_ps, j + 1)
                if j:
                    act.wait_ge(gate_ps, j)
                act.copy(g1, ps_g1[IR:IR + H, 0:P]).then_inc(g1_ready, 1)
                act.wait_ge(q_ps, j + 1)
                if j:
                    act.wait_ge(q_out, 16 * j)
                    act.wait_ge(qt_ps, j)
                    act.wait_ge(q_ready, 2 * j)
                act.activation(q[:, 0:D + H], ps_q[:, 0:D + H], ACT.Sigmoid).then_inc(sig_ready, 1)
                act.wait_ge(kv_ps, j + 1)
                if j:
                    act.wait_ge(v_ready, 2 * j)
                act.copy(x[:, j, :], ps_kv[:, 0:D])
                act.activation(ps_sq[:, 0:D], ps_kv[:, 0:D], ACT.Square).then_inc(kv_read, 1)
                act.wait_ge(gate_ps, j + 1)
                if j:
                    act.wait_ge(gate_out, 16 * j)
                act.activation(gate[:], ps_gate[:, 0:D], ACT.Sigmoid).then_inc(gate_ready, 1)
                act.wait_ge(qt_ps, j + 1)
                act.copy(by_chunk(qt, j), ps_qt[:, 0:D].rearrange("p (f r c) -> p f r c", f=2, r=CT)).then_inc(qt_ready, 1)

        @block.tensor
        def _(pe):
            pe.wait_ge(w_in, 48)
            for j in range(NT):
                pe.wait_ge(xn_ready, j + 1)
                if j:
                    pe.wait_ge(xt_ready, j)
                for f in range(DH):
                    mm = pe.transpose(ps_t[:, f * P:(f + 1) * P], xn[:, f * P:(f + 1) * P], S["ident"][:])
                mm.then_inc(xt_ps, 1)
                pe.wait_ge(xt_ready, j + 1)
                if j:
                    pe.wait_ge(g1_ready, j)
                for f in range(DH):
                    mm = pe.matmul(ps_g1[IR:IR + H, 0:P], w_q[:, f, D + H:D + 2 * H], xt[:, f * P:(f + 1) * P],
                                   start=(f == 0), stop=(f == DH - 1))
                mm.then_inc(g1_ps, 1)
                if j:
                    pe.wait_ge(q_ready, 2 * j)
                for f in range(DH):
                    mm = pe.matmul(ps_q[:, 0:D + H], xt[:, f * P:(f + 1) * P], w_q[:, f, 0:D + H],
                                   start=(f == 0), stop=(f == DH - 1))
                mm.then_inc(q_ps, 1)
                if j:
                    pe.wait_ge(v_ready, 2 * j)
                for f in range(DH):
                    mm = pe.matmul(ps_kv[:, 0:2 * D], xt[:, f * P:(f + 1) * P], w_kv[:, f, :],
                                   start=(f == 0), stop=(f == DH - 1))
                mm.then_inc(kv_ps, 1)
                pe.wait_ge(g1_ready, j + 1)
                if j:
                    pe.wait_ge(gate_ready, j)
                pe.matmul(ps_gate[:, 0:D], g1, w_g2, start=True, stop=True).then_inc(gate_ps, 1)
                pe.wait_ge(q_ready, 2 * (j + 1))
                if j:
                    pe.wait_ge(qt_ready, j)
                for f in range(DH):
                    mm = pe.transpose(ps_qt[:, f * P:(f + 1) * P], q[:, f * P:(f + 1) * P], S["ident"][:])
                mm.then_inc(qt_ps, 1)

    kn, z, w_row, b_row = R2["kn"], R2["z"], R2["w_row"], R2["b_row"]
    rows_ready = g("rows_ready")
    row_in, ss_ready, norm_ready = g("row_in"), g("ss_ready"), g("norm_ready")
    kn_ready, kt_ps, kt_ready, z_ready, zw_ready = g("kn_ready"), g("kt_ps"), g("kt_ready"), g("z_ready"), g("zw_ready")
    r_ready, r_out, eta_ps, step, w_step = g("r_ready"), [g("r_out0"), g("r_out1")], g("eta_ps"), g("step"), g("w_step")
    ps_e = bank[2:4]
    with nc.Block() as block:
        @block.sync
        def _(sp):
            sp.dma_start(w_row, d["ln_w_row"].broadcast_to([P, D])).then_inc(row_in, 16)
            sp.dma_start(b_row, d["ln_b_row"].broadcast_to([P, D])).then_inc(row_in, 16)
            rows = S["r_d"].rearrange("(j p) n -> j p n", p=P)
            for j in range(NT):
                sp.wait_ge(r_ready, j + 1)
                sp.dma_start(rows[j], z[:, j % 2, :]).then_inc(r_out[j % 2], 16)
            for u in range(2):
                sp.wait_ge(r_out[u], 16 * NT // 2)

        @block.vector
        def _(dve):
            n = [0]

            def then(ins):
                n[0] += 1
                ins.then_inc(step, 1)
                dve.wait_ge(step, n[0])

            dve.tensor_copy(rows_of.rearrange("p (r h c) -> p r h c", h=HH, c=C),
                            S["ident"][:].rearrange("p (r c) -> p r c", c=C).unsqueeze(2).broadcast_to([P, CT, HH, C])
                            ).then_inc(rows_ready, 1)
            then(dve.tensor_scalar(ss, ss, EPS, None, ALU.add))
            dve.reciprocal(ss, ss).then_inc(ss_ready, 1)
            tmp = R2["tmp"].rearrange("p (n f h) -> p n f h", f=2, h=HH)
            dve.wait_ge(eta_ps, 1)
            own = S["same_head"][:].rearrange("p (h c) -> p h c", c=C)[:, :, 0]
            for b in range(2):
                then(dve.tensor_tensor(tmp, ps_e[b][:].rearrange("p (n f h) -> p n f h", f=2, h=HH),
                                       own.unsqueeze(1).unsqueeze(1).broadcast_to([P, 4 * NT, 2, HH]), ALU.mult))
                for r in range(4):
                    dst = V["eta"].rearrange("p (j r) f -> p r j f", r=CT)[:, 4 * b + r]
                    then(dve.tensor_reduce(dst, tmp[:, r * NT:(r + 1) * NT], AX_X, ALU.add))
            dve.wait_ge(norm_ready, 1)

            def k_and_z(j):
                u = j % 2
                if j >= 2:
                    dve.wait_ge(kt_ps, j - 1)
                    dve.wait_ge(r_out[u], 16 * (j // 2))
                dve.tensor_tensor(kn[:, u].rearrange(IN_HEADS, e=DK), x[:, j, :].rearrange(IN_HEADS, e=DK),
                                  ss[:, j * H:(j + 1) * H].unsqueeze(2).broadcast_to([P, H, DK]),
                                  ALU.mult).then_inc(kn_ready, 1)
                dve.wait_ge(kn_ready, j + 1)
                dve.tensor_tensor(z[:, u], v_nat[:, j, :], kn[:, u], ALU.subtract).then_inc(z_ready, 1)

            k_and_z(0)
            for j in range(NT):
                u = j % 2
                if j + 1 < NT:
                    k_and_z(j + 1)
                dve.wait_ge(zw_ready, j + 1)
                then(dve.tensor_reduce(V["mean_r"][:, u, :], z[:, u].rearrange(IN_HEADS, e=DK), AX_X, ALU.add))
                dve.scalar_tensor_tensor(out=z[:, u].rearrange(IN_HEADS, e=DK),
                                         in0=V["mean_r"][:, u, :].unsqueeze(2).broadcast_to([P, H, DK]),
                                         scalar=-1.0 / DK, in1=z[:, u].rearrange(IN_HEADS, e=DK), op0=ALU.mult,
                                         op1=ALU.add).then_inc(r_ready, 1)

        @block.gpsimd
        def _(pool):
            pool.wait_ge(row_in, 32)
            for j in range(NT):
                u = j % 2
                pool.wait_ge(z_ready, j + 1)
                pool.tensor_tensor(z[:, u], z[:, u], b_row, ALU.subtract).then_inc(w_step, 1)
                pool.wait_ge(w_step, j + 1)
                pool.tensor_tensor(z[:, u], z[:, u], w_row, ALU.mult).then_inc(zw_ready, 1)

        @block.scalar
        def _(act):
            act.wait_ge(ss_ready, 1)
            act.activation(ss, ss, ACT.Sqrt).then_inc(norm_ready, 1)
            for j in range(NT):
                act.wait_ge(kt_ps, j + 1)
                act.copy(by_chunk(kt, j), bank[j % 2][:, 0:D].rearrange("p (f r c) -> p f r c", f=2, r=CT)).then_inc(kt_ready, 1)

        @block.tensor
        def _(pe):
            pe.wait_ge(rows_ready, 1)
            for r in range(CT):
                mm = pe.matmul(ps_e[r // 4][:, (r % 4) * P:(r % 4 + 1) * P],
                               rows_of[:, r * P:(r + 1) * P], eta_n,
                               start=True, stop=True)
            mm.then_inc(eta_ps, 1)
            for j in range(NT):
                pe.wait_ge(kn_ready, j + 1)
                if j >= 2:
                    pe.wait_ge(kt_ready, j - 1)
                for f in range(DH):
                    mm = pe.transpose(bank[j % 2][:, f * P:(f + 1) * P], kn[:, j % 2, f * P:(f + 1) * P], S["ident"][:])
                mm.then_inc(kt_ps, 1)


def scan(nc, S, d):
    V = carve(S["work"], ATT + [
        ("eta2", (NC, 2)), ("k_bd", (2, 2 * P)), ("q_bd", (2, 2 * P)), ("kq_bd", (2, 2 * P)), ("k_n", (2, 2 * P)),
        ("kq", (2, 2 * C)), ("state", (2 * DK,)), ("one_a", (2, 2 * DK)), ("terms", (2, 5 * (DK + 1))),
        ("sums", (2, 4)), ("rho", (2,)), ("rho2", (2,)), ("root", (2,)), ("ae", (2,)), ("s1", (2,)), ("s2", (2,)),
        ("u1", (2, DK)), ("u2", (2, DK)), ("e1", (2, DK)), ("e2", (2, DK)), ("v", (2, 2 * DK)), ("smean", (2,)),
        ("zero", (2 * DK,))])
    kt, qt, r, eta, eta2 = (V[n] for n in ("kt", "qt", "r", "eta", "eta2"))
    halves = lambda t: t.rearrange("p (f n) -> p f n", f=2)
    terms = V["terms"].rearrange("p f (g e) -> p f g e", g=5)
    one_a = V["one_a"].rearrange("p f (g e) -> p f g e", g=2)
    state = V["state"]
    bank = S["bank"]
    ps_kh, ps_s, ps_kn, ps_kq, ps_o = bank[0], bank[1], bank[2:4], bank[4:6], bank[6:8]
    g = lambda n: S["sem"](f"scan_{n}")
    r_in, a_in, setup, zeroed = g("r_in"), g("a_in"), g("setup"), g("zeroed")
    k_ready, q_ready, kq_ready = g("k_bd_ready"), g("q_bd_ready"), g("kq_bd_ready")
    prep_ps, kn_ready, kqc_ready = g("prep_ps"), g("kn_ready"), g("kqc_ready")
    state_ready, kh_ps, rho2_ready, root_ready, v_ready = (
        g("state_ready"), g("kh_ps"), g("rho2_ready"), g("root_ready"), g("v_ready"))
    s_ps, o_ps, o_ready, step = g("s_ps"), g("o_ps"), g("o_ready"), g("step")
    OPS = 17

    def chunks(eng, body):
        body(0, 0)
        body(1, 1)
        with eng.Fori(1, NC // 2) as n:
            body(n * 2, 0)
            body(n * 2 + 1, 1)

    later = lambda i: not isinstance(i, int)
    chunk = lambda t, i: t[:, bass.ds(i, 1), :].rearrange("p a (f c) -> p (a f) c", f=2)

    with nc.Block() as block:
        @block.sync
        def _(sp):
            src = S["r_d"].rearrange("(i c) (f h e) -> h f c i e", c=C, f=2, h=HH)
            for h in range(HH):
                for f in range(2):
                    sp.dma_start(r[h * C:(h + 1) * C, :, f * DK:(f + 1) * DK], src[h, f]).then_inc(r_in, 16)
            w = d["ln_w"]
            for f in range(2):
                sp.dma_start(one_a[:, f, 1, :], w[f * HH:(f + 1) * HH, :].unsqueeze(1).broadcast_to([HH, C, DK])
                             ).then_inc(a_in, 16)

        @block.gpsimd
        def _(pool):
            heads = lambda t: t.rearrange("p (f h c) -> p f h c", f=2, h=HH)
            mask = lambda m: m[:].rearrange("p (h c) -> p h c", h=HH).unsqueeze(1).broadcast_to([P, 2, HH, C])
            wide = lambda t: t.unsqueeze(2).broadcast_to([P, 2, HH, C])

            def spread_k(i, u):
                if later(i) or i >= 2:
                    pool.wait_ge(kh_ps, i - 1)
                pool.tensor_tensor(heads(V["k_bd"][:, u]), wide(chunk(kt, i)), mask(S["same_head"]),
                                   ALU.mult).then_inc(k_ready, 1)

            def body(i, u):
                if later(i) or i >= 2:
                    pool.wait_ge(o_ps, i - 1)
                pool.tensor_tensor(heads(V["q_bd"][:, u]), wide(chunk(qt, i)), mask(S["same_head"]),
                                   ALU.mult).then_inc(q_ready, 1)
                pool.wait_ge(kqc_ready, i + 1)
                pool.tensor_tensor(heads(V["kq_bd"][:, u]), wide(halves(V["kq"][:, u])), mask(S["causal"]),
                                   ALU.mult).then_inc(kq_ready, 1)

            spread_k(0, 0)
            spread_k(1, 1)
            body(0, 0)
            spread_k(2, 0)
            body(1, 1)
            spread_k(3, 1)
            with pool.Fori(1, NC // 2 - 1) as n:
                for u in range(2):
                    body(n * 2 + u, u)
                    spread_k(n * 2 + (u + 2), u)
            body(NC - 2, 0)
            body(NC - 1, 1)

        @block.scalar
        def _(act):
            act.wait_ge(a_in, 32)
            act.activation(one_a[:, :, 0, :], one_a[:, :, 1, :], ACT.Square).then_inc(setup, 1)

            def prepared(i, u):
                act.wait_ge(prep_ps, i + 1)
                if later(i) or i >= 2:
                    act.wait_ge(s_ps, i - 1)
                    act.wait_ge(kq_ready, i - 1)
                act.activation(V["k_n"][:, u], ps_kn[u][:, 0:2 * P], ACT.Copy, scale=-1.0).then_inc(kn_ready, 1)
                act.activation(V["kq"][:, u], ps_kq[u][:, 0:2 * C], ACT.Copy, scale=-1.0).then_inc(kqc_ready, 1)

            def body(i, u, more=True):
                if more:
                    prepared(i + 1, 1 - u)
                act.wait_ge(rho2_ready, i + 1)
                act.activation(V["root"], V["rho2"], ACT.Sqrt, scale=float(DK)).then_inc(root_ready, 1)
                act.wait_ge(o_ps, i + 1)
                act.copy(r[:, bass.ds(i, 1), :].rearrange("p a n -> p (a n)"), ps_o[u][:, 0:2 * DK]).then_inc(o_ready, 1)

            prepared(0, 0)
            body(0, 0)
            body(1, 1)
            with act.Fori(1, NC // 2 - 1) as n:
                body(n * 2, 0)
                body(n * 2 + 1, 1)
            body(NC - 2, 0)
            body(NC - 1, 1, False)

        @block.tensor
        def _(pe):
            def prepare(i, u):
                pe.wait_ge(k_ready, i + 1)
                if later(i) or i >= 2:
                    pe.wait_ge(kqc_ready, i - 1)
                for f in range(2):
                    pe.transpose(ps_kn[u][:, f * P:(f + 1) * P], V["k_bd"][:, u, f * P:(f + 1) * P], S["ident"][:])
                q = chunk(qt, i)
                for f in range(2):
                    mm = pe.matmul(ps_kq[u][:, f * C:(f + 1) * C], V["k_bd"][:, u, f * P:(f + 1) * P], q[:, f, :],
                                   start=True, stop=True)
                mm.then_inc(prep_ps, 1)

            def body(i, u, more=True):
                half = lambda t, f, n: t[:, f * n:(f + 1) * n]
                pe.wait_ge(state_ready, i + 1)
                for f in range(2):
                    mm = pe.matmul(half(ps_kh, f, DK), half(V["k_bd"][:, u], f, P), half(state, f, DK),
                                   start=True, stop=True)
                mm.then_inc(kh_ps, 1)
                if more:
                    prepare(i + 1, 1 - u)
                pe.wait_ge(q_ready, i + 1)
                if later(i) or i >= 2:
                    pe.wait_ge(o_ready, i - 1)
                for f in range(2):
                    pe.matmul(half(ps_o[u], f, DK), half(V["q_bd"][:, u], f, P), half(state, f, DK),
                              start=(f == 0), stop=False, skip_group_check=True)
                pe.wait_ge(v_ready, 2 * (i + 1) if not later(i) else i * 2 + 2)
                pe.wait_ge(kn_ready, i + 1)
                for f in range(2):
                    mm = pe.matmul(half(ps_s, f, DK), half(V["k_n"][:, u], f, P), half(V["v"][:, u], f, DK),
                                   start=False, stop=False, skip_group_check=True)
                mm.then_inc(s_ps, 1)
                pe.wait_ge(kq_ready, i + 1)
                for f in range(2):
                    mm = pe.matmul(half(ps_o[u], f, DK), half(V["kq_bd"][:, u], f, P), half(V["v"][:, u], f, DK),
                                   start=False, stop=(f == 1), skip_group_check=True)
                mm.then_inc(o_ps, 1)

            pe.wait_ge(zeroed, 1)
            pe.matmul(ps_s[:, 0:2 * DK], S["ident"][:], V["zero"], start=True, stop=False, skip_group_check=True)
            prepare(0, 0)
            body(0, 0)
            body(1, 1)
            with pe.Fori(1, NC // 2 - 1) as n:
                body(n * 2, 0)
                body(n * 2 + 1, 1)
            body(NC - 2, 0)
            body(NC - 1, 1, False)

        @block.vector
        def _(dve):
            f2 = lambda t: t.unsqueeze(2).broadcast_to([P, 2, DK])
            dve.memset(V["zero"], 0.0).then_inc(zeroed, 1)
            dve.memset(V["terms"], 0.0).then_inc(step, 1)
            dve.wait_ge(step, 1)
            dve.memset(terms[:, :, 3, DK:DK + 1], float(DK) * EPS).then_inc(step, 1)
            dve.tensor_tensor(eta2, eta, eta, ALU.mult).then_inc(step, 1)
            dve.wait_ge(setup, 1)
            dve.tensor_scalar(one_a[:, :, 1, :], one_a[:, :, 0, :], -float(DK), None, ALU.mult).then_inc(step, 1)
            dve.wait_ge(step, 4)
            dve.memset(one_a[:, :, 0, :], 1.0).then_inc(step, 1)
            dve.wait_ge(step, 5)
            dve.wait_ge(r_in, 16 * 2 * HH)
            base = 5

            def body(i, u):
                def counted(ins):
                    ins.then_inc(step, 1)

                def upto(n):
                    dve.wait_ge(step, i * OPS + (base + n))

                eta_i = eta[:, bass.ds(i, 1), :].rearrange("p a f -> p (a f)")
                eta2_i = eta2[:, bass.ds(i, 1), :].rearrange("p a f -> p (a f)")
                r_i = chunk(r, i)
                x_ps = halves(ps_kh[:, 0:2 * DK])
                x = terms[:, :, 0, 0:DK]
                sums = V["sums"]
                rho, s1, s2, root = V["rho"], V["s1"], V["s2"], V["root"]
                if later(i) or i >= 1:
                    dve.wait_ge(s_ps, i)
                    dve.tensor_copy(state, ps_s[:, 0:2 * DK]).then_inc(state_ready, 1)
                else:
                    dve.tensor_copy(state, V["zero"]).then_inc(state_ready, 1)
                dve.wait_ge(kh_ps, i + 1)
                counted(dve.tensor_tensor(terms[:, :, 0:2, 0:DK], x_ps.unsqueeze(2).broadcast_to([P, 2, 2, DK]),
                                          one_a, ALU.mult))
                counted(dve.tensor_tensor(terms[:, :, 2, 0:DK], x_ps, r_i, ALU.mult))
                upto(1)
                counted(dve.tensor_tensor(terms[:, :, 3:5, 0:DK], terms[:, :, 0:2, 0:DK],
                                          x.unsqueeze(2).broadcast_to([P, 2, 2, DK]), ALU.mult))
                upto(3)
                counted(dve.tensor_reduce(sums, terms[:, :, 1:5, :], AX_X, ALU.add))
                upto(4)
                counted(dve.reciprocal(rho, sums[:, :, 2]))
                counted(dve.scalar_tensor_tensor(out=V["u1"], in0=f2(sums[:, :, 0]), scalar=1.0 / DK,
                                                 in1=terms[:, :, 1, 0:DK], op0=ALU.mult, op1=ALU.subtract))
                counted(dve.tensor_tensor(V["ae"], sums[:, :, 3], eta_i, ALU.mult))
                upto(5)
                dve.tensor_tensor(V["rho2"], rho, eta2_i, ALU.mult).then_inc(rho2_ready, 1)
                counted(dve.tensor_tensor(s2, rho, sums[:, :, 1], ALU.mult))
                upto(7)
                for f in range(2):
                    counted(dve.tensor_scalar(s1[:, f:f + 1], V["ae"][:, f:f + 1], rho[:, f:f + 1], rho[:, f:f + 1],
                                              ALU.mult, ALU.mult))
                for f in range(2):
                    counted(dve.tensor_scalar(V["u2"][:, f], V["u1"][:, f], eta_i[:, f:f + 1], rho[:, f:f + 1],
                                              ALU.mult, ALU.mult))
                upto(8)
                for f in range(2):
                    counted(dve.scalar_tensor_tensor(out=V["e2"][:, f], in0=x[:, f], scalar=s2[:, f:f + 1],
                                                     in1=r_i[:, f], op0=ALU.mult, op1=ALU.subtract))
                upto(12)
                for f in range(2):
                    counted(dve.scalar_tensor_tensor(out=V["e1"][:, f], in0=x[:, f], scalar=s1[:, f:f + 1],
                                                     in1=V["u2"][:, f], op0=ALU.mult, op1=ALU.add))
                counted(dve.tensor_copy(V["smean"], sums[:, :, 0]))
                upto(16)
                dve.wait_ge(root_ready, i + 1)
                for f in range(2):
                    dve.scalar_tensor_tensor(out=V["v"][:, u, f * DK:(f + 1) * DK], in0=V["e2"][:, f],
                                             scalar=root[:, f:f + 1], in1=V["e1"][:, f], op0=ALU.mult,
                                             op1=ALU.add).then_inc(v_ready, 1)

            chunks(dve, body)


def attention_output(nc, S, d, x1_d, x2_d):
    V = carve(S["work"], [
        ("qh", (NT, D)), ("q", (NT, D)), ("r", (NC, 2 * DK)), ("gate", (NT, D)), ("w_o", (DH, D)), ("w_row", (D,)),
        ("b_row", (D,)), ("norm", (DH,)), ("ss", (NT * H,)), ("mean", (NT * H,))])
    qh, q, r, gate, w_o, ss, mean = (V[n] for n in ("qh", "q", "r", "gate", "w_o", "ss", "mean"))
    x1 = r.rearrange("p i n -> p (i n)").rearrange("p (j n) -> p j n", j=NT)
    turned = q
    bank = S["bank"]
    g = lambda n: S["sem"](f"out_{n}")
    o_out, load, qh_in, x1_in = g("o_out"), g("load"), g("qh_in"), g("x1_in")
    centred, sq_ps, ss_done, var_ready, rstd_ready = g("centred"), g("sq_ps"), g("ss_done"), g("var_ready"), g("rstd_ready")
    scaled, wb_done, gated, ot_ps, ot_ready, y_ps, y_done, y_out = (
        g("scaled"), g("wb_done"), g("gated"), g("ot_ps"), g("ot_ready"), g("y_ps"), g("y_done"), g("y_out"))
    step, w_step, unit = g("step"), g("w_step"), g("unit")
    with nc.Block() as block:
        @block.sync
        def _(sp):
            dst = S["qh_d"].rearrange("(i c) (f h e) -> h f c i e", c=C, f=2, h=HH)
            for h in range(HH):
                for f in range(2):
                    sp.dma_start(dst[h, f], r[h * C:(h + 1) * C, :, f * DK:(f + 1) * DK]).then_inc(o_out, 16)
            sp.wait_ge(o_out, 16 * 2 * HH)
            sp.dma_start(qh, by_tile(S["qh_d"])).then_inc(qh_in, 16)
            sp.dma_start(x1, by_tile(x1_d)).then_inc(x1_in, 16)
            rows = x2_d.rearrange("(j p) n -> j p n", p=P)
            for j in range(NT):
                sp.wait_ge(y_done, j + 1)
                sp.dma_start(rows[j], x1[:, j, :]).then_inc(y_out, 16)
            sp.wait_ge(y_out, 16 * NT)

        @block.scalar
        def _(act):
            act.dma_start(q, by_tile(S["q_d"])).then_inc(load, 16)
            act.dma_start(gate, by_tile(S["gate_d"])).then_inc(load, 16)
            act.dma_start(w_o, d["w_o"]).then_inc(load, 16)
            act.dma_start(V["norm"], d["norm_w"]).then_inc(load, 16)
            act.dma_start(V["w_row"], d["ln_w_row"].broadcast_to([P, D])).then_inc(load, 16)
            act.dma_start(V["b_row"], d["ln_b_row"].broadcast_to([P, D])).then_inc(load, 16)

            def squares(j, n, ready):
                act.wait_ge(ready, j + 1)
                if n >= 2:
                    act.wait_ge(ss_done, n - 1)
                act.activation(bank[n % 2][:, 0:D], qh[:, j, :], ACT.Square).then_inc(sq_ps, 1)

            for j in range(NT):
                squares(j, j, centred)
            act.wait_ge(var_ready, 1)
            act.activation(ss, ss, ACT.Sqrt).then_inc(rstd_ready, 1)
            for j in range(NT):
                squares(j, NT + j, gated)
            act.wait_ge(var_ready, 2)
            act.activation(ss, ss, ACT.Sqrt).then_inc(rstd_ready, 1)
            act.wait_ge(load, 96)
            for j in range(NT):
                act.wait_ge(ot_ps, j + 1)
                for f in range(DH):
                    act.activation(turned[:, j, f * P:(f + 1) * P], bank[2 + j % 2][:, f * P:(f + 1) * P], ACT.Copy,
                                   scale=V["norm"][:, f:f + 1]).then_inc(ot_ready, 1)

        @block.gpsimd
        def _(pool):
            pool.wait_ge(load, 96)
            for j in range(NT):
                pool.wait_ge(scaled, j + 1)
                pool.tensor_tensor(qh[:, j, :], qh[:, j, :], V["w_row"], ALU.mult).then_inc(w_step, 1)
                pool.wait_ge(w_step, j + 1)
                pool.tensor_tensor(qh[:, j, :], qh[:, j, :], V["b_row"], ALU.add).then_inc(wb_done, 1)

        @block.vector
        def _(dve):
            n = [0]

            def then(ins):
                n[0] += 1
                ins.then_inc(step, 1)
                dve.wait_ge(step, n[0])

            hd = lambda t: t.rearrange(IN_HEADS, e=DK)
            per = lambda t, j: t[:, j * H:(j + 1) * H].unsqueeze(2).broadcast_to([P, H, DK])
            dve.wait_ge(qh_in, 16)

            def summed(j, n):
                dve.wait_ge(sq_ps, n + 1)
                dve.tensor_reduce(ss[:, j * H:(j + 1) * H], hd(bank[n % 2][:, 0:D]), AX_X, ALU.add).then_inc(ss_done, 1)

            def inverse(n):
                dve.wait_ge(ss_done, NT * n)
                then(dve.tensor_scalar(ss, ss, 1.0 / DK, EPS, ALU.mult, ALU.add))
                dve.reciprocal(ss, ss).then_inc(var_ready, 1)
                dve.wait_ge(rstd_ready, n)

            then(dve.tensor_reduce(mean, qh.rearrange("p j n -> p (j n)").rearrange(IN_HEADS, e=DK), AX_X, ALU.add))
            for j in range(NT):
                dve.scalar_tensor_tensor(out=hd(qh[:, j, :]), in0=per(mean, j), scalar=-1.0 / DK, in1=hd(qh[:, j, :]),
                                         op0=ALU.mult, op1=ALU.add).then_inc(centred, 1)
                if j:
                    summed(j - 1, j - 1)
            summed(NT - 1, NT - 1)
            inverse(1)
            for j in range(NT):
                dve.tensor_tensor(hd(qh[:, j, :]), hd(qh[:, j, :]), per(ss, j), ALU.mult).then_inc(scaled, 1)
            dve.wait_ge(load, 96)
            for j in range(NT):
                dve.wait_ge(wb_done, j + 1)
                then(dve.tensor_tensor(qh[:, j, :], qh[:, j, :], q[:, j, :], ALU.add))
                dve.tensor_tensor(qh[:, j, :], qh[:, j, :], gate[:, j, :], ALU.mult).then_inc(gated, 1)
                if j:
                    summed(j - 1, NT + j - 1)
            summed(NT - 1, 2 * NT - 1)
            inverse(2)
            for j in range(NT):
                dve.tensor_tensor(hd(qh[:, j, :]), hd(qh[:, j, :]), per(ss, j), ALU.mult).then_inc(unit, 1)
            dve.wait_ge(x1_in, 16)
            for j in range(NT):
                dve.wait_ge(y_ps, j + 1)
                dve.tensor_tensor(x1[:, j, :], x1[:, j, :], bank[4 + j % 2][:, 0:D], ALU.add).then_inc(y_done, 1)

        @block.tensor
        def _(pe):
            def turn(j):
                pe.wait_ge(unit, j + 1)
                if j >= 2:
                    pe.wait_ge(ot_ready, 2 * (j - 1))
                for f in range(DH):
                    mm = pe.transpose(bank[2 + j % 2][:, f * P:(f + 1) * P], qh[:, j, f * P:(f + 1) * P], S["ident"][:])
                mm.then_inc(ot_ps, 1)

            turn(0)
            for j in range(NT):
                if j + 1 < NT:
                    turn(j + 1)
                pe.wait_ge(ot_ready, 2 * (j + 1))
                if j >= 2:
                    pe.wait_ge(y_done, j - 1)
                for f in range(DH):
                    mm = pe.matmul(bank[4 + j % 2][:, 0:D], turned[:, j, f * P:(f + 1) * P], w_o[:, f, :],
                                   start=(f == 0), stop=(f == DH - 1))
                mm.then_inc(y_ps, 1)


def kernel(**inputs):
    import numpy as np
    import concourse.bacc as bacc
    from concourse.bass_utils import run_bass_kernel_spmd

    a = {k: np.asarray(v) for k, v in inputs.items()}
    rows = lambda w: np.ascontiguousarray(w.reshape(DH, P, -1).transpose(1, 0, 2))
    att = lambda n: a["L0_attn_" + n]
    ffn = lambda n: a["L0_ffn_" + n]
    gu = np.concatenate([np.concatenate([ffn("gate_w"), ffn("shared_gate_w")[None]]),
                         np.concatenate([ffn("up_w"), ffn("shared_up_w")[None]])], axis=1)
    down = np.concatenate([ffn("down_w"), ffn("shared_down_w")[None]]).transpose(2, 0, 1)
    arrays = {
        "x": att("x").reshape(T, D),
        "w_gu": gu.reshape(E + 1, 2 * I, DH, P).transpose(3, 0, 2, 1).reshape(P, E + 1, DH * 2 * I),
        "w_d1": down[0:P], "w_d2": down[P:],
        "rt": rows(ffn("router_w").T).reshape(P, DH * E), "rb": ffn("router_b")[None],
        "w_kv": rows(np.concatenate([att("Wk"), att("Wv")], axis=1)),
        "w_q": rows(np.concatenate([att("Wq"), att("Wbeta"), att("Wg1")], axis=1)),
        "w_g2": att("Wg2"), "w_o": rows(att("Wo")), "norm_w": att("norm_w").reshape(DH, P).T,
        "ln_w": att("ln_w"), "ln_w_row": att("ln_w").reshape(1, D), "ln_b_row": att("ln_b").reshape(1, D),
    }
    arrays = {k: np.ascontiguousarray(v) for k, v in arrays.items()}
    nc = bacc.Bacc("TRN2", target_bir_lowering=False, num_devices=1)
    d = {k: nc.dram_tensor(k + "_in", v.shape, F32, kind="ExternalInput").ap() for k, v in arrays.items()}
    d["out"] = nc.dram_tensor("out", (T, D), F32, kind="ExternalOutput").ap()
    build(nc, d)
    r = run_bass_kernel_spmd(nc, [{k + "_in": v for k, v in arrays.items()}], core_ids=[0])
    return r.results[0]["out"].reshape(1, T, D)
```

```python
from contextlib import ExitStack

import concourse.bass as bass
from concourse import mybir

ALU = mybir.AluOpType
ACT = mybir.ActivationFunctionType
F32 = mybir.dt.float32
I32 = mybir.dt.int32
U32 = mybir.dt.uint32
AX_X = mybir.AxisListType.X

P = 128
T, D = 1024, 256
NT = T // P
DH = D // P
E, I, K = 32, 192, 4
IR = I - P
H, DK, C = 16, 16, 16
HH = H // 2
NC = T // C
CT = P // C
ROUTED = (T * K + E * (P - 1)) // P
TILES = NT + ROUTED
SKIP = 100000
LN_EPS, EPS = 1e-5, 1e-6
SCALE = 1.8
ROWS = (K + 1) * T


def build(nc, d):
    with ExitStack() as ctx:
        def sb(name, shape, dt=F32):
            return ctx.enter_context(nc.sbuf_tensor(name, shape, dt))

        def sem(name):
            return ctx.enter_context(nc.semaphore(name))

        def dram(name, shape):
            return nc.dram_tensor(name, shape, F32, kind="Internal").ap()

        def named(name):
            if name not in sems:
                sems[name] = sem(name)
            return sems[name]

        sems = {}

        w_gu = sb("w_gu", [P, E + 1, DH * 2 * I])
        w_d1 = sb("w_d1", [P, E + 1, D])
        w_d2 = sb("w_d2", [P, E + 1, D])
        aux = w_d2[IR:P, :, :].rearrange("p e n -> p (e n)")
        ident = sb("ident", [P, P])
        same_head = sb("same_head", [P, P])
        own_head = sb("own_head", [P, 2 * C])
        causal = sb("causal", [P, 2 * C])
        earlier = sb("earlier", [P, P])
        ones = sb("ones", [P, P])
        count = sb("count", [P, P])
        pair_row = sb("pair_row", [P, NT, K])
        take = sb("take", [P, TILES], I32)
        put = sb("put", [P, TILES], I32)
        tile_expert = sb("tile_expert", [1, TILES], I32)
        mix = sb("mix", [P, NT, K])
        rt = sb("rt", [P, DH * E])
        rb = sb("rb", [1, E])
        work = sb("work", [P, 9500])
        bank = [ctx.enter_context(nc.psum_tensor(f"bank{n}", [P, 512], F32)) for n in range(8)]

        S = dict(w_gu=w_gu, aux=aux, w_d1=w_d1, w_d2=w_d2, ident=ident, same_head=same_head, own_head=own_head, causal=causal,
                 earlier=earlier, ones=ones, count=count, pair_row=pair_row, take=take, put=put,
                 tile_expert=tile_expert, mix=mix, rt=rt, rb=rb, work=work, bank=bank,
                 weights_in=sem("weights_in"), sem=named)
        S["xln_d"] = dram("xln_d", [T, D])
        S["res_d"] = dram("res_d", [ROWS, D])
        x1_d, x2_d = dram("x1_d", [T, D]), dram("x2_d", [T, D])
        S["q_d"], S["gate_d"] = dram("q_d", [T, D]), dram("gate_d", [T, D])
        S["r_d"], S["qh_d"] = dram("r_d", [T, D]), dram("qh_d", [T, D])

        constants(nc, S, d, sem)
        route(nc, S, "a", d["x"])
        expert_tiles(nc, S, "a")
        combine(nc, S, "a", x1_d)
        clear(nc, [sems[name] for name in sems if name.startswith("ffn_")])
        attention_inputs(nc, S, d)
        scan(nc, S, d)
        attention_output(nc, S, d, x1_d, x2_d)
        route(nc, S, "b", x2_d)
        expert_tiles(nc, S, "b")
        combine(nc, S, "b", d["out"])


def clear(nc, semaphores):
    with nc.Block() as block:
        @block.sync
        def _(sp):
            for s in semaphores:
                sp.sem_clear(s)


def carve(work, sizes):
    out, at = {}, 0
    for name, shape in sizes:
        n = 1
        for s in shape:
            n *= s
        v = work[:, at:at + n]
        if len(shape) == 2:
            v = v.rearrange("p (a b) -> p a b", a=shape[0])
        elif len(shape) == 3:
            v = v.rearrange("p (a b c) -> p a b c", a=shape[0], b=shape[1])
        out[name] = v
        at += n
    assert at <= work.shape[1], at
    return out


def by_tile(ap):
    return ap.rearrange("(j p) n -> p j n", p=P)


def constants(nc, S, d, sem):
    made, read = sem("made"), sem("c_read")
    with nc.Block() as block:
        @block.sync
        def _(sp):
            sp.dma_start(S["rt"][:], d["rt"]).then_inc(read, 16)
            sp.dma_start(S["rb"][:], d["rb"]).then_inc(read, 16)
            sp.wait_ge(read, 32)

        @block.gpsimd
        def _(pool):
            ident, same, earlier = S["ident"], S["same_head"], S["earlier"]
            causal = S["work"][:, NT * D:NT * D + P]
            heads = lambda t: t[:].rearrange("p (h c) -> p h c", c=C)
            heads3 = lambda t: t.rearrange("p (h c) -> p h c", c=C)
            pool.memset(S["ones"][:], 1.0).then_inc(made, 1)
            pool.iota(S["count"][:], [[1, P]], base=0, channel_multiplier=0,
                      allow_small_or_imprecise_dtypes=True)
            pool.iota(S["pair_row"][:], [[P, NT], [T, K]], base=1, channel_multiplier=1,
                      allow_small_or_imprecise_dtypes=True)
            pool.iota(S["take"][:, 0:NT], [[P, NT]], base=0, channel_multiplier=1)
            pool.iota(S["put"][:, 0:NT], [[P, NT]], base=K * T, channel_multiplier=1)
            pool.iota(S["tile_expert"][:, 0:NT], [[0, NT]], base=E, channel_multiplier=0).then_inc(made, 1)
            pool.wait_ge(made, 2)
            pool.affine_select(out=ident[:], in_=S["ones"][:], pattern=[[-1, P]], compare_op=ALU.is_equal,
                               fill=0.0, base=0, channel_multiplier=1).then_inc(made, 1)
            pool.affine_select(out=earlier[:], in_=S["ones"][:], pattern=[[1, P]], compare_op=ALU.is_ge,
                               fill=0.0, base=-1, channel_multiplier=-1).then_inc(made, 1)
            pool.affine_select(out=heads3(causal), in_=heads(S["ones"]), pattern=[[-C, HH], [0, C]],
                               compare_op=ALU.is_ge, fill=0.0, base=0, channel_multiplier=1).then_inc(made, 1)
            pool.wait_ge(made, 5)
            pool.affine_select(out=heads(same), in_=heads3(causal), pattern=[[C, HH], [0, C]],
                               compare_op=ALU.is_ge, fill=0.0, base=C - 1, channel_multiplier=-1).then_inc(made, 1)
            pool.wait_ge(made, 6)
            pool.affine_select(out=heads3(causal), in_=heads(same), pattern=[[C, HH], [1, C]],
                               compare_op=ALU.is_ge, fill=0.0, base=0, channel_multiplier=-1).then_inc(made, 1)

        @block.vector
        def _(dve):
            dve.wait_ge(made, 7)
            fold = lambda t: t.rearrange("p (b n) -> p n b", b=P // (2 * C))
            dve.tensor_reduce(S["own_head"][:], fold(S["same_head"][:]), AX_X, ALU.add)
            dve.tensor_reduce(S["causal"][:], fold(S["work"][:, NT * D:NT * D + P]), AX_X, ALU.add)

        @block.scalar
        def _(act):
            act.dma_start(ffn_views(S)["x"], by_tile(d["x"])).then_inc(S["sem"]("ffn_x_in"), 16)
            step = 11
            for e in range(0, E + 1, step):
                act.dma_start(S["w_gu"][:, e:e + step, :], d["w_gu"][:, e:e + step, :]).then_inc(S["weights_in"], 16)
                act.dma_start(S["w_d1"][:, e:e + step, :], d["w_d1"][:, e:e + step, :]).then_inc(S["weights_in"], 16)
                act.dma_start(S["w_d2"][0:IR, e:e + step, :], d["w_d2"][:, e:e + step, :]).then_inc(S["weights_in"], 16)


WEIGHT_LOADS = 9


def ffn_views(S):
    return carve(S["work"], [
        ("x", (NT, D)), ("xn", (2, D)), ("xt", (2, D)), ("logits", (NT, E)), ("top", (NT, 8)),
        ("top_i", (NT, 8)), ("expert", (NT, 8)), ("chosen", (NT * K, E)), ("members", (NT, E)),
        ("before", (NT, E)), ("slot_of", (NT, E)), ("picked", (NT * K, E)), ("slot", (NT * K,)),
        ("slot_tile", (NT * K,)), ("slot_pos", (NT * K,)), ("is_pos", (2, K * P)), ("is_tile", (2, K * ROUTED)),
        ("small", (600,))])


def layer_stats(nc, dve, act_sem, V, x, loaded, tag, sem):
    done = sem(f"{tag}_stat")
    st, mean, var = V["stats"], V["mean"], V["var"]
    if loaded:
        dve.wait_ge(loaded, 16)
    with dve.Fori(0, NT) as j:
        dve.bn_stats(st[:, bass.ds(j, 1), :], x[:, bass.ds(j, 1), :]).then_inc(done, 1)
    dve.wait_ge(done, NT)
    dve.tensor_tensor(V["t1"], st[:, :, 1], st[:, :, 4], ALU.subtract).then_inc(done, 1)
    dve.tensor_tensor(V["t2"], st[:, :, 1], st[:, :, 4], ALU.add).then_inc(done, 1)
    dve.tensor_tensor(V["t3"], st[:, :, 2], st[:, :, 5], ALU.add).then_inc(done, 1)
    dve.wait_ge(done, NT + 3)
    dve.scalar_tensor_tensor(out=V["t4"], in0=V["t1"], scalar=0.25, in1=V["t1"], op0=ALU.mult,
                             op1=ALU.mult).then_inc(done, 1)
    dve.tensor_scalar(mean, V["t2"], 0.5, None, ALU.mult).then_inc(done, 1)
    dve.tensor_scalar(V["t5"], V["t3"], 1.0 / D, LN_EPS, ALU.mult, ALU.add).then_inc(done, 1)
    dve.wait_ge(done, NT + 6)
    dve.tensor_tensor(var, V["t5"], V["t4"], ALU.add).then_inc(done, 1)
    dve.wait_ge(done, NT + 7)
    dve.reciprocal(V["t6"], var).then_inc(act_sem, 1)


def stat_views(at):
    V = {"stats": at[:, 0:48].rearrange("p (j s) -> p j s", s=6)}
    for n, name in enumerate(("mean", "rstd", "var", "t1", "t2", "t3", "t4", "t5", "t6")):
        V[name] = at[:, 48 + 8 * n:56 + 8 * n]
    return V


def route(nc, S, tag, x_d):
    V = ffn_views(S)
    small = V["small"]
    st = stat_views(small[:, 0:120])
    shifted = small[:, 120:152].rearrange("p (j k) -> p j k", k=K)
    exps = small[:, 152:184].rearrange("p (j k) -> p j k", k=K)
    total = small[:, 184:192]
    per = small[:, 192:200]
    members_all = small[:, 200:232]
    counted = small[:, 232:264].bitcast(I32)
    tiles_of = small[:, 264:296].bitcast(I32)
    tiles_end = small[:, 296:328]
    first_slot = small[:, 328:360]
    slot_int = small[:, 360:392].bitcast(I32)
    tile_int = small[:, 392:424].bitcast(I32)
    pos_int = small[:, 424:456].bitcast(I32)
    row_f = small[:, 456:456 + ROUTED]
    empty = small[:, 520:520 + ROUTED]
    x, xn, xt = V["x"], V["xn"], V["xt"]
    logits, top, expert = V["logits"], V["top"], V["expert"]
    top_i = V["top_i"].bitcast(U32)
    chosen = V["chosen"].rearrange("p (j k) e -> p j k e", k=K)
    picked = V["picked"].rearrange("p (j k) e -> p j k e", k=K)
    is_pos = V["is_pos"].rearrange("p u (k q) -> p u k q", k=K)
    is_tile = V["is_tile"].rearrange("p u (k q) -> p u k q", k=K)
    bank = S["bank"]
    ps_t, ps_l = bank[0:2], bank[2:4]
    ps_cum, ps_all, ps_pair = bank[4], bank[5], bank[6]
    rt = S["rt"][:].rearrange("p (f e) -> p f e", f=DH)

    g = lambda n: S["sem"](f"ffn_{n}")
    x_in, var_ready, rstd_ready = g("x_in"), g("var_ready"), g("rstd_ready")
    xn_ready, xn_out = g("xn_ready"), [g("xn_out0"), g("xn_out1")]
    xt_ps, xt_ready, logit_ps, logit_ready = g("xt_ps"), g("xt_ready"), g("logit_ps"), g("logit_ready")
    shifted_ready, exp_ready = g("shifted_ready"), g("exp_ready")
    members_ready, cum_ps = g("members_ready"), g("cum_ps")
    onehot_ready, pair_ps = g("onehot_ready"), g("pair_ps")
    step = g("route_step")

    with nc.Block() as block:
        @block.sync
        def _(sp):
            if tag == "b":
                sp.dma_start(x[:], by_tile(x_d)).then_inc(x_in, 16)
            out = S["xln_d"].rearrange("(j p) n -> j p n", p=P)
            for j in range(NT):
                sp.wait_ge(xn_ready, j + 1)
                sp.dma_start(out[j], xn[:, j % 2, :]).then_inc(xn_out[j % 2], 16)
            for u in range(2):
                sp.wait_ge(xn_out[u], 16 * NT // 2)

        @block.vector
        def _(dve):
            n = [0]

            def then(ins):
                n[0] += 1
                ins.then_inc(step, 1)
                dve.wait_ge(step, n[0])

            layer_stats(nc, dve, var_ready, st, x, x_in, "ffn", S["sem"])
            dve.wait_ge(rstd_ready, 1)
            for j in range(NT):
                if j >= 2:
                    dve.wait_ge(xn_out[j % 2], 16 * (j // 2))
                    dve.wait_ge(xt_ps, j - 1)
                dve.tensor_scalar(xn[:, j % 2, :], x[:, j, :], st["mean"][:, j:j + 1], st["rstd"][:, j:j + 1],
                                  ALU.subtract, ALU.mult).then_inc(xn_ready, 1)
            dve.wait_ge(logit_ready, NT)
            for j in range(NT):
                dve.max(top[:, j, :], logits[:, j, :]).then_inc(step, 1)
            n[0] = NT
            dve.wait_ge(step, NT)
            dve.tensor_tensor(shifted, top[:, :, 0:K], top[:, :, 0:1].broadcast_to([P, NT, K]),
                              ALU.subtract).then_inc(shifted_ready, 1)
            for j in range(NT):
                dve.max_index(top_i[:, j, :], top[:, j, :], logits[:, j, :]).then_inc(step, 1)
            n[0] += NT
            dve.wait_ge(step, n[0])
            then(dve.tensor_copy(expert[:], top_i[:]))
            then(dve.tensor_tensor(
                chosen, S["count"][:, 0:E].unsqueeze(1).unsqueeze(1).broadcast_to([P, NT, K, E]),
                expert[:, :, 0:K].unsqueeze(3).broadcast_to([P, NT, K, E]), ALU.is_equal))
            then(dve.tensor_reduce(V["members"], chosen.rearrange("p j k e -> p j e k"), AX_X, ALU.add))
            then(dve.memset(V["before"][:, 0, :], 0.0))
            for j in range(1, NT):
                then(dve.tensor_tensor(V["before"][:, j, :], V["before"][:, j - 1, :], V["members"][:, j - 1, :],
                                       ALU.add))
            dve.tensor_tensor(members_all, V["before"][:, NT - 1, :], V["members"][:, NT - 1, :],
                              ALU.add).then_inc(members_ready, 1)
            dve.wait_ge(exp_ready, 1)
            then(dve.tensor_reduce(total, exps, AX_X, ALU.add))
            then(dve.reciprocal(per, total))
            then(dve.scalar_tensor_tensor(out=S["mix"][:], in0=exps, scalar=0.5 * SCALE,
                                          in1=per.unsqueeze(2).broadcast_to([P, NT, K]), op0=ALU.mult, op1=ALU.mult))
            dve.wait_ge(cum_ps, 1)
            then(dve.tensor_scalar(counted, bank[5][:, 0:E], float(P - 1), None, ALU.add))
            then(dve.tensor_scalar(tiles_of, counted, 7, None, ALU.logical_shift_right))
            then(dve.tensor_copy(row_f[:, 0:E], tiles_of))
            then(dve.tensor_tensor_scan(tiles_end, S["ones"][:, 0:E], row_f[:, 0:E], 0.0, ALU.mult, ALU.add))
            then(dve.tensor_tensor(first_slot, tiles_end, row_f[:, 0:E], ALU.subtract))
            then(dve.scalar_tensor_tensor(out=V["slot_of"], in0=first_slot.unsqueeze(1).broadcast_to([P, NT, E]),
                                          scalar=float(P), in1=ps_cum[:, 0:NT * E].rearrange("p (j e) -> p j e", e=E),
                                          op0=ALU.mult, op1=ALU.add))
            then(dve.tensor_tensor(picked, chosen, V["slot_of"].unsqueeze(2).broadcast_to([P, NT, K, E]), ALU.mult))
            then(dve.tensor_reduce(V["slot"], V["picked"], AX_X, ALU.add))
            then(dve.tensor_copy(slot_int, V["slot"]))
            then(dve.tensor_scalar(tile_int, slot_int, 7, None, ALU.logical_shift_right))
            then(dve.tensor_scalar(pos_int, slot_int, P - 1, None, ALU.bitwise_and))
            then(dve.tensor_copy(V["slot_tile"], tile_int))
            then(dve.tensor_copy(V["slot_pos"], pos_int))
            half = (ROUTED + 1) // 2
            for a, b in ((0, half), (half, ROUTED)):
                w = (b - a) * E
                v = V["picked"].rearrange("p n e -> p (n e)")[0:1, 0:w].rearrange("p (i e) -> p i e", e=E)
                then(dve.tensor_tensor(v, tiles_end[0:1, :].unsqueeze(1).broadcast_to([1, b - a, E]),
                                       S["count"][0:1, a:b].unsqueeze(2).broadcast_to([1, b - a, E]), ALU.is_le))
                then(dve.tensor_reduce(row_f[0:1, a:b], v, AX_X, ALU.add))
            then(dve.tensor_scalar(S["tile_expert"][0:1, NT:TILES], row_f[0:1, :], float(E - 1), None, ALU.min))
            at = lambda v, j: v.rearrange("p (j k) -> p j k", k=K)[:, j, :]
            for j in range(NT):
                u = j % 2
                if j >= 2:
                    dve.wait_ge(pair_ps, j - 1)
                dve.tensor_tensor(is_pos[:, u], S["count"][:].unsqueeze(1).broadcast_to([P, K, P]),
                                  at(V["slot_pos"], j).unsqueeze(2).broadcast_to([P, K, P]),
                                  ALU.is_equal).then_inc(onehot_ready, 1)
                then(dve.tensor_tensor(is_tile[:, u], S["count"][:, 0:ROUTED].unsqueeze(1).broadcast_to([P, K, ROUTED]),
                                       at(V["slot_tile"], j).unsqueeze(2).broadcast_to([P, K, ROUTED]), ALU.is_equal))
                dve.tensor_tensor(is_tile[:, u], is_tile[:, u],
                                  S["pair_row"][:, j, :].unsqueeze(2).broadcast_to([P, K, ROUTED]),
                                  ALU.mult).then_inc(onehot_ready, 1)
            dve.wait_ge(pair_ps, NT)
            pair = ps_pair[:, 0:ROUTED]
            then(dve.tensor_scalar(row_f, pair, -1.0, None, ALU.add))
            then(dve.tensor_scalar(empty, pair, 0.0, float(SKIP), ALU.is_equal, ALU.mult))
            then(dve.tensor_tensor(S["put"][:, NT:TILES], row_f, empty, ALU.add))
            then(dve.tensor_scalar(S["take"][:, NT:TILES], row_f, 0.0, None, ALU.max))
            then(dve.tensor_scalar(S["take"][:, NT:TILES], S["take"][:, NT:TILES], T - 1, None, ALU.bitwise_and))

        @block.scalar
        def _(act):
            act.wait_ge(var_ready, 1)
            act.activation(st["rstd"], st["t6"], ACT.Sqrt).then_inc(rstd_ready, 1)
            for j in range(NT):
                act.wait_ge(xt_ps, j + 1)
                if j >= 2:
                    act.wait_ge(logit_ps, j - 1)
                act.copy(xt[:, j % 2, :], ps_t[j % 2][:, 0:D]).then_inc(xt_ready, 1)
                act.wait_ge(logit_ps, j + 1)
                act.copy(logits[:, j, :], ps_l[j % 2][:, 0:E]).then_inc(logit_ready, 1)
            act.wait_ge(shifted_ready, 1)
            act.activation(exps, shifted, ACT.Exp).then_inc(exp_ready, 1)

        @block.tensor
        def _(pe):
            for j in range(NT):
                u = j % 2
                pe.wait_ge(xn_ready, j + 1)
                if j >= 2:
                    pe.wait_ge(xt_ready, j - 1)
                for f in range(DH):
                    mm = pe.transpose(ps_t[u][:, f * P:(f + 1) * P], xn[:, u, f * P:(f + 1) * P], S["ident"][:])
                mm.then_inc(xt_ps, 1)
                pe.wait_ge(xt_ready, j + 1)
                if j >= 2:
                    pe.wait_ge(logit_ready, j - 1)
                for f in range(DH):
                    pe.matmul(ps_l[u][:, 0:E], xt[:, u, f * P:(f + 1) * P], rt[:, f, :], start=(f == 0), stop=False)
                pe.matmul(ps_l[u][:, 0:E], S["ones"][0:1, :], S["rb"][:], start=False, stop=True).then_inc(logit_ps, 1)
            pe.wait_ge(members_ready, 1)
            flat = lambda v: v.rearrange("p j e -> p (j e)")
            pe.matmul(ps_cum[:, 0:NT * E], S["earlier"][:], flat(V["members"]), start=True, stop=False)
            pe.matmul(ps_cum[:, 0:NT * E], S["ones"][:], flat(V["before"]), start=False, stop=True)
            pe.matmul(ps_all[:, 0:E], S["ones"][:], members_all, start=True, stop=True).then_inc(cum_ps, 1)
            for j in range(NT):
                u = j % 2
                pe.wait_ge(onehot_ready, 2 * (j + 1))
                for k in range(K):
                    mm = pe.matmul(ps_pair[:, 0:ROUTED], is_pos[:, u, k, :], is_tile[:, u, k, :],
                                   start=(j == 0 and k == 0), stop=(j == NT - 1 and k == K - 1))
                mm.then_inc(pair_ps, 1)


def expert_tiles(nc, S, tag):
    W = carve(S["work"][:, NT * D:], [
        ("xg", (4, D)), ("xt", (2, D)), ("gated", (2, I)), ("h", (2, I)), ("ht", (2, D)), ("y", (4, D)),
        ("take4", (4,)), ("put4", (4,))])
    xg, xt, gated, h, ht, y = (W[n] for n in ("xg", "xt", "gated", "h", "ht", "y"))
    take4, put4 = W["take4"].bitcast(I32), W["put4"].bitcast(I32)
    bank = S["bank"]
    ps_x, ps_gu, ps_h, ps_y = bank[0:2], bank[2:4], bank[4:6], bank[6:8]
    g = lambda n: S["sem"](f"ffn_{n}")
    x_in = [S["sem"](f"{tag}_xg_in{u}") for u in range(4)]
    y_out = [S["sem"](f"{tag}_y_out{u}") for u in range(4)]
    take_ready, put_ready = g("take_ready"), g("put_ready")
    x_ps, x_ready = g("x_ps"), g("x_ready")
    gu_ps, gated_ready, h_ready = g("gu_ps"), g("gated_ready"), g("h_ready")
    h_ps, ht_ready = g("h_ps"), g("ht_ready")
    y_ps, y_ready = g("y_ps"), g("y_ready")
    U, WARM, AHEAD, LAG = 4, 2, 5, 7
    ROUNDS = (TILES - AHEAD) // U

    def steps(eng, step, last):
        for s in range(WARM * U):
            step(s // U, s % U)
        with eng.Fori(WARM, ROUNDS) as n:
            for u in range(U):
                step(n, u)
        for s in range(ROUNDS * U, last):
            step(s // U, s % U)

    def back(n, u, by):
        return (n, u - by) if u >= by else (n - 1, u - by + U)

    def is_tile(n, u, ahead=0):
        return not isinstance(n, int) or 0 <= n * U + u + ahead < TILES

    def from_tile(n, u, first):
        return not isinstance(n, int) or n * U + u >= first

    with nc.Block() as block:
        @block.gpsimd
        def _(pool):
            last_row = pool.to_reg(ROWS - 1)

            def gather(u):
                pool.indirect_dma_start(xg[:, u, :], None, S["xln_d"],
                                        bass.IndirectOffsetOnAxis(ap=take4[:, u:u + 1], axis=0)).then_inc(x_in[u], 16)

            def scatter(u):
                pool.indirect_dma_start(S["res_d"], bass.IndirectOffsetOnAxis(ap=put4[:, u:u + 1], axis=0),
                                        y[:, u, :], None, bounds_check=last_row,
                                        oob_is_err=False).then_inc(y_out[u], 16)

            def step(n, u):
                s = n * U + u
                v = (u - LAG) % U
                if isinstance(n, int):
                    if is_tile(n, u):
                        pool.wait_ge(take_ready, s + 1)
                        gather(u)
                    if from_tile(n, u, LAG):
                        pool.wait_ge(put_ready, s - LAG + 1)
                        scatter(v)
                    return
                take_at, put_at = pool.to_reg(s + 1), pool.to_reg(s - (LAG - 1))
                pool.wait_ge(take_ready, 1)
                pool.wait_ge(take_ready, take_at)
                gather(u)
                pool.wait_ge(put_ready, 1)
                pool.wait_ge(put_ready, put_at)
                scatter(v)

            steps(pool, step, TILES + LAG)
            for u in range(4):
                pool.wait_ge(y_out[u], 16 * len(range(u, TILES, 4)))

        @block.vector
        def _(dve):
            def take_numbers(s, u):
                dve.tensor_copy(take4[:, u:u + 1], S["take"][:, bass.ds(s, 1)]).then_inc(take_ready, 1)

            for s in range(4):
                take_numbers(s, s)
            dve.wait_ge(x_ps, 1)
            take_numbers(4, 0)

            def step(n, u):
                s = n * U + u
                if is_tile(n, u):
                    dve.wait_ge(gated_ready, s + 1)
                    if from_tile(n, u, 2):
                        dve.wait_ge(h_ps, s - 1)
                    dve.tensor_tensor(h[:, u % 2, :], gated[:, u % 2, :], ps_gu[u % 2][:, I:2 * I],
                                      ALU.mult).then_inc(h_ready, 1)
                    if is_tile(n, u, AHEAD):
                        dve.wait_ge(x_ps, s + 2)
                        take_numbers(s + AHEAD, (u + 1) % U)
                if from_tile(n, u, 2):
                    m, v = back(n, u, 2)
                    dve.wait_ge(y_ps, s - 1)
                    if from_tile(n, u, 6):
                        dve.wait_ge(y_out[v], m * 16)
                    dve.tensor_copy(y[:, v, :], ps_y[u % 2][:, 0:D]).then_inc(y_ready, 1)
                    dve.wait_ge(y_ready, s - 1)
                    dve.tensor_copy(put4[:, v:v + 1], S["put"][:, bass.ds(s - 2, 1)]).then_inc(put_ready, 1)

            steps(dve, step, TILES + 2)

        @block.scalar
        def _(act):
            def x_copy(s, n, u):
                act.wait_ge(x_ps, s + 1)
                if from_tile(n, u, 2):
                    act.wait_ge(gu_ps, s - 1)
                act.copy(xt[:, u % 2, :], ps_x[u % 2][:, 0:D]).then_inc(x_ready, 1)

            def step(n, u):
                s = n * U + u
                if is_tile(n, u):
                    act.wait_ge(gu_ps, s + 1)
                    if from_tile(n, u, 2):
                        act.wait_ge(h_ready, s - 1)
                    act.activation(gated[:, u % 2, :], ps_gu[u % 2][:, 0:I], ACT.Silu).then_inc(gated_ready, 1)
                if is_tile(n, u, 1):
                    x_copy(s + 1, n, u + 1)
                if is_tile(n, u, -1):
                    v = (u + 1) % 2
                    act.wait_ge(h_ps, s)
                    if from_tile(n, u, 3):
                        act.wait_ge(y_ps, s - 2)
                    act.copy(ht[:, v, 0:P], ps_h[v][:, 0:P]).then_inc(ht_ready, 1)
                    act.copy(ht[0:IR, v, P:D], ps_h[v][0:IR, P:D]).then_inc(ht_ready, 1)

            x_copy(0, 0, 0)
            steps(act, step, TILES + 1)

        @block.tensor
        def _(pe):
            def turn_x(s, n, u):
                pe.wait_ge(x_in[u], n * 16 + 16)
                if from_tile(n, u, 2):
                    pe.wait_ge(x_ready, s - 1)
                for f in range(DH):
                    mm = pe.transpose(ps_x[u % 2][:, f * P:(f + 1) * P], xg[:, u, f * P:(f + 1) * P], S["ident"][:])
                mm.then_inc(x_ps, 1)

            def gate_up(s, n, u, e):
                pe.wait_ge(x_ready, s + 1)
                if from_tile(n, u, 2):
                    pe.wait_ge(h_ready, s - 1)
                for f in range(DH):
                    mm = pe.matmul(ps_gu[u % 2][:, 0:2 * I], xt[:, u % 2, f * P:(f + 1) * P],
                                   S["w_gu"][:, bass.ds(e, 1), f * 2 * I:(f + 1) * 2 * I],
                                   start=(f == 0), stop=(f == DH - 1))
                mm.then_inc(gu_ps, 1)

            def turn_h(s, n, u):
                pe.wait_ge(h_ready, s + 1)
                if from_tile(n, u, 2):
                    pe.wait_ge(ht_ready, s * 2 - 2)
                pe.transpose(ps_h[u % 2][:, 0:P], h[:, u % 2, 0:P], S["ident"][:])
                pe.transpose(ps_h[u % 2][0:IR, P:D], h[:, u % 2, P:I], S["ident"][:]).then_inc(h_ps, 1)

            def down(s, n, u, e):
                pe.wait_ge(ht_ready, s * 2 + 2)
                if from_tile(n, u, 2):
                    pe.wait_ge(y_ready, s - 1)
                pe.matmul(ps_y[u % 2][:, 0:D], ht[:, u % 2, 0:P], S["w_d1"][:, bass.ds(e, 1), :],
                          start=True, stop=False)
                pe.matmul(ps_y[u % 2][:, 0:D], ht[0:IR, u % 2, P:D], S["w_d2"][0:IR, bass.ds(e, 1), :],
                          start=False, stop=True).then_inc(y_ps, 1)

            def expert_of(s):
                return pe.value_load(S["tile_expert"][0:1, bass.ds(s, 1)], min_val=0, max_val=E)

            def step(n, u):
                s = n * U + u
                if is_tile(n, u):
                    gate_up(s, n, u, expert_of(s))
                if is_tile(n, u, 1):
                    turn_x(s + 1, *((n, u + 1) if u + 1 < U else (n + 1, 0)))
                if is_tile(n, u, -1):
                    turn_h(s - 1, *back(n, u, 1))
                if is_tile(n, u, -2):
                    down(s - 2, *back(n, u, 2), expert_of(s - 2))

            if tag == "a":
                pe.wait_ge(S["weights_in"], 16 * WEIGHT_LOADS)
            turn_x(0, 0, 0)
            steps(pe, step, TILES + 2)


def combine(nc, S, tag, out_d):
    V = ffn_views(S)
    x = V["x"]
    rows = S["work"][:, NT * D:NT * D + 2 * (K + 1) * D].rearrange("p (u k n) -> p u k n", u=2, k=K + 1)
    res = S["res_d"].rearrange("(k j p) n -> j p k n", p=P, j=NT)
    out = out_d.rearrange("(j p) n -> j p n", p=P)
    rows_in = [S["sem"](f"ffn_rows_in{u}") for u in range(2)]
    added, stored = S["sem"](f"ffn_added"), S["sem"](f"ffn_stored")

    with nc.Block() as block:
        @block.sync
        def _(sp):
            for j in range(NT):
                if j >= 2:
                    sp.wait_ge(added, (K + 1) * (j - 1))
                sp.dma_start(rows[:, j % 2, :, :], res[j]).then_inc(rows_in[j % 2], 16)

        @block.scalar
        def _(act):
            for j in range(NT):
                act.wait_ge(added, (K + 1) * (j + 1))
                act.dma_start(out[j], x[:, j, :]).then_inc(stored, 16)
            act.wait_ge(stored, 16 * NT)

        @block.vector
        def _(dve):
            for j in range(NT):
                dve.wait_ge(rows_in[j % 2], 16 * (j // 2 + 1))
                for k in range(K + 1):
                    if k:
                        dve.wait_ge(added, (K + 1) * j + k)
                    dve.scalar_tensor_tensor(out=x[:, j, :], in0=rows[:, j % 2, k, :],
                                             scalar=S["mix"][:, j, k:k + 1] if k < K else 0.5, in1=x[:, j, :],
                                             op0=ALU.mult, op1=ALU.add).then_inc(added, 1)


ATT = [("kt", (NC, 2 * C)), ("qt", (NC, 2 * C)), ("r", (NC, 2 * DK)), ("eta", (NC, 2))]
IN_HEADS = "p (h e) -> p h e"


def attention_inputs(nc, S, d):
    V = carve(S["work"], ATT + [
        ("w_kv", (DH, 2 * D)), ("w_q", (DH, D + 2 * H)), ("stat", (120,)), ("xn", (D,)), ("xt", (D,)),
        ("eta_n", (NT * H,)), ("ss", (NT * H,)), ("q", (D + H,)), ("gate", (D,)), ("mean_r", (2, H))])
    R2 = carve(S["work"][:, 6272:], [("kn", (2, D)), ("z", (2, D)), ("w_row", (D,)), ("b_row", (D,)), ("tmp", (2 * D,))])
    rows_of = S["work"][:, 6272:6272 + CT * P]
    kt, qt, xn, xt, q, gate = (V[n] for n in ("kt", "qt", "xn", "xt", "q", "gate"))
    w_kv, w_q, ss, eta_n = V["w_kv"], V["w_q"], V["ss"], V["eta_n"]
    w_g2, g1 = S["aux"][0:H, 0:D], S["aux"][0:H, D:D + P]
    tiles = lambda v: v.rearrange("p i n -> p (i n)").rearrange("p (j n) -> p j n", j=NT)
    x, v_nat = tiles(kt), tiles(V["r"])
    by_chunk = lambda t, j: t[:, j * CT:(j + 1) * CT, :].rearrange("p r (f c) -> p f r c", f=2)
    st = stat_views(V["stat"])
    bank = S["bank"]
    ps_t, ps_kv, ps_q, ps_g1, ps_gate, ps_sq = bank[0], bank[1], bank[2], bank[3], bank[4], bank[5]
    ps_qt = bank[6]
    g = lambda n: S["sem"](f"att_{n}")
    w_in, x_in, var_ready, rstd_ready = g("w_in"), g("x_in"), g("var_ready"), g("rstd_ready")
    xn_ready, xt_ps, xt_ready = g("xn_ready"), g("xt_ps"), g("xt_ready")
    g1_ps, g1_ready, q_ps, sig_ready, q_ready = g("g1_ps"), g("g1_ready"), g("q_ps"), g("sig_ready"), g("q_ready")
    kv_ps, kv_read, gate_ps, gate_ready = g("kv_ps"), g("kv_read"), g("gate_ps"), g("gate_ready")
    qt_ps, qt_ready, v_ready = g("qt_ps"), g("qt_ready"), g("v_ready")
    q_out, gate_out = g("q_out"), g("gate_out")

    with nc.Block() as block:
        @block.sync
        def _(sp):
            sp.dma_start(w_kv[:], d["w_kv"]).then_inc(w_in, 16)
            sp.dma_start(w_q[:], d["w_q"]).then_inc(w_in, 16)
            sp.dma_start(w_g2, d["w_g2"]).then_inc(w_in, 16)
            sp.wait_ge(w_in, 48)
            q_rows = S["q_d"].rearrange("(j p) n -> j p n", p=P)
            gate_rows = S["gate_d"].rearrange("(j p) n -> j p n", p=P)
            for j in range(NT):
                sp.wait_ge(q_ready, 2 * (j + 1))
                sp.dma_start(q_rows[j], q[:, 0:D]).then_inc(q_out, 16)
                sp.wait_ge(gate_ready, j + 1)
                sp.dma_start(gate_rows[j], gate[:]).then_inc(gate_out, 16)
            sp.wait_ge(q_out, 16 * NT)
            sp.wait_ge(gate_out, 16 * NT)

        @block.vector
        def _(dve):
            layer_stats(nc, dve, var_ready, st, x, None, "att", S["sem"])
            dve.wait_ge(rstd_ready, 1)
            for j in range(NT):
                if j:
                    dve.wait_ge(xt_ps, j)
                dve.tensor_scalar(xn, x[:, j, :], st["mean"][:, j:j + 1], st["rstd"][:, j:j + 1],
                                  ALU.subtract, ALU.mult).then_inc(xn_ready, 1)
                dve.wait_ge(sig_ready, j + 1)
                dve.tensor_tensor(q[:, 0:D], q[:, 0:D], ps_q[:, 0:D], ALU.mult).then_inc(q_ready, 1)
                dve.tensor_scalar(eta_n[:, j * H:(j + 1) * H], q[:, D:D + H], 2.0, None, ALU.mult).then_inc(q_ready, 1)
                dve.wait_ge(kv_read, j + 1)
                dve.tensor_reduce(ss[:, j * H:(j + 1) * H], ps_sq[:, 0:D].rearrange(IN_HEADS, e=DK), AX_X,
                                  ALU.add).then_inc(v_ready, 1)
                dve.tensor_copy(v_nat[:, j, :], ps_kv[:, D:2 * D]).then_inc(v_ready, 1)

        @block.scalar
        def _(act):
            act.wait_ge(var_ready, 1)
            act.activation(st["rstd"], st["t6"], ACT.Sqrt).then_inc(rstd_ready, 1)
            for j in range(NT):
                act.wait_ge(xt_ps, j + 1)
                if j:
                    act.wait_ge(kv_ps, j)
                act.copy(xt, ps_t[:, 0:D]).then_inc(xt_ready, 1)
                act.wait_ge(g1_ps, j + 1)
                if j:
                    act.wait_ge(gate_ps, j)
                act.copy(g1, ps_g1[IR:IR + H, 0:P]).then_inc(g1_ready, 1)
                act.wait_ge(q_ps, j + 1)
                if j:
                    act.wait_ge(q_out, 16 * j)
                    act.wait_ge(qt_ps, j)
                    act.wait_ge(q_ready, 2 * j)
                act.activation(q[:, 0:D + H], ps_q[:, 0:D + H], ACT.Sigmoid).then_inc(sig_ready, 1)
                act.wait_ge(kv_ps, j + 1)
                if j:
                    act.wait_ge(v_ready, 2 * j)
                act.copy(x[:, j, :], ps_kv[:, 0:D])
                act.activation(ps_sq[:, 0:D], ps_kv[:, 0:D], ACT.Square).then_inc(kv_read, 1)
                act.wait_ge(gate_ps, j + 1)
                if j:
                    act.wait_ge(gate_out, 16 * j)
                act.activation(gate[:], ps_gate[:, 0:D], ACT.Sigmoid).then_inc(gate_ready, 1)
                act.wait_ge(qt_ps, j + 1)
                act.copy(by_chunk(qt, j), ps_qt[:, 0:D].rearrange("p (f r c) -> p f r c", f=2, r=CT)).then_inc(qt_ready, 1)

        @block.tensor
        def _(pe):
            pe.wait_ge(w_in, 48)
            for j in range(NT):
                pe.wait_ge(xn_ready, j + 1)
                if j:
                    pe.wait_ge(xt_ready, j)
                for f in range(DH):
                    mm = pe.transpose(ps_t[:, f * P:(f + 1) * P], xn[:, f * P:(f + 1) * P], S["ident"][:])
                mm.then_inc(xt_ps, 1)
                pe.wait_ge(xt_ready, j + 1)
                if j:
                    pe.wait_ge(g1_ready, j)
                for f in range(DH):
                    mm = pe.matmul(ps_g1[IR:IR + H, 0:P], w_q[:, f, D + H:D + 2 * H], xt[:, f * P:(f + 1) * P],
                                   start=(f == 0), stop=(f == DH - 1))
                mm.then_inc(g1_ps, 1)
                if j:
                    pe.wait_ge(q_ready, 2 * j)
                for f in range(DH):
                    mm = pe.matmul(ps_q[:, 0:D + H], xt[:, f * P:(f + 1) * P], w_q[:, f, 0:D + H],
                                   start=(f == 0), stop=(f == DH - 1))
                mm.then_inc(q_ps, 1)
                if j:
                    pe.wait_ge(v_ready, 2 * j)
                for f in range(DH):
                    mm = pe.matmul(ps_kv[:, 0:2 * D], xt[:, f * P:(f + 1) * P], w_kv[:, f, :],
                                   start=(f == 0), stop=(f == DH - 1))
                mm.then_inc(kv_ps, 1)
                pe.wait_ge(g1_ready, j + 1)
                if j:
                    pe.wait_ge(gate_ready, j)
                pe.matmul(ps_gate[:, 0:D], g1, w_g2, start=True, stop=True).then_inc(gate_ps, 1)
                pe.wait_ge(q_ready, 2 * (j + 1))
                if j:
                    pe.wait_ge(qt_ready, j)
                for f in range(DH):
                    mm = pe.transpose(ps_qt[:, f * P:(f + 1) * P], q[:, f * P:(f + 1) * P], S["ident"][:])
                mm.then_inc(qt_ps, 1)

    kn, z, w_row, b_row = R2["kn"], R2["z"], R2["w_row"], R2["b_row"]
    rows_ready = g("rows_ready")
    row_in, ss_ready, norm_ready = g("row_in"), g("ss_ready"), g("norm_ready")
    kn_ready, kt_ps, kt_ready, z_ready, zw_ready = g("kn_ready"), g("kt_ps"), g("kt_ready"), g("z_ready"), g("zw_ready")
    r_ready, r_out, eta_ps, step, w_step = g("r_ready"), [g("r_out0"), g("r_out1")], g("eta_ps"), g("step"), g("w_step")
    ps_e = bank[2:4]
    with nc.Block() as block:
        @block.sync
        def _(sp):
            sp.dma_start(w_row, d["ln_w_row"].broadcast_to([P, D])).then_inc(row_in, 16)
            sp.dma_start(b_row, d["ln_b_row"].broadcast_to([P, D])).then_inc(row_in, 16)
            rows = S["r_d"].rearrange("(j p) n -> j p n", p=P)
            for j in range(NT):
                sp.wait_ge(r_ready, j + 1)
                sp.dma_start(rows[j], z[:, j % 2, :]).then_inc(r_out[j % 2], 16)
            for u in range(2):
                sp.wait_ge(r_out[u], 16 * NT // 2)

        @block.vector
        def _(dve):
            n = [0]

            def then(ins):
                n[0] += 1
                ins.then_inc(step, 1)
                dve.wait_ge(step, n[0])

            dve.tensor_copy(rows_of.rearrange("p (r h c) -> p r h c", h=HH, c=C),
                            S["ident"][:].rearrange("p (r c) -> p r c", c=C).unsqueeze(2).broadcast_to([P, CT, HH, C])
                            ).then_inc(rows_ready, 1)
            then(dve.tensor_scalar(ss, ss, EPS, None, ALU.add))
            dve.reciprocal(ss, ss).then_inc(ss_ready, 1)
            tmp = R2["tmp"].rearrange("p (n f h) -> p n f h", f=2, h=HH)
            dve.wait_ge(eta_ps, 1)
            own = S["same_head"][:].rearrange("p (h c) -> p h c", c=C)[:, :, 0]
            for b in range(2):
                then(dve.tensor_tensor(tmp, ps_e[b][:].rearrange("p (n f h) -> p n f h", f=2, h=HH),
                                       own.unsqueeze(1).unsqueeze(1).broadcast_to([P, 4 * NT, 2, HH]), ALU.mult))
                for r in range(4):
                    dst = V["eta"].rearrange("p (j r) f -> p r j f", r=CT)[:, 4 * b + r]
                    then(dve.tensor_reduce(dst, tmp[:, r * NT:(r + 1) * NT], AX_X, ALU.add))
            dve.wait_ge(norm_ready, 1)

            def k_and_z(j):
                u = j % 2
                if j >= 2:
                    dve.wait_ge(kt_ps, j - 1)
                    dve.wait_ge(r_out[u], 16 * (j // 2))
                dve.tensor_tensor(kn[:, u].rearrange(IN_HEADS, e=DK), x[:, j, :].rearrange(IN_HEADS, e=DK),
                                  ss[:, j * H:(j + 1) * H].unsqueeze(2).broadcast_to([P, H, DK]),
                                  ALU.mult).then_inc(kn_ready, 1)
                dve.wait_ge(kn_ready, j + 1)
                dve.tensor_tensor(z[:, u], v_nat[:, j, :], kn[:, u], ALU.subtract).then_inc(z_ready, 1)

            k_and_z(0)
            for j in range(NT):
                u = j % 2
                if j + 1 < NT:
                    k_and_z(j + 1)
                dve.wait_ge(zw_ready, j + 1)
                then(dve.tensor_reduce(V["mean_r"][:, u, :], z[:, u].rearrange(IN_HEADS, e=DK), AX_X, ALU.add))
                dve.scalar_tensor_tensor(out=z[:, u].rearrange(IN_HEADS, e=DK),
                                         in0=V["mean_r"][:, u, :].unsqueeze(2).broadcast_to([P, H, DK]),
                                         scalar=-1.0 / DK, in1=z[:, u].rearrange(IN_HEADS, e=DK), op0=ALU.mult,
                                         op1=ALU.add).then_inc(r_ready, 1)

        @block.gpsimd
        def _(pool):
            pool.wait_ge(row_in, 32)
            for j in range(NT):
                u = j % 2
                pool.wait_ge(z_ready, j + 1)
                pool.tensor_tensor(z[:, u], z[:, u], b_row, ALU.subtract).then_inc(w_step, 1)
                pool.wait_ge(w_step, j + 1)
                pool.tensor_tensor(z[:, u], z[:, u], w_row, ALU.mult).then_inc(zw_ready, 1)

        @block.scalar
        def _(act):
            act.wait_ge(ss_ready, 1)
            act.activation(ss, ss, ACT.Sqrt).then_inc(norm_ready, 1)
            for j in range(NT):
                act.wait_ge(kt_ps, j + 1)
                act.copy(by_chunk(kt, j), bank[j % 2][:, 0:D].rearrange("p (f r c) -> p f r c", f=2, r=CT)).then_inc(kt_ready, 1)

        @block.tensor
        def _(pe):
            pe.wait_ge(rows_ready, 1)
            for r in range(CT):
                mm = pe.matmul(ps_e[r // 4][:, (r % 4) * P:(r % 4 + 1) * P],
                               rows_of[:, r * P:(r + 1) * P], eta_n,
                               start=True, stop=True)
            mm.then_inc(eta_ps, 1)
            for j in range(NT):
                pe.wait_ge(kn_ready, j + 1)
                if j >= 2:
                    pe.wait_ge(kt_ready, j - 1)
                for f in range(DH):
                    mm = pe.transpose(bank[j % 2][:, f * P:(f + 1) * P], kn[:, j % 2, f * P:(f + 1) * P], S["ident"][:])
                mm.then_inc(kt_ps, 1)


def scan(nc, S, d):
    B = 2 * C
    V = carve(S["work"], ATT + [
        ("k_bd", (2, 2 * B)), ("eye_q", (2, 4 * B)), ("kq_bd", (2, 2 * B)), ("turned", (2, 4 * B)),
        ("state", (2 * DK,)), ("one_a", (2, 2 * DK)), ("terms", (2, 5 * (DK + 1))),
        ("sums", (2, 6)), ("rho", (2,)), ("by_rho", (2, 6)), ("root", (2,)), ("rate", (2,)),
        ("u", (2, DK)), ("w", (2, DK)), ("xx", (2, 2 * DK)), ("e", (2, DK)), ("f", (2, DK)), ("y", (2, DK)),
        ("v", (2, 2 * DK)), ("zero", (2 * DK,))])
    kt, qt, r, eta = (V[n] for n in ("kt", "qt", "r", "eta"))
    halves = lambda t: t.rearrange("p (f n) -> p f n", f=2)
    terms = V["terms"].rearrange("p f (g e) -> p f g e", g=5)
    one_a = V["one_a"].rearrange("p f (g e) -> p f g e", g=2)
    xx = V["xx"].rearrange("p f (g e) -> p f g e", g=2)
    state, k_bd, kq_bd, v = (V[n] for n in ("state", "k_bd", "kq_bd", "v"))
    eye_q = V["eye_q"].rearrange("p u (f n) -> p u f n", f=2)
    turned = V["turned"].rearrange("p u (f n) -> p u f n", f=2)
    bank = S["bank"]
    ps_kh, ps_s, ps_prep, ps_o = bank[0], bank[1], bank[2:4], bank[4:6]
    g = lambda n: S["sem"](f"scan_{n}")
    r_in, a_in, setup, zeroed = g("r_in"), g("a_in"), g("setup"), g("zeroed")
    k_ready, q_ready, kq_ready = g("k_bd_ready"), g("q_bd_ready"), g("kq_bd_ready")
    prep_ps, turned_ready = g("prep_ps"), g("turned_ready")
    state_ready, kh_ps, rho_ready, root_ready, v_ready = (
        g("state_ready"), g("kh_ps"), g("rho_ready"), g("root_ready"), g("v_ready"))
    s_ps, qs_ps, o_ps, o_ready, step = g("s_ps"), g("qs_ps"), g("o_ps"), g("o_ready"), g("step")

    later = lambda i: not isinstance(i, int)
    chunk = lambda t, i: t[:, bass.ds(i, 1), :].rearrange("p a (f c) -> p (a f) c", f=2)

    with nc.Block() as block:
        @block.sync
        def _(sp):
            src = S["r_d"].rearrange("(i c) (f h e) -> h f c i e", c=C, f=2, h=HH)
            for h in range(HH):
                for f in range(2):
                    sp.dma_start(r[h * C:(h + 1) * C, :, f * DK:(f + 1) * DK], src[h, f]).then_inc(r_in, 16)
            w = d["ln_w"]
            for f in range(2):
                sp.dma_start(one_a[:, f, 1, :], w[f * HH:(f + 1) * HH, :].unsqueeze(1).broadcast_to([HH, C, DK])
                             ).then_inc(a_in, 16)

        @block.gpsimd
        def _(pool):
            pairs = lambda t: t.rearrange("p (f h c) -> p f h c", f=2, h=2)
            mask = lambda m: m[:].rearrange("p (h c) -> p h c", h=2).unsqueeze(1).broadcast_to([P, 2, 2, C])
            wide = lambda t: t.unsqueeze(2).broadcast_to([P, 2, 2, C])

            def spread(i, u):
                if later(i) or i >= 2:
                    pool.wait_ge(kh_ps, i - 1)
                pool.tensor_tensor(pairs(k_bd[:, u]), wide(chunk(kt, i)), mask(S["own_head"]),
                                   ALU.mult).then_inc(k_ready, 1)
                if later(i) or i >= 2:
                    pool.wait_ge(qs_ps, i - 1)
                pool.tensor_tensor(eye_q[:, u, :, B:].rearrange("p f (h c) -> p f h c", h=2), wide(chunk(qt, i)), mask(S["own_head"]),
                                   ALU.mult).then_inc(q_ready, 1)

            def cut(i, u):
                pool.wait_ge(turned_ready, i + 1)
                if later(i) or i >= 2:
                    pool.wait_ge(o_ps, i - 1)
                pool.tensor_tensor(halves(kq_bd[:, u]), turned[:, u, :, B:],
                                   S["causal"][:].unsqueeze(1).broadcast_to([P, 2, B]),
                                   ALU.mult).then_inc(kq_ready, 1)

            spread(0, 0)
            spread(1, 1)
            cut(0, 0)
            spread(2, 0)
            cut(1, 1)
            spread(3, 1)
            with pool.Fori(1, NC // 2 - 1) as n:
                for u in range(2):
                    cut(n * 2 + u, u)
                    spread(n * 2 + (u + 2), u)
            cut(NC - 2, 0)
            cut(NC - 1, 1)

        @block.scalar
        def _(act):
            act.wait_ge(a_in, 32)
            act.activation(one_a[:, :, 0, :], one_a[:, :, 1, :], ACT.Square).then_inc(setup, 1)

            def prepared(i, u):
                act.wait_ge(prep_ps, i + 1)
                if later(i) or i >= 2:
                    act.wait_ge(s_ps, i - 1)
                    act.wait_ge(kq_ready, i - 1)
                act.activation(V["turned"][:, u], ps_prep[u][:, 0:4 * B], ACT.Copy, scale=-1.0).then_inc(turned_ready, 1)

            def output(i, u):
                act.wait_ge(o_ps, i + 1)
                act.copy(r[:, bass.ds(i, 1), :].rearrange("p a n -> p (a n)"), ps_o[u][:, 0:2 * DK]).then_inc(o_ready, 1)

            def root(i):
                act.wait_ge(rho_ready, i + 1)
                act.activation(V["root"], V["rho"], ACT.Sqrt, scale=float(DK)).then_inc(root_ready, 1)

            def body(i, u):
                output(i - 1, 1 - u)
                root(i)
                prepared(i + 1, 1 - u)

            prepared(0, 0)
            root(0)
            prepared(1, 1)
            body(1, 1)
            with act.Fori(1, NC // 2 - 1) as n:
                body(n * 2, 0)
                body(n * 2 + 1, 1)
            body(NC - 2, 0)
            output(NC - 2, 0)
            root(NC - 1)
            output(NC - 1, 1)

        @block.tensor
        def _(pe):
            at = lambda n: pe.to_reg(n) if later(n) else n

            def blocks(out, lhs, rhs, start, stop):
                for f in range(2):
                    for b in range(0, P, B):
                        q = slice(b, b + B)
                        mm = pe.matmul(out[q, f], lhs[q, f], rhs[q, f],
                                       start=start and f == 0, stop=stop and f == 1, skip_group_check=True,
                                       tile_position=(b, b))
                return mm

            def prepare(i, u):
                spread, read = at(i + 1), at(i - 1)
                pe.wait_ge(zeroed, 1)
                pe.wait_ge(k_ready, spread)
                pe.wait_ge(q_ready, spread)
                if later(i) or i >= 2:
                    pe.wait_ge(turned_ready, read)
                blocks(halves(ps_prep[u][:, 0:4 * B]), halves(k_bd[:, u]), eye_q[:, u], True, True).then_inc(prep_ps, 1)

            def kh(i, u):
                done = at(i + 1)
                pe.wait_ge(zeroed, 1)
                pe.wait_ge(state_ready, done)
                blocks(halves(ps_kh[:, 0:2 * DK]), halves(k_bd[:, u]), halves(state), True, True).then_inc(kh_ps, 1)

            def q_state(i, u):
                done = at(i - 1)
                if later(i) or i >= 2:
                    pe.wait_ge(zeroed, 1)
                    pe.wait_ge(o_ready, done)
                blocks(halves(ps_o[u][:, 0:2 * DK]), eye_q[:, u, :, B:], halves(state), True, False).then_inc(qs_ps, 1)

            def update(i, u):
                done = at(i + 1)
                pe.wait_ge(zeroed, 1)
                pe.wait_ge(v_ready, done)
                pe.wait_ge(turned_ready, done)
                blocks(halves(ps_s[:, 0:2 * DK]), turned[:, u, :, 0:B], halves(v[:, u]), False, False).then_inc(s_ps, 1)

            def finish(i, u):
                done = at(i + 1)
                pe.wait_ge(zeroed, 1)
                pe.wait_ge(kq_ready, done)
                blocks(halves(ps_o[u][:, 0:2 * DK]), halves(kq_bd[:, u]), halves(v[:, u]), False, True).then_inc(o_ps, 1)

            def body(i, u, more=True):
                kh(i, u)
                if later(i) or i:
                    finish(i - 1, 1 - u)
                q_state(i, u)
                if more:
                    prepare(i + 1, 1 - u)
                update(i, u)

            pe.wait_ge(zeroed, 1)
            pe.matmul(ps_s[:, 0:2 * DK], S["ident"][:], V["zero"], start=True, stop=False, skip_group_check=True)
            prepare(0, 0)
            body(0, 0)
            body(1, 1)
            with pe.Fori(1, NC // 2 - 1) as n:
                body(n * 2, 0)
                body(n * 2 + 1, 1)
            body(NC - 2, 0)
            body(NC - 1, 1, False)
            finish(NC - 1, 1)

        @block.vector
        def _(dve):
            f2 = lambda t: t.unsqueeze(2).broadcast_to([P, 2, DK])
            eye = S["ident"][:].rearrange("p (b n) -> p n b", n=B)
            for u in range(2):
                for f in range(2):
                    dve.tensor_reduce(eye_q[:, u, f, 0:B], eye, AX_X, ALU.add)
            dve.memset(V["zero"], 0.0).then_inc(zeroed, 1)
            dve.memset(V["terms"], 0.0).then_inc(step, 1)
            dve.wait_ge(step, 1)
            dve.memset(terms[:, :, 3, DK:DK + 1], float(DK) * EPS).then_inc(step, 1)
            dve.wait_ge(setup, 1)
            dve.tensor_scalar(one_a[:, :, 1, :], one_a[:, :, 0, :], -float(DK), None, ALU.mult).then_inc(step, 1)
            dve.wait_ge(step, 3)
            dve.memset(one_a[:, :, 0, :], 1.0).then_inc(step, 1)
            dve.wait_ge(step, 4)
            dve.wait_ge(r_in, 16 * 2 * HH)
            base, OPS = 4, 14

            def body(i, u):
                def upto(n):
                    dve.wait_ge(step, i * OPS + (base + n))

                eta_i = eta[:, bass.ds(i, 1), :].rearrange("p a f -> p (a f)")
                r_i = chunk(r, i)
                x_ps = halves(ps_kh[:, 0:2 * DK])
                x = terms[:, :, 0, 0:DK]
                sums, rho, by_rho, u_, w = V["sums"], V["rho"], V["by_rho"], V["u"], V["w"]
                if later(i) or i >= 1:
                    dve.wait_ge(s_ps, i)
                    dve.tensor_copy(state, ps_s[:, 0:2 * DK]).then_inc(state_ready, 1)
                else:
                    dve.tensor_copy(state, V["zero"]).then_inc(state_ready, 1)
                dve.tensor_copy(sums[:, :, 5], eta_i).then_inc(step, 1)
                dve.wait_ge(kh_ps, i + 1)
                dve.tensor_tensor(terms[:, :, 0:2, 0:DK], x_ps.unsqueeze(2).broadcast_to([P, 2, 2, DK]),
                                  one_a, ALU.mult).then_inc(step, 1)
                dve.tensor_tensor(terms[:, :, 2, 0:DK], x_ps, r_i, ALU.mult).then_inc(step, 1)
                upto(2)
                dve.tensor_tensor(terms[:, :, 3:5, 0:DK], terms[:, :, 0:2, 0:DK],
                                  x.unsqueeze(2).broadcast_to([P, 2, 2, DK]), ALU.mult).then_inc(step, 1)
                upto(4)
                dve.tensor_reduce(sums[:, :, 0:4], terms[:, :, 1:5, :], AX_X, ALU.add).then_inc(step, 1)
                upto(5)
                dve.reciprocal(rho, sums[:, :, 2]).then_inc(rho_ready, 1)
                dve.scalar_tensor_tensor(out=u_, in0=f2(sums[:, :, 0]), scalar=1.0 / DK, in1=terms[:, :, 1, 0:DK],
                                         op0=ALU.mult, op1=ALU.subtract).then_inc(step, 1)
                dve.wait_ge(rho_ready, i + 1)
                dve.tensor_tensor(by_rho[:, :, 0:5:2], sums[:, :, 1:6:2], rho.unsqueeze(2).broadcast_to([P, 2, 3]),
                                  ALU.mult).then_inc(step, 1)
                upto(7)
                dve.tensor_tensor(by_rho[:, :, 1], by_rho[:, :, 2], by_rho[:, :, 4], ALU.mult).then_inc(step, 1)
                dve.tensor_tensor(w, u_, f2(by_rho[:, :, 4]), ALU.mult).then_inc(step, 1)
                upto(8)
                dve.tensor_tensor(xx, x.unsqueeze(2).broadcast_to([P, 2, 2, DK]),
                                  by_rho[:, :, 0:2].unsqueeze(3).broadcast_to([P, 2, 2, DK]),
                                  ALU.mult).then_inc(step, 1)
                dve.wait_ge(root_ready, i + 1)
                dve.tensor_tensor(V["rate"], V["root"], eta_i, ALU.mult).then_inc(step, 1)
                upto(10)
                dve.tensor_tensor(V["e"], xx[:, :, 0], r_i, ALU.subtract).then_inc(step, 1)
                dve.tensor_tensor(V["f"], xx[:, :, 1], w, ALU.add).then_inc(step, 1)
                upto(12)
                dve.tensor_tensor(V["y"], V["e"], f2(V["rate"]), ALU.mult).then_inc(step, 1)
                upto(14)
                dve.tensor_tensor(halves(v[:, u]), V["y"], V["f"], ALU.add).then_inc(v_ready, 1)

            body(0, 0)
            body(1, 1)
            with dve.Fori(1, NC // 2) as n:
                body(n * 2, 0)
                body(n * 2 + 1, 1)


def attention_output(nc, S, d, x1_d, x2_d):
    V = carve(S["work"], [
        ("qh", (NT, D)), ("q", (NT, D)), ("r", (NC, 2 * DK)), ("gate", (NT, D)), ("w_o", (DH, D)), ("w_row", (D,)),
        ("b_row", (D,)), ("norm", (DH,)), ("ss", (NT * H,)), ("mean", (NT * H,))])
    qh, q, r, gate, w_o, ss, mean = (V[n] for n in ("qh", "q", "r", "gate", "w_o", "ss", "mean"))
    x1 = r.rearrange("p i n -> p (i n)").rearrange("p (j n) -> p j n", j=NT)
    turned = q
    bank = S["bank"]
    g = lambda n: S["sem"](f"out_{n}")
    o_out, load, qh_in, x1_in = g("o_out"), g("load"), g("qh_in"), g("x1_in")
    centred, sq_ps, ss_done, var_ready, rstd_ready = g("centred"), g("sq_ps"), g("ss_done"), g("var_ready"), g("rstd_ready")
    scaled, wb_done, gated, ot_ps, ot_ready, y_ps, y_done, y_out = (
        g("scaled"), g("wb_done"), g("gated"), g("ot_ps"), g("ot_ready"), g("y_ps"), g("y_done"), g("y_out"))
    step, w_step, unit = g("step"), g("w_step"), g("unit")
    with nc.Block() as block:
        @block.sync
        def _(sp):
            dst = S["qh_d"].rearrange("(i c) (f h e) -> h f c i e", c=C, f=2, h=HH)
            for h in range(HH):
                for f in range(2):
                    sp.dma_start(dst[h, f], r[h * C:(h + 1) * C, :, f * DK:(f + 1) * DK]).then_inc(o_out, 16)
            sp.wait_ge(o_out, 16 * 2 * HH)
            sp.dma_start(qh, by_tile(S["qh_d"])).then_inc(qh_in, 16)
            sp.dma_start(x1, by_tile(x1_d)).then_inc(x1_in, 16)
            rows = x2_d.rearrange("(j p) n -> j p n", p=P)
            for j in range(NT):
                sp.wait_ge(y_done, j + 1)
                sp.dma_start(rows[j], x1[:, j, :]).then_inc(y_out, 16)
            sp.wait_ge(y_out, 16 * NT)

        @block.scalar
        def _(act):
            act.dma_start(q, by_tile(S["q_d"])).then_inc(load, 16)
            act.dma_start(gate, by_tile(S["gate_d"])).then_inc(load, 16)
            act.dma_start(w_o, d["w_o"]).then_inc(load, 16)
            act.dma_start(V["norm"], d["norm_w"]).then_inc(load, 16)
            act.dma_start(V["w_row"], d["ln_w_row"].broadcast_to([P, D])).then_inc(load, 16)
            act.dma_start(V["b_row"], d["ln_b_row"].broadcast_to([P, D])).then_inc(load, 16)

            def squares(j, n, ready):
                act.wait_ge(ready, j + 1)
                if n >= 2:
                    act.wait_ge(ss_done, n - 1)
                act.activation(bank[n % 2][:, 0:D], qh[:, j, :], ACT.Square).then_inc(sq_ps, 1)

            for j in range(NT):
                squares(j, j, centred)
            act.wait_ge(var_ready, 1)
            act.activation(ss, ss, ACT.Sqrt).then_inc(rstd_ready, 1)
            for j in range(NT):
                squares(j, NT + j, gated)
            act.wait_ge(var_ready, 2)
            act.activation(ss, ss, ACT.Sqrt).then_inc(rstd_ready, 1)
            act.wait_ge(load, 96)
            for j in range(NT):
                act.wait_ge(ot_ps, j + 1)
                for f in range(DH):
                    act.activation(turned[:, j, f * P:(f + 1) * P], bank[2 + j % 2][:, f * P:(f + 1) * P], ACT.Copy,
                                   scale=V["norm"][:, f:f + 1]).then_inc(ot_ready, 1)

        @block.gpsimd
        def _(pool):
            pool.wait_ge(load, 96)
            for j in range(NT):
                pool.wait_ge(scaled, j + 1)
                pool.tensor_tensor(qh[:, j, :], qh[:, j, :], V["w_row"], ALU.mult).then_inc(w_step, 1)
                pool.wait_ge(w_step, j + 1)
                pool.tensor_tensor(qh[:, j, :], qh[:, j, :], V["b_row"], ALU.add).then_inc(wb_done, 1)

        @block.vector
        def _(dve):
            n = [0]

            def then(ins):
                n[0] += 1
                ins.then_inc(step, 1)
                dve.wait_ge(step, n[0])

            hd = lambda t: t.rearrange(IN_HEADS, e=DK)
            per = lambda t, j: t[:, j * H:(j + 1) * H].unsqueeze(2).broadcast_to([P, H, DK])
            dve.wait_ge(qh_in, 16)

            def summed(j, n):
                dve.wait_ge(sq_ps, n + 1)
                dve.tensor_reduce(ss[:, j * H:(j + 1) * H], hd(bank[n % 2][:, 0:D]), AX_X, ALU.add).then_inc(ss_done, 1)

            def inverse(n):
                dve.wait_ge(ss_done, NT * n)
                then(dve.tensor_scalar(ss, ss, 1.0 / DK, EPS, ALU.mult, ALU.add))
                dve.reciprocal(ss, ss).then_inc(var_ready, 1)
                dve.wait_ge(rstd_ready, n)

            then(dve.tensor_reduce(mean, qh.rearrange("p j n -> p (j n)").rearrange(IN_HEADS, e=DK), AX_X, ALU.add))
            for j in range(NT):
                dve.scalar_tensor_tensor(out=hd(qh[:, j, :]), in0=per(mean, j), scalar=-1.0 / DK, in1=hd(qh[:, j, :]),
                                         op0=ALU.mult, op1=ALU.add).then_inc(centred, 1)
                if j:
                    summed(j - 1, j - 1)
            summed(NT - 1, NT - 1)
            inverse(1)
            for j in range(NT):
                dve.tensor_tensor(hd(qh[:, j, :]), hd(qh[:, j, :]), per(ss, j), ALU.mult).then_inc(scaled, 1)
            dve.wait_ge(load, 96)
            for j in range(NT):
                dve.wait_ge(wb_done, j + 1)
                then(dve.tensor_tensor(qh[:, j, :], qh[:, j, :], q[:, j, :], ALU.add))
                dve.tensor_tensor(qh[:, j, :], qh[:, j, :], gate[:, j, :], ALU.mult).then_inc(gated, 1)
                if j:
                    summed(j - 1, NT + j - 1)
            summed(NT - 1, 2 * NT - 1)
            inverse(2)
            for j in range(NT):
                dve.tensor_tensor(hd(qh[:, j, :]), hd(qh[:, j, :]), per(ss, j), ALU.mult).then_inc(unit, 1)
            dve.wait_ge(x1_in, 16)
            for j in range(NT):
                dve.wait_ge(y_ps, j + 1)
                dve.tensor_tensor(x1[:, j, :], x1[:, j, :], bank[4 + j % 2][:, 0:D], ALU.add).then_inc(y_done, 1)

        @block.tensor
        def _(pe):
            def turn(j):
                pe.wait_ge(unit, j + 1)
                if j >= 2:
                    pe.wait_ge(ot_ready, 2 * (j - 1))
                for f in range(DH):
                    mm = pe.transpose(bank[2 + j % 2][:, f * P:(f + 1) * P], qh[:, j, f * P:(f + 1) * P], S["ident"][:])
                mm.then_inc(ot_ps, 1)

            turn(0)
            for j in range(NT):
                if j + 1 < NT:
                    turn(j + 1)
                pe.wait_ge(ot_ready, 2 * (j + 1))
                if j >= 2:
                    pe.wait_ge(y_done, j - 1)
                for f in range(DH):
                    mm = pe.matmul(bank[4 + j % 2][:, 0:D], turned[:, j, f * P:(f + 1) * P], w_o[:, f, :],
                                   start=(f == 0), stop=(f == DH - 1))
                mm.then_inc(y_ps, 1)


def kernel(**inputs):
    import numpy as np
    import concourse.bacc as bacc
    from concourse.bass_utils import run_bass_kernel_spmd

    a = {k: np.asarray(v) for k, v in inputs.items()}
    rows = lambda w: np.ascontiguousarray(w.reshape(DH, P, -1).transpose(1, 0, 2))
    att = lambda n: a["L0_attn_" + n]
    ffn = lambda n: a["L0_ffn_" + n]
    gu = np.concatenate([np.concatenate([ffn("gate_w"), ffn("shared_gate_w")[None]]),
                         np.concatenate([ffn("up_w"), ffn("shared_up_w")[None]])], axis=1)
    down = np.concatenate([ffn("down_w"), ffn("shared_down_w")[None]]).transpose(2, 0, 1)
    arrays = {
        "x": att("x").reshape(T, D),
        "w_gu": gu.reshape(E + 1, 2 * I, DH, P).transpose(3, 0, 2, 1).reshape(P, E + 1, DH * 2 * I),
        "w_d1": down[0:P], "w_d2": down[P:],
        "rt": rows(ffn("router_w").T).reshape(P, DH * E), "rb": ffn("router_b")[None],
        "w_kv": rows(np.concatenate([att("Wk"), att("Wv")], axis=1)),
        "w_q": rows(np.concatenate([att("Wq"), att("Wbeta"), att("Wg1")], axis=1)),
        "w_g2": att("Wg2"), "w_o": rows(att("Wo")), "norm_w": att("norm_w").reshape(DH, P).T,
        "ln_w": att("ln_w"), "ln_w_row": att("ln_w").reshape(1, D), "ln_b_row": att("ln_b").reshape(1, D),
    }
    arrays = {k: np.ascontiguousarray(v) for k, v in arrays.items()}
    nc = bacc.Bacc("TRN2", target_bir_lowering=False, num_devices=1)
    d = {k: nc.dram_tensor(k + "_in", v.shape, F32, kind="ExternalInput").ap() for k, v in arrays.items()}
    d["out"] = nc.dram_tensor("out", (T, D), F32, kind="ExternalOutput").ap()
    build(nc, d)
    r = run_bass_kernel_spmd(nc, [{k + "_in": v for k, v in arrays.items()}], core_ids=[0])
    return r.results[0]["out"].reshape(1, T, D)
```

```python
from contextlib import ExitStack

import concourse.bass as bass
from concourse import mybir

ALU = mybir.AluOpType
ACT = mybir.ActivationFunctionType
F32 = mybir.dt.float32
I32 = mybir.dt.int32
U32 = mybir.dt.uint32
AX_X = mybir.AxisListType.X

P = 128
T, D = 1024, 256
NT = T // P
DH = D // P
E, I, K = 32, 192, 4
IR = I - P
H, DK, C = 16, 16, 16
HH = H // 2
NC = T // C
CT = P // C
TILES = (T * K + E * (P - 1)) // P
SKIP = 100000
LN_EPS, EPS = 1e-5, 1e-6
SCALE = 1.8
ROWS = K * T


def build(nc, d):
    with ExitStack() as ctx:
        def sb(name, shape, dt=F32):
            return ctx.enter_context(nc.sbuf_tensor(name, shape, dt))

        def sem(name):
            return ctx.enter_context(nc.semaphore(name))

        def dram(name, shape):
            return nc.dram_tensor(name, shape, F32, kind="Internal").ap()

        def named(name):
            if name not in sems:
                sems[name] = sem(name)
            return sems[name]

        sems = {}

        w_gu = sb("w_gu", [P, E + 1, DH * 2 * I])
        w_d1 = sb("w_d1", [P, E + 1, D])
        w_d2 = sb("w_d2", [P, E + 1, D])
        aux = w_d2[IR:P, :, :].rearrange("p e n -> p (e n)")
        ident = sb("ident", [P, P])
        same_head = sb("same_head", [P, P])
        own_head = sb("own_head", [P, 2 * C])
        causal = sb("causal", [P, 2 * C])
        earlier = sb("earlier", [P, P])
        ones = sb("ones", [P, P])
        count = sb("count", [P, P])
        pair_row = sb("pair_row", [P, NT, K])
        take = sb("take", [P, TILES], I32)
        put = sb("put", [P, TILES], I32)
        tile_expert = sb("tile_expert", [1, TILES], I32)
        mix = sb("mix", [P, NT, K])
        rt = sb("rt", [P, DH * E])
        rb = sb("rb", [P, E])
        work = sb("work", [P, 9888])
        bank = [ctx.enter_context(nc.psum_tensor(f"bank{n}", [P, 512], F32)) for n in range(8)]

        S = dict(w_gu=w_gu, aux=aux, w_d1=w_d1, w_d2=w_d2, ident=ident, same_head=same_head,
                 own_head=own_head, causal=causal,
                 earlier=earlier, ones=ones, count=count, pair_row=pair_row, take=take, put=put,
                 tile_expert=tile_expert, mix=mix, rt=rt, rb=rb, work=work, bank=bank,
                 weights_in=sem("weights_in"), back=sem("back"), shared_in=sem("shared_in"), sem=named)
        S["xln_d"] = dram("xln_d", [T, D])
        S["res_d"] = dram("res_d", [ROWS, D])
        x1_d = dram("x1_d", [T, D])
        S["q_d"], S["gate_d"] = dram("q_d", [T, D]), dram("gate_d", [T, D])
        S["r_d"], S["qh_d"] = dram("r_d", [T, D]), dram("qh_d", [T, D])

        constants(nc, S, d, sem)
        route(nc, S, d, "a")
        expert_tiles(nc, S, "a")
        combine(nc, S, "a", x1_d)
        attention_inputs(nc, S, d)
        clear(nc, [sems[name] for name in sems if name.startswith("ffn_")])
        scan(nc, S, d, x1_d)
        attention_output(nc, S, d, x1_d)
        route(nc, S, d, "b")
        expert_tiles(nc, S, "b")
        combine(nc, S, "b", d["out"])


def clear(nc, semaphores):
    with nc.Block() as block:
        @block.sync
        def _(sp):
            for s in semaphores:
                sp.sem_clear(s)


def warm_up(pe, S, out, count):
    for _ in range(count):
        pe.matmul(out[:, 0:P], S["ident"][:], S["ident"][:], start=True, stop=True)


def carve(work, sizes):
    out, at = {}, 0
    for name, shape in sizes:
        n = 1
        for s in shape:
            n *= s
        v = work[:, at:at + n]
        if len(shape) == 2:
            v = v.rearrange("p (a b) -> p a b", a=shape[0])
        elif len(shape) == 3:
            v = v.rearrange("p (a b c) -> p a b c", a=shape[0], b=shape[1])
        out[name] = v
        at += n
    assert at <= work.shape[1], at
    return out


def by_tile(ap):
    return ap.rearrange("(j p) n -> p j n", p=P)


def constants(nc, S, d, sem):
    made, read = sem("made"), sem("c_read")
    with nc.Block() as block:
        @block.sync
        def _(sp):
            sp.dma_start(S["rt"][:], d["rt"]).then_inc(read, 16)
            sp.dma_start(S["rb"][:], d["rb"].broadcast_to([P, E])).then_inc(read, 16)
            sp.wait_ge(read, 32)

        @block.gpsimd
        def _(pool):
            ident, same, earlier = S["ident"], S["same_head"], S["earlier"]
            causal = S["work"][:, NT * D:NT * D + P]
            heads = lambda t: t.rearrange("p (h c) -> p h c", c=C)
            pool.memset(S["ones"][:], 1.0).then_inc(made, 1)
            pool.iota(S["count"][:], [[1, P]], base=0, channel_multiplier=0,
                      allow_small_or_imprecise_dtypes=True)
            pool.iota(S["pair_row"][:], [[P, NT], [T, K]], base=1, channel_multiplier=1,
                      allow_small_or_imprecise_dtypes=True).then_inc(made, 1)
            pool.wait_ge(made, 2)
            pool.affine_select(out=ident[:], in_=S["ones"][:], pattern=[[-1, P]], compare_op=ALU.is_equal,
                               fill=0.0, base=0, channel_multiplier=1).then_inc(made, 1)
            pool.affine_select(out=earlier[:], in_=S["ones"][:], pattern=[[1, P]], compare_op=ALU.is_ge,
                               fill=0.0, base=-1, channel_multiplier=-1).then_inc(made, 1)
            pool.affine_select(out=heads(causal), in_=heads(S["ones"][:]), pattern=[[-C, HH], [0, C]],
                               compare_op=ALU.is_ge, fill=0.0, base=0, channel_multiplier=1).then_inc(made, 1)
            pool.wait_ge(made, 5)
            pool.affine_select(out=heads(same[:]), in_=heads(causal), pattern=[[C, HH], [0, C]],
                               compare_op=ALU.is_ge, fill=0.0, base=C - 1, channel_multiplier=-1).then_inc(made, 1)
            pool.wait_ge(made, 6)
            pool.affine_select(out=heads(causal), in_=heads(same[:]), pattern=[[C, HH], [1, C]],
                               compare_op=ALU.is_ge, fill=0.0, base=0, channel_multiplier=-1).then_inc(made, 1)

        @block.vector
        def _(dve):
            dve.wait_ge(made, 7)
            fold = lambda t: t.rearrange("p (b n) -> p n b", b=P // (2 * C))
            dve.tensor_reduce(S["own_head"][:], fold(S["same_head"][:]), AX_X, ALU.add)
            dve.tensor_reduce(S["causal"][:], fold(S["work"][:, NT * D:NT * D + P]), AX_X, ALU.add)

        @block.scalar
        def _(act):
            act.dma_start(ffn_views(S)["x"], by_tile(d["x"])).then_inc(S["sem"]("ffn_x_in"), 16)
            load_experts(act, S, d, E, E + 1, S["shared_in"])
            load_experts(act, S, d, *GROUPS[0], S["weights_in"])


GROUPS = ((0, 5), (5, 14), (14, 23), (23, E))


def load_experts(eng, S, d, a, b, loaded):
    eng.dma_start(S["w_gu"][:, a:b, :], d["w_gu"][:, a:b, :]).then_inc(loaded, 16)
    eng.dma_start(S["w_d1"][:, a:b, :], d["w_d1"][:, a:b, :]).then_inc(loaded, 16)
    eng.dma_start(S["w_d2"][0:IR, a:b, :], d["w_d2"][:, a:b, :]).then_inc(loaded, 16)


def ffn_views(S):
    return carve(S["work"], [
        ("x", (NT, D)), ("chosen", (NT * K, E)), ("picked", (NT * K, E)), ("xt", (NT, D)), ("logits", (NT, E)),
        ("top", (NT, 8)), ("top_i", (NT, 8)), ("expert", (NT, 8)), ("members", (NT, E)),
        ("before", (NT, E)), ("slot_of", (NT, E)), ("slot", (NT * K,)),
        ("slot_tile", (NT * K,)), ("slot_pos", (NT * K,)), ("shared", (1536,)),
        ("turn", (P,)), ("small", (656,))])


def layer_stats(dve, inverse_ready, V, x, loaded, done):
    st, mean, var = V["stats"], V["mean"], V["var"]
    if loaded:
        dve.wait_ge(loaded, 16)
    for j in range(NT):
        dve.bn_stats(st[:, j, :], x[:, j, :]).then_inc(done, 1)
    dve.wait_ge(done, NT)
    dve.tensor_tensor(V["t1"], st[:, :, 1], st[:, :, 4], ALU.subtract).then_inc(done, 1)
    dve.tensor_tensor(V["t2"], st[:, :, 1], st[:, :, 4], ALU.add).then_inc(done, 1)
    dve.tensor_tensor(V["t3"], st[:, :, 2], st[:, :, 5], ALU.add).then_inc(done, 1)
    dve.wait_ge(done, NT + 3)
    dve.scalar_tensor_tensor(out=V["t4"], in0=V["t1"], scalar=0.25, in1=V["t1"], op0=ALU.mult,
                             op1=ALU.mult).then_inc(done, 1)
    dve.tensor_scalar(mean, V["t2"], 0.5, None, ALU.mult).then_inc(done, 1)
    dve.tensor_scalar(V["t5"], V["t3"], 1.0 / D, LN_EPS, ALU.mult, ALU.add).then_inc(done, 1)
    dve.wait_ge(done, NT + 6)
    dve.tensor_tensor(var, V["t5"], V["t4"], ALU.add).then_inc(done, 1)
    dve.wait_ge(done, NT + 7)
    dve.reciprocal(V["t6"], var).then_inc(inverse_ready, 1)


def stat_views(at):
    V = {"stats": at[:, 0:48].rearrange("p (j s) -> p j s", s=6)}
    for n, name in enumerate(("mean", "rstd", "var", "t1", "t2", "t3", "t4", "t5", "t6")):
        V[name] = at[:, 48 + 8 * n:56 + 8 * n]
    return V


def route(nc, S, d, tag):
    V = ffn_views(S)
    small = V["small"]
    st = stat_views(small[:, 0:120])
    shifted = small[:, 120:152].rearrange("p (j k) -> p j k", k=K)
    exps = small[:, 152:184].rearrange("p (j k) -> p j k", k=K)
    total = small[:, 184:192]
    per = small[:, 192:200]
    members_all = small[:, 200:232]
    counted = small[:, 232:264].bitcast(I32)
    tiles_of = small[:, 264:296].bitcast(I32)
    tiles_end = small[:, 296:328]
    first_slot = small[:, 328:360]
    slot_int = small[:, 360:392].bitcast(I32)
    tile_int = small[:, 392:424].bitcast(I32)
    pos_int = small[:, 424:456].bitcast(I32)
    row_f = small[:, 456:456 + TILES]
    empty = small[:, 520:520 + TILES]
    ended = small[0:E, 584:584 + TILES]
    counted_c = small[0:E, 648:649].bitcast(I32)
    tiles_c = small[0:E, 649:650].bitcast(I32)
    tiles_cf = small[0:E, 650:651]
    x, xt = V["x"], V["xt"]
    xn = S["work"][:, NT * D:2 * NT * D].rearrange("p (j n) -> p j n", j=NT)
    logits, top, expert = V["logits"], V["top"], V["expert"]
    top_i = V["top_i"].bitcast(U32)
    chosen = V["chosen"].rearrange("p (j k) e -> p j k e", k=K)
    picked = V["picked"].rearrange("p (j k) e -> p j k e", k=K)
    is_pos = S["work"][:, NT * D:NT * D + 2 * K * P].rearrange("p (u k q) -> p u k q", u=2, k=K)
    is_tile = S["work"][:, NT * D + 2 * K * P:NT * D + 2 * K * (P + TILES)].rearrange(
        "p (u k q) -> p u k q", u=2, k=K)
    B = carve(V["shared"], [("gated", (2, I)), ("h", (2, I)), ("ht", (2, D)), ("y", (D,))])
    gated, h, ht, y = (B[n] for n in ("gated", "h", "ht", "y"))
    bank = S["bank"]
    ps_t, ps_l = bank[0:2], bank[2]
    ps_cum, ps_all, ps_pair = bank[4], bank[5], bank[6]
    ps_row, ps_col = bank[4][:, 256:512], bank[6]
    ps_gu, ps_h, ps_y = bank[0:2], bank[3], bank[7]
    rt = S["rt"][:].rearrange("p (f e) -> p f e", f=DH)

    g = lambda n: S["sem"](f"ffn_{n}")
    x_in, var_ready, rstd_ready = g("x_in"), g("var_ready"), g("rstd_ready")
    xn_ready, xn_out = g("xn_ready"), g("xn_out")
    xt_ps, xt_ready, logit_ps = g("xt_ps"), g("xt_ready"), g("logit_ps")
    shifted_ready, exp_ready = g("shifted_ready"), g("exp_ready")
    members_ready, cum_ps = g("members_ready"), g("cum_ps")
    pos_ready, tile_ready, onehot_ready, pair_ps = g("pos_ready"), g("tile_ready"), g("onehot_ready"), g("pair_ps")
    col_ready, col_ps, later_ready, row_ps, pair_ready = (
        g("col_ready"), g("col_ps"), g("later_ready"), g("row_ps"), g("pair_ready"))
    step = g("route_step")
    sh_gu, sh_gated, sh_h, sh_turned, sh_ht, sh_down, sh_y, sh_added = (
        g("sh_gu"), g("sh_gated"), g("sh_h"), g("sh_turned"), g("sh_ht"), g("sh_down"), g("sh_y"), g("sh_added"))

    with nc.Block() as block:
        @block.sync
        def _(sp):
            out = S["xln_d"].rearrange("(j p) n -> j p n", p=P)
            for j in range(NT):
                sp.wait_ge(xn_ready, j + 1)
                sp.dma_start(out[j], xn[:, j, :]).then_inc(xn_out, 16)
            if tag == "a":
                for a, b in GROUPS[1:]:
                    load_experts(sp, S, d, a, b, S["weights_in"])
            sp.wait_ge(xn_out, 16 * NT)

        @block.vector
        def _(dve):
            n = [0]

            def then(ins):
                n[0] += 1
                ins.then_inc(step, 1)
                dve.wait_ge(step, n[0])

            layer_stats(dve, var_ready, st, x, x_in if tag == "a" else None, g("stat"))
            dve.wait_ge(rstd_ready, 1)
            for j in range(NT):
                dve.tensor_scalar(xn[:, j, :], x[:, j, :], st["mean"][:, j:j + 1], st["rstd"][:, j:j + 1],
                                  ALU.subtract, ALU.mult).then_inc(xn_ready, 1)
            dve.wait_ge(logit_ps, NT)
            then(dve.tensor_tensor(logits, ps_l[:, 0:NT * E].rearrange("p (j e) -> p j e", e=E),
                                   S["rb"][:].unsqueeze(1).broadcast_to([P, NT, E]), ALU.add))
            for j in range(NT):
                dve.max(top[:, j, :], logits[:, j, :]).then_inc(step, 1)
            n[0] += NT
            dve.wait_ge(step, n[0])
            dve.tensor_tensor(shifted, top[:, :, 0:K], top[:, :, 0:1].broadcast_to([P, NT, K]),
                              ALU.subtract).then_inc(shifted_ready, 1)
            for j in range(NT):
                dve.max_index(top_i[:, j, :], top[:, j, :], logits[:, j, :]).then_inc(step, 1)
            n[0] += NT
            dve.wait_ge(step, n[0])
            then(dve.tensor_copy(expert[:], top_i[:]))
            dve.wait_ge(xn_out, 16 * NT)
            then(dve.tensor_tensor(
                chosen, S["count"][:, 0:E].unsqueeze(1).unsqueeze(1).broadcast_to([P, NT, K, E]),
                expert[:, :, 0:K].unsqueeze(3).broadcast_to([P, NT, K, E]), ALU.is_equal))
            then(dve.tensor_reduce(V["members"], chosen.rearrange("p j k e -> p j e k"), AX_X, ALU.add))
            then(dve.memset(V["before"][:, 0, :], 0.0))
            for j in range(1, NT):
                then(dve.tensor_tensor(V["before"][:, j, :], V["before"][:, j - 1, :], V["members"][:, j - 1, :],
                                       ALU.add))
            dve.tensor_tensor(members_all, V["before"][:, NT - 1, :], V["members"][:, NT - 1, :],
                              ALU.add).then_inc(members_ready, 1)
            dve.wait_ge(exp_ready, 1)
            then(dve.tensor_reduce(total, exps, AX_X, ALU.add))
            then(dve.reciprocal(per, total))
            then(dve.scalar_tensor_tensor(out=S["mix"][:], in0=exps, scalar=0.5 * SCALE,
                                          in1=per.unsqueeze(2).broadcast_to([P, NT, K]), op0=ALU.mult, op1=ALU.mult))
            dve.wait_ge(cum_ps, 1)
            dve.tensor_scalar(counted_c, ps_all[0:E, E:E + 1], float(P - 1), None, ALU.add).then_inc(step, 1)
            n[0] += 1
            then(dve.tensor_scalar(counted, ps_all[:, 0:E], float(P - 1), None, ALU.add))
            dve.tensor_scalar(tiles_c, counted_c, 7, None, ALU.logical_shift_right).then_inc(step, 1)
            n[0] += 1
            then(dve.tensor_scalar(tiles_of, counted, 7, None, ALU.logical_shift_right))
            dve.tensor_copy(tiles_cf, tiles_c).then_inc(col_ready, 1)
            then(dve.tensor_copy(row_f[:, 0:E], tiles_of))
            then(dve.tensor_tensor_scan(tiles_end, S["ones"][:, 0:E], row_f[:, 0:E], 0.0, ALU.mult, ALU.add))
            then(dve.tensor_tensor(first_slot, tiles_end, row_f[:, 0:E], ALU.subtract))
            dve.wait_ge(cum_ps, 2)
            then(dve.scalar_tensor_tensor(out=V["slot_of"], in0=first_slot.unsqueeze(1).broadcast_to([P, NT, E]),
                                          scalar=float(P), in1=ps_cum[:, 0:NT * E].rearrange("p (j e) -> p j e", e=E),
                                          op0=ALU.mult, op1=ALU.add))
            then(dve.tensor_tensor(picked, chosen, V["slot_of"].unsqueeze(2).broadcast_to([P, NT, K, E]), ALU.mult))
            then(dve.tensor_reduce(V["slot"], V["picked"], AX_X, ALU.add))
            dve.wait_ge(col_ps, 1)
            dve.tensor_tensor(ended, S["count"][0:E, 0:TILES], ps_col[0:E, 0:1].broadcast_to([E, TILES]),
                              ALU.is_ge).then_inc(later_ready, 1)
            then(dve.tensor_copy(slot_int, V["slot"]))
            then(dve.tensor_scalar(tile_int, slot_int, 7, None, ALU.logical_shift_right))
            then(dve.tensor_scalar(pos_int, slot_int, P - 1, None, ALU.bitwise_and))
            then(dve.tensor_copy(V["slot_tile"], tile_int))
            then(dve.tensor_copy(V["slot_pos"], pos_int))
            at = lambda v, j: v.rearrange("p (j k) -> p j k", k=K)[:, j, :]
            for j in range(NT):
                u = j % 2
                if j >= 2:
                    dve.wait_ge(pair_ps, j - 1)
                dve.tensor_tensor(is_tile[:, u], S["count"][:, 0:TILES].unsqueeze(1).broadcast_to([P, K, TILES]),
                                  at(V["slot_tile"], j).unsqueeze(2).broadcast_to([P, K, TILES]),
                                  ALU.is_equal).then_inc(tile_ready, 1)
                dve.tensor_tensor(is_pos[:, u], S["count"][:].unsqueeze(1).broadcast_to([P, K, P]),
                                  at(V["slot_pos"], j).unsqueeze(2).broadcast_to([P, K, P]),
                                  ALU.is_equal).then_inc(pos_ready, 1)
            dve.wait_ge(row_ps, 1)
            dve.tensor_scalar(S["tile_expert"][:], ps_row[0:1, 0:TILES], float(E - 1), None, ALU.min)
            dve.wait_ge(pair_ps, NT)
            dve.tensor_copy(V["turn"][0:TILES, :], ps_pair[0:TILES, 0:P]).then_inc(pair_ready, 1)
            dve.wait_ge(pair_ps, NT + 1)
            pair = ps_row[:, P:P + TILES]
            then(dve.tensor_scalar(row_f, pair, -1.0, None, ALU.add))
            then(dve.tensor_scalar(empty, pair, 0.0, float(SKIP), ALU.is_equal, ALU.mult))
            then(dve.tensor_tensor(S["put"][:], row_f, empty, ALU.add))
            then(dve.tensor_scalar(S["take"][:], row_f, 0.0, None, ALU.max))
            then(dve.tensor_scalar(S["take"][:], S["take"][:], T - 1, None, ALU.bitwise_and))

        @block.gpsimd
        def _(pool):
            def shared(j):
                if j < NT:
                    pool.wait_ge(sh_gated, 2 * (j + 1))
                    pool.tensor_tensor(h[:, j % 2, :], h[:, j % 2, :], gated[:, j % 2, :], ALU.mult).then_inc(sh_h, 1)
                if j >= 2:
                    pool.wait_ge(sh_y, j - 1)
                    pool.tensor_tensor(x[:, j - 2, :], x[:, j - 2, :], y, ALU.add).then_inc(sh_added, 1)

            def pairs(j):
                pool.wait_ge(tile_ready, j + 1)
                pool.tensor_tensor(is_tile[:, j % 2], is_tile[:, j % 2],
                                   S["pair_row"][:, j, :].unsqueeze(2).broadcast_to([P, K, TILES]),
                                   ALU.mult).then_inc(onehot_ready, 1)

            for j in range(NT + 2):
                shared(j)
                for t in {5: (0, 1, 2, 3), 6: (4, 5), 7: (6, 7)}.get(j, ()):
                    pairs(t)

        @block.scalar
        def _(act):
            act.wait_ge(var_ready, 1)
            act.activation(st["rstd"], st["t6"], ACT.Sqrt).then_inc(rstd_ready, 1)
            for j in range(NT):
                act.wait_ge(xt_ps, j + 1)
                act.copy(xt[:, j, :], ps_t[j % 2][:, 0:D]).then_inc(xt_ready, 1)
            act.wait_ge(shifted_ready, 1)
            act.activation(exps, shifted, ACT.Exp).then_inc(exp_ready, 1)
            for j in range(NT + 2):
                if j < NT:
                    act.wait_ge(sh_gu, j + 1)
                    if j >= 2:
                        act.wait_ge(sh_h, j - 1)
                        act.wait_ge(sh_turned, j - 1)
                    act.activation(gated[:, j % 2, :], ps_gu[j % 2][:, 0:I], ACT.Silu).then_inc(sh_gated, 1)
                    act.copy(h[:, j % 2, :], ps_gu[j % 2][:, I:2 * I]).then_inc(sh_gated, 1)
                if 1 <= j <= NT:
                    act.wait_ge(sh_turned, j)
                    if j >= 3:
                        act.wait_ge(sh_down, j - 2)
                    act.copy(ht[:, (j - 1) % 2, 0:P], ps_h[:, 0:P]).then_inc(sh_ht, 1)
                    act.copy(ht[0:IR, (j - 1) % 2, P:D], ps_h[0:IR, P:D]).then_inc(sh_ht, 1)
                if j >= 2:
                    act.wait_ge(sh_down, j - 1)
                    if j >= 3:
                        act.wait_ge(sh_added, j - 2)
                    act.activation(y, ps_y[:, 0:D], ACT.Copy, scale=0.5).then_inc(sh_y, 1)

        @block.tensor
        def _(pe):
            def turn(j):
                u = j % 2
                pe.wait_ge(xn_ready, j + 1)
                if j >= 2:
                    pe.wait_ge(xt_ready, j - 1)
                for f in range(DH):
                    mm = pe.transpose(ps_t[u][:, f * P:(f + 1) * P], xn[:, j, f * P:(f + 1) * P], S["ident"][:])
                mm.then_inc(xt_ps, 1)

            def router(j):
                pe.wait_ge(xt_ready, j + 1)
                out = ps_l[:, j * E:(j + 1) * E]
                for f in range(DH):
                    mm = pe.matmul(out, xt[:, j, f * P:(f + 1) * P], rt[:, f, :], start=(f == 0), stop=(f == DH - 1))
                mm.then_inc(logit_ps, 1)

            warm_up(pe, S, ps_y, 12)
            turn(0)
            for j in range(NT):
                if j + 1 < NT:
                    turn(j + 1)
                router(j)

            def shared(j):
                if j < NT:
                    if j >= 2:
                        pe.wait_ge(sh_gated, 2 * (j - 1))
                    for f in range(DH):
                        mm = pe.matmul(ps_gu[j % 2][:, 0:2 * I], xt[:, j, f * P:(f + 1) * P],
                                       S["w_gu"][:, E, f * 2 * I:(f + 1) * 2 * I], start=(f == 0), stop=(f == DH - 1))
                    mm.then_inc(sh_gu, 1)
                if 1 <= j <= NT:
                    pe.wait_ge(sh_h, j)
                    if j >= 2:
                        pe.wait_ge(sh_ht, 2 * (j - 1))
                    pe.transpose(ps_h[:, 0:P], h[:, (j - 1) % 2, 0:P], S["ident"][:])
                    pe.transpose(ps_h[0:IR, P:D], h[:, (j - 1) % 2, P:I], S["ident"][:]).then_inc(sh_turned, 1)
                if j >= 2:
                    pe.wait_ge(sh_ht, 2 * (j - 1))
                    if j >= 3:
                        pe.wait_ge(sh_y, j - 2)
                    pe.matmul(ps_y[:, 0:D], ht[:, j % 2, 0:P], S["w_d1"][:, E, :], start=True, stop=False)
                    pe.matmul(ps_y[:, 0:D], ht[0:IR, j % 2, P:D], S["w_d2"][0:IR, E, :],
                              start=False, stop=True).then_inc(sh_down, 1)

            if tag == "a":
                pe.wait_ge(S["shared_in"], 16 * 3)
            pe.wait_ge(xt_ready, NT)
            for j in range(3):
                shared(j)
            pe.wait_ge(members_ready, 1)
            flat = lambda v: v.rearrange("p j e -> p (j e)")
            pe.matmul(ps_all[:, 0:E], S["ones"][:], members_all, start=True, stop=True)
            pe.matmul(ps_all[0:E, E:E + 1], members_all, S["ones"][:, 0:1], start=True, stop=True).then_inc(cum_ps, 1)
            pe.matmul(ps_cum[:, 0:NT * E], S["earlier"][:], flat(V["members"]), start=True, stop=False)
            pe.matmul(ps_cum[:, 0:NT * E], S["ones"][:], flat(V["before"]), start=False, stop=True).then_inc(cum_ps, 1)
            shared(3)
            pe.wait_ge(col_ready, 1)
            pe.matmul(ps_col[0:E, 0:1], S["earlier"][0:E, 0:E], tiles_cf, start=True, stop=False)
            pe.matmul(ps_col[0:E, 0:1], S["ident"][0:E, 0:E], tiles_cf, start=False, stop=True).then_inc(col_ps, 1)
            shared(4)
            shared(5)
            pe.wait_ge(later_ready, 1)
            pe.matmul(ps_row[0:1, 0:TILES], S["ones"][0:E, 0:1], ended, start=True, stop=True).then_inc(row_ps, 1)

            def pairs(j):
                u = j % 2
                pe.wait_ge(pos_ready, j + 1)
                pe.wait_ge(onehot_ready, j + 1)
                for k in range(K):
                    mm = pe.matmul(ps_pair[0:TILES, 0:P], is_tile[:, u, k, :], is_pos[:, u, k, :],
                                   start=(j == 0 and k == 0), stop=(j == NT - 1 and k == K - 1))
                mm.then_inc(pair_ps, 1)

            for j in range(6, NT + 2):
                pairs(2 * (j - 6))
                pairs(2 * (j - 6) + 1)
                shared(j)
            pe.wait_ge(pair_ready, 1)
            pe.transpose(ps_row[:, P:P + TILES], V["turn"][0:TILES, :],
                         S["ident"][0:TILES, 0:TILES]).then_inc(pair_ps, 1)


def expert_tiles(nc, S, tag):
    W = carve(S["work"][:, NT * D:], [
        ("xg", (4, D)), ("xt", (2, D)), ("gated", (2, I)), ("h", (2, I)), ("ht", (2, D)), ("y", (4, D)),
        ("take4", (4,)), ("put4", (4,))])
    xg, xt, gated, h, ht, y = (W[n] for n in ("xg", "xt", "gated", "h", "ht", "y"))
    take4, put4 = W["take4"].bitcast(I32), W["put4"].bitcast(I32)
    bank = S["bank"]
    ps_x, ps_gu, ps_h, ps_y = bank[0:2], bank[2:4], bank[4:6], bank[6:8]
    g = lambda n: S["sem"](f"ffn_{n}")
    x_in = [S["sem"](f"{tag}_xg_in{u}") for u in range(4)]
    y_out = [S["sem"](f"{tag}_y_out{u}") for u in range(4)]
    take_ready, put_ready = g("take_ready"), g("put_ready")
    x_ps, x_ready = g("x_ps"), g("x_ready")
    gu_ps, gated_ready, h_ready = g("gu_ps"), g("gated_ready"), g("h_ready")
    h_ps, ht_ready = g("h_ps"), g("ht_ready")
    y_ps, y_ready = g("y_ps"), g("y_ready")
    U, WARM, AHEAD, LAG = 8, 1, 5, 7
    RING = 4
    ROUNDS = (TILES - AHEAD) // U

    def steps(eng, step, last):
        for s in range(WARM * U):
            step(s // U, s % U)
        with eng.Fori(WARM, ROUNDS) as n:
            for u in range(U):
                step(n, u)
        for s in range(ROUNDS * U, last):
            step(s // U, s % U)

    def back(n, u, by):
        return (n, u - by) if u >= by else (n - 1, u - by + U)

    def ring_use(n, u):
        return n * (U // RING) + u // RING

    def is_tile(n, u, ahead=0):
        return not isinstance(n, int) or 0 <= n * U + u + ahead < TILES

    def from_tile(n, u, first):
        return not isinstance(n, int) or n * U + u >= first

    with nc.Block() as block:
        @block.gpsimd
        def _(pool):
            last_row = pool.to_reg(ROWS - 1)

            def gather(u):
                pool.indirect_dma_start(xg[:, u, :], None, S["xln_d"],
                                        bass.IndirectOffsetOnAxis(ap=take4[:, u:u + 1], axis=0)).then_inc(x_in[u], 16)

            def scatter(u):
                pool.indirect_dma_start(S["res_d"], bass.IndirectOffsetOnAxis(ap=put4[:, u:u + 1], axis=0),
                                        y[:, u, :], None, bounds_check=last_row,
                                        oob_is_err=False).then_inc(y_out[u], 16)

            def step(n, u):
                s = n * U + u
                v = (u - LAG) % RING
                if isinstance(n, int):
                    if is_tile(n, u):
                        pool.wait_ge(take_ready, s + 1)
                        gather(u % RING)
                    if from_tile(n, u, LAG):
                        pool.wait_ge(put_ready, s - LAG + 1)
                        scatter(v)
                    return
                take_at, put_at = pool.to_reg(s + 1), pool.to_reg(s - (LAG - 1))
                pool.wait_ge(take_ready, 1)
                pool.wait_ge(take_ready, take_at)
                gather(u % RING)
                pool.wait_ge(put_ready, 1)
                pool.wait_ge(put_ready, put_at)
                scatter(v)

            steps(pool, step, TILES + LAG)
            for u in range(4):
                pool.wait_ge(y_out[u], 16 * len(range(u, TILES, 4)))

        @block.vector
        def _(dve):
            def take_numbers(s, u):
                dve.tensor_copy(take4[:, u:u + 1], S["take"][:, bass.ds(s, 1)]).then_inc(take_ready, 1)

            for s in range(4):
                take_numbers(s, s)
            dve.wait_ge(x_ps, 1)
            take_numbers(4, 0)

            def step(n, u):
                s = n * U + u
                if is_tile(n, u):
                    dve.wait_ge(gated_ready, s + 1)
                    if from_tile(n, u, 2):
                        dve.wait_ge(h_ps, s - 1)
                    dve.tensor_tensor(h[:, u % 2, :], gated[:, u % 2, :], ps_gu[u % 2][:, I:2 * I],
                                      ALU.mult).then_inc(h_ready, 1)
                    if is_tile(n, u, AHEAD):
                        dve.wait_ge(x_ps, s + 2)
                        take_numbers(s + AHEAD, (u + 1) % RING)
                if from_tile(n, u, 2):
                    m, v = back(n, u, 2)
                    use, v = ring_use(m, v), v % RING
                    dve.wait_ge(y_ps, s - 1)
                    if from_tile(n, u, 6):
                        dve.wait_ge(y_out[v], use * 16)
                    dve.tensor_copy(y[:, v, :], ps_y[u % 2][:, 0:D]).then_inc(y_ready, 1)
                    dve.wait_ge(y_ready, s - 1)
                    dve.tensor_copy(put4[:, v:v + 1], S["put"][:, bass.ds(s - 2, 1)]).then_inc(put_ready, 1)

            steps(dve, step, TILES + 2)

        @block.scalar
        def _(act):
            def x_copy(s, n, u):
                act.wait_ge(x_ps, s + 1)
                if from_tile(n, u, 2):
                    act.wait_ge(gu_ps, s - 1)
                act.copy(xt[:, u % 2, :], ps_x[u % 2][:, 0:D]).then_inc(x_ready, 1)

            def step(n, u):
                s = n * U + u
                if is_tile(n, u):
                    act.wait_ge(gu_ps, s + 1)
                    if from_tile(n, u, 2):
                        act.wait_ge(h_ready, s - 1)
                    act.activation(gated[:, u % 2, :], ps_gu[u % 2][:, 0:I], ACT.Silu).then_inc(gated_ready, 1)
                if is_tile(n, u, 1):
                    x_copy(s + 1, n, u + 1)
                if is_tile(n, u, -1):
                    v = (u + 1) % 2
                    act.wait_ge(h_ps, s)
                    if from_tile(n, u, 3):
                        act.wait_ge(y_ps, s - 2)
                    act.copy(ht[:, v, 0:P], ps_h[v][:, 0:P]).then_inc(ht_ready, 1)
                    act.copy(ht[0:IR, v, P:D], ps_h[v][0:IR, P:D]).then_inc(ht_ready, 1)

            x_copy(0, 0, 0)
            steps(act, step, TILES + 1)

        @block.tensor
        def _(pe):
            def turn_x(s, n, u):
                pe.wait_ge(x_in[u % RING], ring_use(n, u) * 16 + 16)
                if from_tile(n, u, 2):
                    pe.wait_ge(x_ready, s - 1)
                for f in range(DH):
                    mm = pe.transpose(ps_x[u % 2][:, f * P:(f + 1) * P], xg[:, u % RING, f * P:(f + 1) * P],
                                      S["ident"][:])
                mm.then_inc(x_ps, 1)

            def gate_up(s, n, u, e):
                pe.wait_ge(x_ready, s + 1)
                if from_tile(n, u, 2):
                    pe.wait_ge(h_ready, s - 1)
                for f in range(DH):
                    mm = pe.matmul(ps_gu[u % 2][:, 0:2 * I], xt[:, u % 2, f * P:(f + 1) * P],
                                   S["w_gu"][:, bass.ds(e, 1), f * 2 * I:(f + 1) * 2 * I],
                                   start=(f == 0), stop=(f == DH - 1))
                mm.then_inc(gu_ps, 1)

            def turn_h(s, n, u):
                pe.wait_ge(h_ready, s + 1)
                if from_tile(n, u, 2):
                    pe.wait_ge(ht_ready, s * 2 - 2)
                pe.transpose(ps_h[u % 2][:, 0:P], h[:, u % 2, 0:P], S["ident"][:])
                pe.transpose(ps_h[u % 2][0:IR, P:D], h[:, u % 2, P:I], S["ident"][:]).then_inc(h_ps, 1)

            def down(s, n, u, e):
                pe.wait_ge(ht_ready, s * 2 + 2)
                if from_tile(n, u, 2):
                    pe.wait_ge(y_ready, s - 1)
                pe.matmul(ps_y[u % 2][:, 0:D], ht[:, u % 2, 0:P], S["w_d1"][:, bass.ds(e, 1), :],
                          start=True, stop=False)
                pe.matmul(ps_y[u % 2][:, 0:D], ht[0:IR, u % 2, P:D], S["w_d2"][0:IR, bass.ds(e, 1), :],
                          start=False, stop=True).then_inc(y_ps, 1)

            def expert_of(s):
                return pe.value_load(S["tile_expert"][0:1, bass.ds(s, 1)], min_val=0, max_val=E)

            def step(n, u):
                s = n * U + u
                if is_tile(n, u):
                    gate_up(s, n, u, expert_of(s))
                if is_tile(n, u, 1):
                    turn_x(s + 1, *((n, u + 1) if u + 1 < U else (n + 1, 0)))
                if is_tile(n, u, -1):
                    turn_h(s - 1, *back(n, u, 1))
                if is_tile(n, u, -2):
                    down(s - 2, *back(n, u, 2), expert_of(s - 2))

            warm_up(pe, S, ps_y[1], 8)
            if tag == "a":
                pe.wait_ge(S["weights_in"], 16 * 3 * len(GROUPS))
            turn_x(0, 0, 0)
            steps(pe, step, TILES + 2)


def combine(nc, S, tag, out_d):
    V = ffn_views(S)
    x = V["x"]
    BUF = 7
    rows = S["work"][:, NT * D:NT * D + BUF * K * D].rearrange("p (u k n) -> p u k n", u=BUF, k=K)
    res = S["res_d"].rearrange("(k j p) n -> j p k n", p=P, j=NT)
    out = out_d.rearrange("(j p) n -> j p n", p=P)
    rows_in = [S["sem"](f"ffn_rows_in{u}") for u in range(BUF)]
    added, stored = S["sem"]("ffn_added"), S["sem"]("ffn_stored")

    with nc.Block() as block:
        @block.sync
        def _(sp):
            for j in range(NT):
                if j >= BUF:
                    sp.wait_ge(added, 2 * K * ((j - BUF) // 2 + 1))
                sp.dma_start(rows[:, j % BUF, :, :], res[j]).then_inc(rows_in[j % BUF], 16)

        @block.scalar
        def _(act):
            for j in range(NT):
                act.wait_ge(added, 2 * K * (j // 2) + 2 * K - 1 + j % 2)
                act.dma_start(out[j], x[:, j, :]).then_inc(stored, 16)
            if tag == "b":
                act.wait_ge(stored, 16 * NT)

        @block.vector
        def _(dve):
            for j in range(0, NT, 2):
                for k in range(K):
                    for t in (j, j + 1):
                        if k:
                            dve.wait_ge(added, K * j + 2 * k - 1 + t - j)
                        else:
                            dve.wait_ge(rows_in[t % BUF], 16 * (t // BUF + 1))
                        dve.scalar_tensor_tensor(out=x[:, t, :], in0=rows[:, t % BUF, k, :],
                                                 scalar=S["mix"][:, t, k:k + 1], in1=x[:, t, :],
                                                 op0=ALU.mult, op1=ALU.add).then_inc(added, 1)


ATT = [("kt", (NC, 2 * C)), ("qt", (NC, 2 * C)), ("r", (NC, 2 * DK)), ("eta", (NC, 2))]
IN_HEADS = "p (h e) -> p h e"


def attention_inputs(nc, S, d):
    V = carve(S["work"], ATT + [
        ("w_kv", (DH, 2 * D)), ("w_q", (DH, D + 2 * H)), ("stat", (120,)), ("xn", (D,)), ("xt", (D,)),
        ("q", (D + H,)), ("gate", (D,)), ("eta_n", (NT * H,)), ("ss", (NT * H,))])
    R2 = carve(S["work"][:, 6272:], [
        ("w_row", (D,)), ("b_row", (D,)), ("tmp", (2 * D,)), ("rows_of", (CT * P,)), ("mean_r", (NT, H))])
    mean_r = R2["mean_r"]
    paired = [S["work"][:, at:at + D] for at in (8448, 8704, 9256, 9512)]
    rows_of = R2["rows_of"]
    kt, qt, q, gate = (V[n] for n in ("kt", "qt", "q", "gate"))
    w_kv, w_q, ss, eta_n = V["w_kv"], V["w_q"], V["ss"], V["eta_n"]
    w_g2, g1 = S["aux"][0:H, 0:D], S["aux"][0:H, D:D + P]
    tiles = lambda v: v.rearrange("p i n -> p (i n)").rearrange("p (j n) -> p j n", j=NT)
    x, v_nat = tiles(kt), tiles(V["r"])
    xn, xt = (V["xn"], tiles(qt)[:, NT - 1, :]), (V["xt"], v_nat[:, NT - 1, :])
    by_chunk = lambda t, j: t[:, j * CT:(j + 1) * CT, :].rearrange("p r (f c) -> p f r c", f=2)
    st = stat_views(V["stat"])
    bank = S["bank"]
    ps_t, ps_kv, ps_q, ps_g1, ps_gate, ps_sq = (bank[0], bank[7]), bank[1], bank[2], bank[3], bank[4], bank[5]
    ps_qt = bank[6]
    g = lambda n: S["sem"](f"att_{n}")
    w_in, var_ready, rstd_ready = g("w_in"), g("var_ready"), g("rstd_ready")
    xn_ready, xt_ps, xt_ready = g("xn_ready"), g("xt_ps"), g("xt_ready")
    g1_ps, g1_ready, q_ps, sig_ready, q_ready = g("g1_ps"), g("g1_ready"), g("q_ps"), g("sig_ready"), g("q_ready")
    kv_ps, kv_read, gate_ps, gate_ready = g("kv_ps"), g("kv_read"), g("gate_ps"), g("gate_ready")
    qt_ps, qt_ready, v_ready = g("qt_ps"), g("qt_ready"), g("v_ready")
    q_out, gate_out = g("q_out"), g("gate_out")

    with nc.Block() as block:
        @block.sync
        def _(sp):
            sp.dma_start(w_kv[:], d["w_kv"]).then_inc(w_in, 16)
            sp.dma_start(w_q[:], d["w_q"]).then_inc(w_in, 16)
            sp.dma_start(w_g2, d["w_g2"]).then_inc(w_in, 16)
            sp.wait_ge(w_in, 48)
            q_rows = S["q_d"].rearrange("(j p) n -> j p n", p=P)
            gate_rows = S["gate_d"].rearrange("(j p) n -> j p n", p=P)
            for j in range(NT):
                sp.wait_ge(q_ready, 2 * (j + 1))
                sp.dma_start(q_rows[j], q[:, 0:D]).then_inc(q_out, 16)
                sp.wait_ge(gate_ready, j + 1)
                sp.dma_start(gate_rows[j], gate[:]).then_inc(gate_out, 16)
            sp.wait_ge(q_out, 16 * NT)
            sp.wait_ge(gate_out, 16 * NT)

        @block.vector
        def _(dve):
            layer_stats(dve, var_ready, st, x, None, g("stat"))
            dve.wait_ge(rstd_ready, 1)
            def normalize(j):
                if j >= 2:
                    dve.wait_ge(xt_ps, j - 1)
                dve.tensor_scalar(xn[j % 2], x[:, j, :], st["mean"][:, j:j + 1], st["rstd"][:, j:j + 1],
                                  ALU.subtract, ALU.mult).then_inc(xn_ready, 1)

            normalize(0)
            for j in range(NT):
                if j + 1 < NT:
                    normalize(j + 1)
                dve.wait_ge(sig_ready, j + 1)
                dve.tensor_tensor(q[:, 0:D], q[:, 0:D], ps_q[:, 0:D], ALU.mult).then_inc(q_ready, 1)
                dve.tensor_scalar(eta_n[:, j * H:(j + 1) * H], q[:, D:D + H], 2.0, None, ALU.mult).then_inc(q_ready, 1)
                dve.wait_ge(kv_read, j + 1)
                dve.tensor_reduce(ss[:, j * H:(j + 1) * H], ps_sq[:, 0:D].rearrange(IN_HEADS, e=DK), AX_X,
                                  ALU.add).then_inc(v_ready, 1)
                dve.tensor_copy(v_nat[:, j, :], ps_kv[:, D:2 * D]).then_inc(v_ready, 1)

        @block.scalar
        def _(act):
            act.wait_ge(var_ready, 1)
            act.activation(st["rstd"], st["t6"], ACT.Sqrt).then_inc(rstd_ready, 1)
            act.wait_ge(S["sem"]("ffn_stored"), 16 * NT)

            def x_copy(j):
                act.wait_ge(xt_ps, j + 1)
                if j >= 2:
                    act.wait_ge(kv_ps, j - 1)
                act.copy(xt[j % 2], ps_t[j % 2][:, 0:D]).then_inc(xt_ready, 1)

            x_copy(0)
            for j in range(NT):
                act.wait_ge(g1_ps, j + 1)
                if j:
                    act.wait_ge(gate_ps, j)
                act.copy(g1, ps_g1[IR:IR + H, 0:P]).then_inc(g1_ready, 1)
                act.wait_ge(q_ps, j + 1)
                if j:
                    act.wait_ge(q_out, 16 * j)
                    act.wait_ge(qt_ps, j)
                    act.wait_ge(q_ready, 2 * j)
                act.activation(q[:, 0:D + H], ps_q[:, 0:D + H], ACT.Sigmoid).then_inc(sig_ready, 1)
                if j + 1 < NT:
                    x_copy(j + 1)
                act.wait_ge(kv_ps, j + 1)
                if j:
                    act.wait_ge(v_ready, 2 * j)
                act.copy(x[:, j, :], ps_kv[:, 0:D])
                act.activation(ps_sq[:, 0:D], ps_kv[:, 0:D], ACT.Square).then_inc(kv_read, 1)
                act.wait_ge(gate_ps, j + 1)
                if j:
                    act.wait_ge(gate_out, 16 * j)
                act.activation(gate[:], ps_gate[:, 0:D], ACT.Sigmoid).then_inc(gate_ready, 1)
                act.wait_ge(qt_ps, j + 1)
                act.copy(by_chunk(qt, j), ps_qt[:, 0:D].rearrange("p (f r c) -> p f r c", f=2, r=CT)
                         ).then_inc(qt_ready, 1)

        @block.tensor
        def _(pe):
            warm_up(pe, S, ps_gate, 10)
            pe.wait_ge(w_in, 48)

            def turn(j):
                pe.wait_ge(xn_ready, j + 1)
                if j >= 2:
                    pe.wait_ge(xt_ready, j - 1)
                for f in range(DH):
                    mm = pe.transpose(ps_t[j % 2][:, f * P:(f + 1) * P], xn[j % 2][:, f * P:(f + 1) * P], S["ident"][:])
                mm.then_inc(xt_ps, 1)

            turn(0)
            for j in range(NT):
                x_t = xt[j % 2]
                pe.wait_ge(xt_ready, j + 1)
                if j:
                    pe.wait_ge(g1_ready, j)
                for f in range(DH):
                    mm = pe.matmul(ps_g1[IR:IR + H, 0:P], w_q[:, f, D + H:D + 2 * H], x_t[:, f * P:(f + 1) * P],
                                   start=(f == 0), stop=(f == DH - 1))
                mm.then_inc(g1_ps, 1)
                if j:
                    pe.wait_ge(q_ready, 2 * j)
                for f in range(DH):
                    mm = pe.matmul(ps_q[:, 0:D + H], x_t[:, f * P:(f + 1) * P], w_q[:, f, 0:D + H],
                                   start=(f == 0), stop=(f == DH - 1))
                mm.then_inc(q_ps, 1)
                if j + 1 < NT:
                    turn(j + 1)
                if j:
                    pe.wait_ge(v_ready, 2 * j)
                for f in range(DH):
                    mm = pe.matmul(ps_kv[:, 0:2 * D], x_t[:, f * P:(f + 1) * P], w_kv[:, f, :],
                                   start=(f == 0), stop=(f == DH - 1))
                mm.then_inc(kv_ps, 1)
                pe.wait_ge(g1_ready, j + 1)
                if j:
                    pe.wait_ge(gate_ready, j)
                pe.matmul(ps_gate[:, 0:D], g1, w_g2, start=True, stop=True).then_inc(gate_ps, 1)
                pe.wait_ge(q_ready, 2 * (j + 1))
                if j:
                    pe.wait_ge(qt_ready, j)
                for f in range(DH):
                    mm = pe.transpose(ps_qt[:, f * P:(f + 1) * P], q[:, f * P:(f + 1) * P], S["ident"][:])
                mm.then_inc(qt_ps, 1)

    kn, z, w_row, b_row = x, v_nat, R2["w_row"], R2["b_row"]
    rows_ready, summed, mean_ready = g("rows_ready"), g("summed"), g("mean_ready")
    row_in, ss_ready, norm_ready = g("row_in"), g("ss_ready"), g("norm_ready")
    kn_ready, kt_ps, kt_ready, z_ready, zw_ready = g("kn_ready"), g("kt_ps"), g("kt_ready"), g("z_ready"), g("zw_ready")
    r_ready, r_out = g("r_ready"), [g(f"r_out{u}") for u in range(4)]
    eta_ps, step, w_step = g("eta_ps"), g("step"), g("w_step")
    ps_e = bank[2:4]
    with nc.Block() as block:
        @block.sync
        def _(sp):
            sp.dma_start(w_row, d["ln_w_row"].broadcast_to([P, D])).then_inc(row_in, 16)
            sp.dma_start(b_row, d["ln_b_row"].broadcast_to([P, D])).then_inc(row_in, 16)
            rows = S["r_d"].rearrange("(j p) n -> j p n", p=P)
            for j in range(NT):
                sp.wait_ge(r_ready, j + 1)
                sp.dma_start(rows[j], paired[j % 4]).then_inc(r_out[j % 4], 16)
            for u in range(4):
                sp.wait_ge(r_out[u], 16 * NT // 4)

        @block.vector
        def _(dve):
            n = [0]

            def then(ins):
                n[0] += 1
                ins.then_inc(step, 1)
                dve.wait_ge(step, n[0])

            dve.tensor_copy(rows_of.rearrange("p (r h c) -> p r h c", h=HH, c=C),
                            S["ident"][:].rearrange("p (r c) -> p r c", c=C).unsqueeze(2).broadcast_to([P, CT, HH, C])
                            ).then_inc(rows_ready, 1)
            then(dve.tensor_scalar(ss, ss, EPS, None, ALU.add))
            dve.reciprocal(ss, ss).then_inc(ss_ready, 1)
            dve.wait_ge(norm_ready, 1)
            for j in range(NT):
                dve.tensor_tensor(kn[:, j].rearrange(IN_HEADS, e=DK), x[:, j, :].rearrange(IN_HEADS, e=DK),
                                  ss[:, j * H:(j + 1) * H].unsqueeze(2).broadcast_to([P, H, DK]),
                                  ALU.mult).then_inc(kn_ready, 1)
                if j:
                    dve.wait_ge(kn_ready, j)
                    dve.tensor_tensor(z[:, j - 1], v_nat[:, j - 1, :], kn[:, j - 1], ALU.subtract).then_inc(z_ready, 1)
            dve.wait_ge(kn_ready, NT)
            dve.tensor_tensor(z[:, NT - 1], v_nat[:, NT - 1, :], kn[:, NT - 1], ALU.subtract).then_inc(z_ready, 1)
            tmp = R2["tmp"].rearrange("p (n f h) -> p n f h", f=2, h=HH)
            dve.wait_ge(eta_ps, 1)
            own = S["same_head"][:].rearrange("p (h c) -> p h c", c=C)[:, :, 0]
            for b in range(2):
                then(dve.tensor_tensor(tmp, ps_e[b][:].rearrange("p (n f h) -> p n f h", f=2, h=HH),
                                       own.unsqueeze(1).unsqueeze(1).broadcast_to([P, 4 * NT, 2, HH]), ALU.mult))
                for r in range(4):
                    dst = V["eta"].rearrange("p (j r) f -> p r j f", r=CT)[:, 4 * b + r]
                    dve.tensor_reduce(dst, tmp[:, r * NT:(r + 1) * NT], AX_X, ALU.add).then_inc(step, 1)
                    n[0] += 1
                dve.wait_ge(step, n[0])
            for j in range(NT + 2):
                if j < NT:
                    dve.wait_ge(zw_ready, j + 1)
                    dve.tensor_reduce(mean_r[:, j, :], z[:, j].rearrange(IN_HEADS, e=DK), AX_X,
                                      ALU.add).then_inc(summed, 1)
                if 1 <= j <= NT:
                    dve.wait_ge(summed, j)
                    dve.tensor_scalar(mean_r[:, j - 1, :], mean_r[:, j - 1, :], 1.0 / DK, None,
                                      ALU.mult).then_inc(mean_ready, 1)
                if j >= 2:
                    t = j - 2
                    if t >= 4:
                        dve.wait_ge(r_out[t % 4], 16)
                    dve.wait_ge(mean_ready, t + 1)
                    dve.tensor_tensor(
                        paired[t % 4].rearrange("p (h f e) -> p f h e", f=2, e=DK),
                        z[:, t].rearrange("p (f h e) -> p f h e", f=2, e=DK),
                        mean_r[:, t, :].rearrange("p (f h) -> p f h", f=2).unsqueeze(3).broadcast_to([P, 2, HH, DK]),
                        ALU.subtract).then_inc(r_ready, 1)

        @block.gpsimd
        def _(pool):
            pool.wait_ge(row_in, 32)
            for j in range(NT):
                pool.wait_ge(z_ready, j + 1)
                pool.tensor_tensor(z[:, j], z[:, j], b_row, ALU.subtract).then_inc(w_step, 1)
                pool.wait_ge(w_step, j + 1)
                pool.tensor_tensor(z[:, j], z[:, j], w_row, ALU.mult).then_inc(zw_ready, 1)

        @block.scalar
        def _(act):
            act.wait_ge(ss_ready, 1)
            act.activation(ss, ss, ACT.Sqrt).then_inc(norm_ready, 1)
            for j in range(NT):
                act.wait_ge(kt_ps, j + 1)
                act.copy(by_chunk(kt, j), bank[j % 2][:, 0:D].rearrange("p (f r c) -> p f r c", f=2, r=CT)
                         ).then_inc(kt_ready, 1)

        @block.tensor
        def _(pe):
            pe.wait_ge(rows_ready, 1)
            for r in range(CT):
                mm = pe.matmul(ps_e[r // 4][:, (r % 4) * P:(r % 4 + 1) * P],
                               rows_of[:, r * P:(r + 1) * P], eta_n,
                               start=True, stop=True)
            mm.then_inc(eta_ps, 1)
            for j in range(NT):
                pe.wait_ge(kn_ready, j + 1)
                pe.wait_ge(z_ready, j + 1)
                if j >= 2:
                    pe.wait_ge(kt_ready, j - 1)
                for f in range(DH):
                    mm = pe.transpose(bank[j % 2][:, f * P:(f + 1) * P], kn[:, j, f * P:(f + 1) * P], S["ident"][:])
                mm.then_inc(kt_ps, 1)


PAIR = 2 * DK


def qh_rows(S, h, j):
    return S["qh_d"].rearrange("(j i c) (h n) -> h j c i n", j=NT, c=C, n=PAIR)[h, j]


def outputs(r, h, j):
    return r[h * C:(h + 1) * C, j * CT:(j + 1) * CT, :]


def scan(nc, S, d, x1_d):
    B = 2 * C
    V = carve(S["work"], ATT + [
        ("q_k", (2, 4 * B)), ("kq_bd", (2, 2 * B)), ("k_back", (2, 2 * B)), ("products", (2, 4 * B)),
        ("state", (2 * DK,)), ("one_a", (2, 2 * DK)), ("terms", (2, 5 * (DK + 1))),
        ("sums", (2, 6)), ("rho", (2,)), ("by_rho", (2, 6)), ("root", (2,)), ("rate", (2,)),
        ("u", (2, DK)), ("w", (2, DK)), ("xx", (2, 2 * DK)), ("e", (2, DK)), ("f", (2, DK)), ("y", (2, DK)),
        ("v", (2, 2 * DK)), ("zero", (2 * DK,)), ("gate", (NT, D))])
    S["gate"] = V["gate"]
    kt, qt, r, eta = (V[n] for n in ("kt", "qt", "r", "eta"))
    halves = lambda t: t.rearrange("p (f n) -> p f n", f=2)
    terms = V["terms"].rearrange("p f (g e) -> p f g e", g=5)
    one_a = V["one_a"].rearrange("p f (g e) -> p f g e", g=2)
    xx = V["xx"].rearrange("p f (g e) -> p f g e", g=2)
    state, kq_bd, v = (V[n] for n in ("state", "kq_bd", "v"))
    q_k = V["q_k"].rearrange("p u (f n) -> p u f n", f=2)
    k_bd = lambda u: q_k[:, 1 - u, :, B:2 * B]
    q_bd = lambda u: q_k[:, u, :, 0:B]
    k_back = lambda u: halves(V["k_back"][:, u])
    products = V["products"].rearrange("p u (f n) -> p u f n", f=2)
    bank = S["bank"]
    ps_kh, ps_s, ps_prep, ps_o = (bank[0], bank[6]), bank[1], bank[2:4], bank[4:6]
    g = lambda n: S["sem"](f"scan_{n}")
    r_first, r_rest, a_in, setup, zeroed = g("r_first"), g("r_rest"), g("a_in"), g("setup"), g("zeroed")
    k_ready, q_ready, kq_ready = g("k_bd_ready"), g("q_bd_ready"), g("kq_bd_ready")
    prep_ps, products_ready, k_back_ready = g("prep_ps"), g("products_ready"), g("k_back_ready")
    state_ready, kh_ps, rho_ready, root_ready, v_ready = (
        g("state_ready"), g("kh_ps"), g("rho_ready"), g("root_ready"), g("v_ready"))
    s_ps, qs_ps, o_ps, o_ready, step = g("s_ps"), g("qs_ps"), g("o_ps"), g("o_ready"), g("step")

    o_out, loaded_back = g("o_out"), S["back"]
    tiles = lambda t: t.rearrange("p i n -> p (i n)").rearrange("p (j n) -> p j n", j=NT)
    later = lambda i: not isinstance(i, int)
    chunk = lambda t, i: t[:, bass.ds(i, 1), :].rearrange("p a (f c) -> p (a f) c", f=2)

    with nc.Block() as block:
        @block.sync
        def _(sp):
            src = S["r_d"].rearrange("(i c) (h n) -> h c i n", c=C, n=PAIR)
            w = d["ln_w"]
            for f in range(2):
                sp.dma_start(one_a[:, f, 1, :], w[f * HH:(f + 1) * HH, :].unsqueeze(1).broadcast_to([HH, C, DK])
                             ).then_inc(a_in, 16)
            for part, loaded in ((slice(0, CT), r_first), (slice(CT, NC), r_rest)):
                for h in range(HH):
                    sp.dma_start(r[h * C:(h + 1) * C, part, :], src[h][:, part, :]).then_inc(loaded, 16)
            sp.dma_start(V["gate"], by_tile(S["gate_d"])).then_inc(loaded_back, 16)
            rows = lambda t: t.rearrange("(j p) n -> j p n", p=P)
            for j in range(NT - 1):
                sp.wait_ge(o_ready, CT * (j + 1))
                for h in range(HH):
                    sp.dma_start(qh_rows(S, h, j), outputs(r, h, j)).then_inc(o_out, 16)
                sp.wait_ge(o_out, 16 * HH * (j + 1))
                sp.dma_start(tiles(kt)[:, j, :], rows(S["qh_d"])[j]).then_inc(loaded_back, 16)
                sp.dma_start(tiles(qt)[:, j, :], rows(S["q_d"])[j]).then_inc(loaded_back, 16)
                sp.dma_start(tiles(r)[:, j, :], rows(x1_d)[j]).then_inc(loaded_back, 16)
            sp.wait_ge(loaded_back, 16 * (1 + 3 * (NT - 1)))

        @block.gpsimd
        def _(pool):
            pairs = lambda t: t.rearrange("p (f h c) -> p f h c", f=2, h=2)
            mask = lambda m: m[:].rearrange("p (h c) -> p h c", h=2).unsqueeze(1).broadcast_to([P, 2, 2, C])
            wide = lambda t: t.unsqueeze(2).broadcast_to([P, 2, 2, C])

            two_heads = lambda t: t.rearrange("p f (h c) -> p f h c", h=2)

            def spread_k(i, u):
                pool.tensor_tensor(two_heads(k_bd(u)), wide(chunk(kt, i)), mask(S["own_head"]),
                                   ALU.mult).then_inc(k_ready, 1)

            def spread_q(i, u):
                pool.tensor_tensor(two_heads(q_bd(u)), wide(chunk(qt, i)), mask(S["own_head"]),
                                   ALU.mult).then_inc(q_ready, 1)

            def cut(i, u):
                pool.wait_ge(products_ready, i + 1)
                if later(i) or i >= 2:
                    pool.wait_ge(o_ps, i - 1)
                pool.tensor_tensor(halves(kq_bd[:, u]), products[:, u, :, 0:B],
                                   S["causal"][:].unsqueeze(1).broadcast_to([P, 2, B]),
                                   ALU.mult).then_inc(kq_ready, 1)

            def body(m, u):
                pool.wait_ge(qs_ps, m)
                pool.wait_ge(k_back_ready, m * 2 + 2)
                spread_k(m + 2, u)
                spread_q(m + 1, 1 - u)
                cut(m, u)

            spread_k(0, 0)
            spread_k(1, 1)
            spread_q(0, 0)
            pool.wait_ge(prep_ps, 1)
            pool.wait_ge(k_back_ready, 2)
            spread_k(2, 0)
            spread_q(1, 1)
            cut(0, 0)
            body(1, 1)
            with pool.Fori(1, NC // 2 - 1) as n:
                body(n * 2, 0)
                body(n * 2 + 1, 1)
            pool.wait_ge(qs_ps, NC - 2)
            spread_q(NC - 1, 1)
            cut(NC - 2, 0)
            cut(NC - 1, 1)

        @block.scalar
        def _(act):
            act.wait_ge(a_in, 32)
            act.activation(one_a[:, :, 0, :], one_a[:, :, 1, :], ACT.Square).then_inc(setup, 1)

            def prepared(i, u):
                act.wait_ge(prep_ps, i + 1)
                if later(i) or i >= 2:
                    act.wait_ge(kh_ps, i)
                    act.wait_ge(kq_ready, i - 1)
                act.copy(V["products"][:, u], ps_prep[u][:, 0:4 * B]).then_inc(products_ready, 1)

            def output(i, u):
                act.wait_ge(o_ps, i + 1)
                act.copy(r[:, bass.ds(i, 1), :].rearrange("p a n -> p (a n)"),
                         ps_o[u][:, 0:2 * DK]).then_inc(o_ready, 1)

            def root(i):
                act.wait_ge(rho_ready, i + 1)
                act.activation(V["root"], V["rho"], ACT.Sqrt, scale=float(DK)).then_inc(root_ready, 1)

            def body(i, u, more=True):
                act.wait_ge(s_ps, i)
                act.copy(state, ps_s[:, 0:2 * DK]).then_inc(state_ready, 1)
                root(i)
                output(i - 1, 1 - u)
                if more:
                    prepared(i + 1, 1 - u)

            prepared(0, 0)
            root(0)
            prepared(1, 1)
            body(1, 1)
            with act.Fori(1, NC // 2 - 1) as n:
                body(n * 2, 0)
                body(n * 2 + 1, 1)
            body(NC - 2, 0)
            body(NC - 1, 1, False)
            output(NC - 1, 1)

        @block.tensor
        def _(pe):
            at = lambda n: pe.to_reg(n) if later(n) else n

            def blocks(out, lhs, rhs, start, stop):
                for f in range(2):
                    for b in range(0, P, B):
                        q = slice(b, b + B)
                        mm = pe.matmul(out[q, f], lhs[q, f], rhs[q, f],
                                       start=start and f == 0, stop=stop and f == 1, skip_group_check=True,
                                       tile_position=(b, b))
                return mm

            def prepare(i, u, next_k=True):
                k_at, q_at, read = at(i + 2), at(i + 1), at(i - 1)
                pe.wait_ge(zeroed, 1)
                if next_k:
                    pe.wait_ge(k_ready, k_at)
                pe.wait_ge(q_ready, q_at)
                if later(i) or i >= 2:
                    pe.wait_ge(products_ready, read)
                blocks(halves(ps_prep[u][:, 0:4 * B]), k_bd(u), q_k[:, u], True, True).then_inc(prep_ps, 1)

            def with_state(i, u, more=True):
                done, left = at(i + 1), at(i - 1)
                pe.wait_ge(zeroed, 1)
                pe.wait_ge(state_ready, done)
                if later(i) or i >= 2:
                    pe.wait_ge(o_ready, left)
                if more:
                    blocks(halves(ps_kh[1 - u][:, 0:2 * DK]), k_bd(1 - u), halves(state), True, False)
                blocks(halves(ps_o[u][:, 0:2 * DK]), q_bd(u), halves(state), True, False).then_inc(qs_ps, 1)

            def finish(i, u):
                done = at(i + 1)
                pe.wait_ge(zeroed, 1)
                pe.wait_ge(v_ready, done)
                pe.wait_ge(kq_ready, done)
                blocks(halves(ps_o[u][:, 0:2 * DK]), halves(kq_bd[:, u]), halves(v[:, u]),
                       False, True).then_inc(o_ps, 1)

            def body(i, u):
                now, both = at(i), at(i * 2)
                pe.wait_ge(zeroed, 1)
                pe.wait_ge(v_ready, now)
                pe.wait_ge(products_ready, now)
                last = halves(v[:, 1 - u])
                blocks(halves(ps_kh[u][:, 0:2 * DK]), products[:, 1 - u, :, B:2 * B], last,
                       False, True).then_inc(kh_ps, 1)
                pe.wait_ge(zeroed, 1)
                pe.wait_ge(k_back_ready, both)
                blocks(halves(ps_s[:, 0:2 * DK]), k_back(1 - u), last, False, False).then_inc(s_ps, 1)
                finish(i - 1, 1 - u)

            pe.wait_ge(zeroed, 1)
            pe.matmul(ps_s[:, 0:2 * DK], S["ident"][:], V["zero"], start=True, stop=False, skip_group_check=True)
            pe.wait_ge(k_ready, 1)
            pe.wait_ge(state_ready, 1)
            blocks(halves(ps_kh[0][:, 0:2 * DK]), k_bd(0), halves(state), True, True).then_inc(kh_ps, 1)
            prepare(0, 0)
            prepare(1, 1)
            with_state(0, 0)
            body(1, 1)
            prepare(2, 0)
            with_state(1, 1)
            with pe.Fori(1, NC // 2 - 1) as n:
                for u in range(2):
                    body(n * 2 + u, u)
                    prepare(n * 2 + (u + 1), 1 - u)
                    with_state(n * 2 + u, u)
            body(NC - 2, 0)
            prepare(NC - 1, 1, False)
            with_state(NC - 2, 0)
            body(NC - 1, 1)
            with_state(NC - 1, 1, False)
            finish(NC - 1, 1)

        @block.vector
        def _(dve):
            f2 = lambda t: t.unsqueeze(2).broadcast_to([P, 2, DK])
            dve.memset(state, 0.0).then_inc(state_ready, 1)
            dve.memset(V["zero"], 0.0).then_inc(zeroed, 1)
            dve.memset(V["terms"], 0.0).then_inc(step, 1)
            dve.wait_ge(step, 1)
            dve.memset(terms[:, :, 3, DK:DK + 1], float(DK) * EPS).then_inc(step, 1)
            dve.wait_ge(setup, 1)
            dve.tensor_scalar(one_a[:, :, 1, :], one_a[:, :, 0, :], float(DK), None, ALU.mult).then_inc(step, 1)
            dve.wait_ge(step, 3)
            dve.memset(one_a[:, :, 0, :], 1.0).then_inc(step, 1)
            dve.wait_ge(step, 4)
            dve.wait_ge(r_first, 16 * HH)
            base, OPS = 4, 14

            def turn_k(i, u):
                dve.wait_ge(k_ready, i + 1)
                if later(i) or i >= 2:
                    dve.wait_ge(s_ps, i - 1)
                for f in range(2):
                    dve.transpose(k_back(u)[:, f], k_bd(u)[:, f]).then_inc(k_back_ready, 1)

            def body(i, u, more=True):
                def upto(n):
                    dve.wait_ge(step, i * OPS + (base + n))

                eta_i = eta[:, bass.ds(i, 1), :].rearrange("p a f -> p (a f)")
                r_i = chunk(r, i)
                x_ps = halves(ps_kh[u][:, 0:2 * DK])
                x = terms[:, :, 0, 0:DK]
                sums, rho, by_rho, u_, w = V["sums"], V["rho"], V["by_rho"], V["u"], V["w"]
                dve.tensor_copy(sums[:, :, 5], eta_i).then_inc(step, 1)
                dve.wait_ge(kh_ps, i + 1)
                dve.tensor_tensor(terms[:, :, 0:2, 0:DK], x_ps.unsqueeze(2).broadcast_to([P, 2, 2, DK]),
                                  one_a, ALU.mult).then_inc(step, 1)
                dve.tensor_tensor(terms[:, :, 2, 0:DK], x_ps, r_i, ALU.mult).then_inc(step, 1)
                upto(2)
                dve.tensor_tensor(terms[:, :, 3:5, 0:DK], terms[:, :, 0:2, 0:DK],
                                  x.unsqueeze(2).broadcast_to([P, 2, 2, DK]), ALU.mult).then_inc(step, 1)
                upto(4)
                dve.tensor_reduce(sums[:, :, 0:4], terms[:, :, 1:5, :], AX_X, ALU.add).then_inc(step, 1)
                upto(5)
                dve.reciprocal(rho, sums[:, :, 2]).then_inc(rho_ready, 1)
                dve.scalar_tensor_tensor(out=u_, in0=f2(sums[:, :, 0]), scalar=1.0 / DK, in1=terms[:, :, 1, 0:DK],
                                         op0=ALU.mult, op1=ALU.subtract).then_inc(step, 1)
                dve.wait_ge(rho_ready, i + 1)
                dve.tensor_tensor(by_rho[:, :, 0:5:2], sums[:, :, 1:6:2], rho.unsqueeze(2).broadcast_to([P, 2, 3]),
                                  ALU.mult).then_inc(step, 1)
                upto(7)
                dve.tensor_tensor(by_rho[:, :, 1], by_rho[:, :, 2], by_rho[:, :, 4], ALU.mult).then_inc(step, 1)
                dve.tensor_tensor(w, u_, f2(by_rho[:, :, 4]), ALU.mult).then_inc(step, 1)
                upto(8)
                dve.tensor_tensor(xx, x.unsqueeze(2).broadcast_to([P, 2, 2, DK]),
                                  by_rho[:, :, 0:2].unsqueeze(3).broadcast_to([P, 2, 2, DK]),
                                  ALU.mult).then_inc(step, 1)
                dve.wait_ge(root_ready, i + 1)
                dve.scalar_tensor_tensor(out=V["rate"], in0=V["root"], scalar=-1.0, in1=eta_i, op0=ALU.mult,
                                         op1=ALU.mult).then_inc(step, 1)
                upto(10)
                dve.tensor_tensor(V["e"], xx[:, :, 0], r_i, ALU.subtract).then_inc(step, 1)
                dve.tensor_tensor(V["f"], xx[:, :, 1], w, ALU.add).then_inc(step, 1)
                upto(12)
                dve.tensor_tensor(V["y"], V["e"], f2(V["rate"]), ALU.mult).then_inc(step, 1)
                upto(14)
                dve.tensor_tensor(halves(v[:, u]), V["y"], V["f"], ALU.add).then_inc(v_ready, 1)
                if more:
                    turn_k(i + 1, 1 - u)

            turn_k(0, 0)
            body(0, 0)
            body(1, 1)
            dve.wait_ge(r_rest, 16 * HH)
            with dve.Fori(1, NC // 2 - 1) as n:
                body(n * 2, 0)
                body(n * 2 + 1, 1)
            body(NC - 2, 0)
            body(NC - 1, 1, False)


GROUPS_OUT = ((0, 1, 2, 3), (4, 5, 6), (7,))
POOL_GATES = 3


def attention_output(nc, S, d, x1_d):
    V = carve(S["work"], [
        ("qh", (NT, D)), ("q", (NT, D)), ("r", (NC, 2 * DK)), ("w_o", (DH, D)), ("w_row", (D,)),
        ("b_row", (D,)), ("norm", (DH,)), ("ss", (NT * H,)), ("mean", (NT * H,))])
    qh, q, r, w_o, ss, mean = (V[n] for n in ("qh", "q", "r", "w_o", "ss", "mean"))
    gate = S["gate"]
    x1 = r.rearrange("p i n -> p (i n)").rearrange("p (j n) -> p j n", j=NT)
    turned = q
    bank = S["bank"]
    g = lambda n: S["sem"](f"out_{n}")
    o_out, row_in, q_in, qh_in, x1_in = g("o_out"), g("row_in"), g("q_in"), g("qh_in"), g("x1_in")
    centred, sq_ps, ss_done = g("centred"), g("sq_ps"), g("ss_done")
    var_ready, rstd_ready = g("var_ready"), g("rstd_ready")
    scaled, b_done, w_done, gated, ot_ps, ot_ready, y_ps = (
        g("scaled"), g("b_done"), g("w_done"), g("gated"), g("ot_ps"), g("ot_ready"), g("y_ps"))
    step, unit, w_in = g("step"), g("unit"), g("w_in")
    added_pool, gated_pool = g("added_pool"), g("gated_pool")
    pairs = lambda t: t.rearrange("p (h f e) -> p h f e", f=2, e=DK)
    as_pairs = lambda t: t.rearrange("p (f h e) -> p h f e", f=2, e=DK)
    ps_y = [bank[4 + j // 2][:, j % 2 * D:(j % 2 + 1) * D] for j in range(NT)]
    of = lambda t, group: t[:, group[0] * H:(group[-1] + 1) * H]
    with nc.Block() as block:
        @block.sync
        def _(sp):
            sp.dma_start(V["b_row"], d["ln_b_row"].broadcast_to([P, D])).then_inc(row_in, 16)
            sp.dma_start(V["w_row"], d["ln_w_pairs"].broadcast_to([P, D])).then_inc(row_in, 16)
            for h in range(HH):
                sp.dma_start(qh_rows(S, h, NT - 1), outputs(r, h, NT - 1)).then_inc(o_out, 16)
            last = lambda t: t.rearrange("(j p) n -> j p n", p=P)[NT - 1]
            sp.dma_start(q[:, NT - 1, :], last(S["q_d"])).then_inc(q_in, 16)
            sp.wait_ge(o_out, 16 * HH)
            sp.dma_start(qh[:, NT - 1, :], last(S["qh_d"])).then_inc(qh_in, 16)
            sp.dma_start(w_o, d["w_o"]).then_inc(w_in, 16)
            sp.dma_start(V["norm"], d["norm_w"]).then_inc(w_in, 16)
            sp.dma_start(x1[:, NT - 1, :], last(x1_d)).then_inc(x1_in, 16)

        @block.scalar
        def _(act):
            def squares(j, n):
                if n < NT:
                    act.wait_ge(centred, j + 1)
                elif j < POOL_GATES:
                    act.wait_ge(gated, j + 1)
                else:
                    act.wait_ge(gated_pool, j - POOL_GATES + 1)
                if n >= 2:
                    act.wait_ge(ss_done, n - 1)
                act.activation(bank[n % 2][:, 0:D], qh[:, j, :], ACT.Square).then_inc(sq_ps, 1)

            def root(group, n):
                act.wait_ge(var_ready, n)
                act.activation(of(ss, group), of(ss, group), ACT.Sqrt).then_inc(rstd_ready, 1)

            def turned_copies(tiles):
                for j in tiles:
                    act.wait_ge(ot_ps, j + 1)
                    for f in range(DH):
                        act.activation(turned[:, j, f * P:(f + 1) * P], bank[2 + j % 2][:, f * P:(f + 1) * P], ACT.Copy,
                                       scale=V["norm"][:, f:f + 1]).then_inc(ot_ready, 1)

            for t, group in enumerate(GROUPS_OUT):
                for j in group:
                    squares(j, j)
                root(group, t + 1)
            act.wait_ge(w_in, 32)
            copied = ((), (0, 1), (2, 3))
            for t, group in enumerate(GROUPS_OUT):
                for j in group:
                    squares(j, NT + j)
                root(group, len(GROUPS_OUT) + t + 1)
                turned_copies(copied[t])
            turned_copies(range(4, NT))

        @block.gpsimd
        def _(pool):
            pool.wait_ge(row_in, 32)
            for j in range(NT):
                if j == NT - 1:
                    pool.wait_ge(q_in, 16)
                pool.tensor_tensor(q[:, j, :], q[:, j, :], V["b_row"], ALU.add).then_inc(b_done, 1)
            for group in GROUPS_OUT:
                for j in group:
                    pool.wait_ge(scaled, j + 1)
                    pool.tensor_tensor(qh[:, j, :], qh[:, j, :], V["w_row"], ALU.mult).then_inc(w_done, 1)
                own = [j for j in group if j >= POOL_GATES]
                for j in own:
                    pool.wait_ge(b_done, j + 1)
                    pool.wait_ge(w_done, j + 1)
                    pool.tensor_tensor(pairs(qh[:, j, :]), pairs(qh[:, j, :]), as_pairs(q[:, j, :]),
                                       ALU.add).then_inc(added_pool, 1)
                for j in own:
                    pool.wait_ge(added_pool, j - POOL_GATES + 1)
                    pool.tensor_tensor(pairs(qh[:, j, :]), pairs(qh[:, j, :]), as_pairs(gate[:, j, :]),
                                       ALU.mult).then_inc(gated_pool, 1)

        @block.vector
        def _(dve):
            n = [0]

            def then(ins):
                n[0] += 1
                ins.then_inc(step, 1)
                dve.wait_ge(step, n[0])

            hd = lambda t: t.rearrange(IN_HEADS, e=DK)
            per = lambda t, j: t[:, j * H:(j + 1) * H].unsqueeze(2).broadcast_to([P, H, DK])

            def summed(j, n):
                dve.wait_ge(sq_ps, n + 1)
                dve.tensor_reduce(ss[:, j * H:(j + 1) * H], hd(bank[n % 2][:, 0:D]), AX_X, ALU.add).then_inc(ss_done, 1)

            def inverse(group, count, n):
                dve.wait_ge(ss_done, count)
                then(dve.tensor_scalar(of(ss, group), of(ss, group), 1.0 / DK, EPS, ALU.mult, ALU.add))
                dve.reciprocal(of(ss, group), of(ss, group)).then_inc(var_ready, 1)
                dve.wait_ge(rstd_ready, n)

            for t, group in enumerate(GROUPS_OUT):
                for j in group:
                    if j == NT - 1:
                        dve.wait_ge(qh_in, 16)
                    then(dve.tensor_reduce(mean[:, j * H:(j + 1) * H], hd(qh[:, j, :]), AX_X, ALU.add))
                    dve.scalar_tensor_tensor(out=hd(qh[:, j, :]), in0=per(mean, j), scalar=-1.0 / DK,
                                             in1=hd(qh[:, j, :]), op0=ALU.mult, op1=ALU.add).then_inc(centred, 1)
                    if j > group[0]:
                        summed(j - 1, j - 1)
                summed(group[-1], group[-1])
                inverse(group, group[-1] + 1, t + 1)
                for j in group:
                    dve.tensor_tensor(hd(qh[:, j, :]), hd(qh[:, j, :]), per(ss, j), ALU.mult).then_inc(scaled, 1)
            for t, group in enumerate(GROUPS_OUT):
                for j in group:
                    if j < POOL_GATES:
                        dve.wait_ge(b_done, j + 1)
                        dve.wait_ge(w_done, j + 1)
                        then(dve.tensor_tensor(pairs(qh[:, j, :]), pairs(qh[:, j, :]), as_pairs(q[:, j, :]), ALU.add))
                        dve.tensor_tensor(pairs(qh[:, j, :]), pairs(qh[:, j, :]), as_pairs(gate[:, j, :]),
                                          ALU.mult).then_inc(gated, 1)
                    if j > group[0]:
                        summed(j - 1, NT + j - 1)
                summed(group[-1], NT + group[-1])
                inverse(group, NT + group[-1] + 1, len(GROUPS_OUT) + t + 1)
                for j in group:
                    dve.tensor_tensor(hd(qh[:, j, :]), hd(qh[:, j, :]), per(ss, j), ALU.mult).then_inc(unit, 1)
            dve.wait_ge(x1_in, 16)
            for j in range(NT):
                dve.wait_ge(y_ps, j // 2 * 2 + 2)
                dve.tensor_tensor(qh[:, j, :], x1[:, j, :], ps_y[j], ALU.add)

        @block.tensor
        def _(pe):
            def turn(j):
                pe.wait_ge(unit, j + 1)
                if j >= 2:
                    pe.wait_ge(ot_ready, 2 * (j - 1))
                for f in range(DH):
                    mm = pe.transpose(bank[2 + j % 2][:, f * P:(f + 1) * P], qh[:, j, f * P:(f + 1) * P], S["ident"][:])
                mm.then_inc(ot_ps, 1)

            pe.wait_ge(gated_pool, 1)
            warm_up(pe, S, bank[7], 6)
            turn(0)
            for j in range(NT):
                if j + 1 < NT:
                    turn(j + 1)
                pe.wait_ge(ot_ready, 2 * (j + 1))
                for f in range(DH):
                    mm = pe.matmul(ps_y[j], turned[:, j, f * P:(f + 1) * P], w_o[:, f, :],
                                   start=(f == 0), stop=(f == DH - 1))
                mm.then_inc(y_ps, 1)


def kernel(**inputs):
    import numpy as np
    import concourse.bacc as bacc
    from concourse.bass_utils import run_bass_kernel_spmd

    a = {k: np.asarray(v) for k, v in inputs.items()}
    rows = lambda w: np.ascontiguousarray(w.reshape(DH, P, -1).transpose(1, 0, 2))
    att = lambda n: a["L0_attn_" + n]
    pairs = lambda w: w.reshape(2, HH, DK, -1).transpose(1, 0, 2, 3).reshape(D, -1)
    ffn = lambda n: a["L0_ffn_" + n]
    gu = np.concatenate([np.concatenate([ffn("gate_w"), ffn("shared_gate_w")[None]]),
                         np.concatenate([ffn("up_w"), ffn("shared_up_w")[None]])], axis=1)
    down = np.concatenate([ffn("down_w"), ffn("shared_down_w")[None]]).transpose(2, 0, 1)
    arrays = {
        "x": att("x").reshape(T, D),
        "w_gu": gu.reshape(E + 1, 2 * I, DH, P).transpose(3, 0, 2, 1).reshape(P, E + 1, DH * 2 * I),
        "w_d1": down[0:P], "w_d2": down[P:],
        "rt": rows(ffn("router_w").T).reshape(P, DH * E), "rb": ffn("router_b")[None],
        "w_kv": rows(np.concatenate([att("Wk"), att("Wv")], axis=1)),
        "w_q": rows(np.concatenate([att("Wq"), att("Wbeta"), att("Wg1")], axis=1)),
        "w_g2": att("Wg2"), "w_o": rows(pairs(att("Wo"))), "norm_w": pairs(att("norm_w")).reshape(DH, P).T,
        "ln_w_pairs": pairs(att("ln_w")).reshape(1, D),
        "ln_w": att("ln_w"), "ln_w_row": att("ln_w").reshape(1, D), "ln_b_row": att("ln_b").reshape(1, D),
    }
    arrays = {k: np.ascontiguousarray(v) for k, v in arrays.items()}
    nc = bacc.Bacc("TRN2", target_bir_lowering=False, num_devices=1)
    d = {k: nc.dram_tensor(k + "_in", v.shape, F32, kind="ExternalInput").ap() for k, v in arrays.items()}
    d["out"] = nc.dram_tensor("out", (T, D), F32, kind="ExternalOutput").ap()
    build(nc, d)
    r = run_bass_kernel_spmd(nc, [{k + "_in": v for k, v in arrays.items()}], core_ids=[0])
    return r.results[0]["out"].reshape(1, T, D)
```
